# Optimizing a Trainium2 kernel written in Bass

```python
import numpy as np
import jax
import jax.numpy as jnp

def _softmax(x, axis=-1):
    return jax.nn.softmax(x, axis=axis)

def _gelu(x):
    return jax.nn.gelu(x, approximate=True)

def _silu(x):
    return jax.nn.silu(x)

def _sigmoid(x):
    return jax.nn.sigmoid(x)

def _layernorm(x, axis=-1, eps=1e-05):
    m = jnp.mean(x, axis=axis, keepdims=True)
    v = jnp.var(x, axis=axis, keepdims=True)
    return (x - m) / jnp.sqrt(v + eps)

def _scatter_add(tgt, idx, src, axis=0):
    return tgt.at[idx].add(src)

def _segment_sum(src, seg, n):
    return jax.ops.segment_sum(src, seg, n)
kernel_name = 'mk_metaformer_d1_conv_nhwc256_r2_0e5ce5'

def setup_inputs(seed: int=0):
    np.random.seed(seed)
    _w = jnp.asarray

    def _rec_inputs():
        import jax
        import jax.numpy as jnp
        _gk = jax.random.key(seed)
        x = -9.26e-05 + 0.9999 * jax.random.normal(jax.random.fold_in(_gk, 1), (1, 192, 192, 128), jnp.float32)
        return x
    x = _rec_inputs()

    def _L0_conv_setup():
        import jax, jax.numpy as jnp
        import numpy as np
        EC = 128
        C = 64
        B, N = (1, 192)

        def _ln(x, g, b, eps=1e-05):
            m = x.mean(-1, keepdims=True)
            v = x.var(-1, keepdims=True)
            return (x - m) / jnp.sqrt(v + eps) * g + b
        key = jax.random.key(seed)
        ks = jax.random.split(key, 16)
        s = 0.02
        d = {'z': jax.random.normal(ks[0], (B, N, N, EC), jnp.float32), 'l_pair': jax.random.normal(ks[1], (B, N, N, EC), jnp.float32), 'protein_pair': jax.random.normal(ks[2], (B, N, N, EC), jnp.float32), 'inter_pair': jax.random.normal(ks[3], (B, N, N, EC), jnp.float32), 'z_mask': jnp.ones((B, N, N), jnp.float32), 'ln_g': jnp.ones((EC,), jnp.float32), 'ln_b': jnp.zeros((EC,), jnp.float32), 'lnc_g': jnp.ones((C,), jnp.float32), 'lnc_b': jnp.zeros((C,), jnp.float32), 'Wg1': s * jax.random.normal(ks[4], (EC, C), jnp.float32), 'bg1': jnp.zeros((C,), jnp.float32), 'Wg2': s * jax.random.normal(ks[5], (EC, C), jnp.float32), 'bg2': jnp.zeros((C,), jnp.float32), 'Wg3': s * jax.random.normal(ks[6], (EC, C), jnp.float32), 'bg3': jnp.zeros((C,), jnp.float32), 'W1': s * jax.random.normal(ks[7], (EC, C), jnp.float32), 'b1': jnp.zeros((C,), jnp.float32), 'W2': s * jax.random.normal(ks[8], (EC, C), jnp.float32), 'b2': jnp.zeros((C,), jnp.float32), 'W3': s * jax.random.normal(ks[9], (EC, C), jnp.float32), 'b3': jnp.zeros((C,), jnp.float32), 'Wend': s * jax.random.normal(ks[10], (EC, EC), jnp.float32), 'bend': jnp.zeros((EC,), jnp.float32), 'Wsum': s * jax.random.normal(ks[11], (C, EC), jnp.float32), 'bsum': jnp.zeros((EC,), jnp.float32)}
        return d
    _L0_conv_all = _L0_conv_setup()
    _L0_conv_in = {k: v for k, v in _L0_conv_all.items() if k in ('l_pair', 'protein_pair', 'inter_pair', 'z_mask', 'ln_g', 'ln_b', 'lnc_g', 'lnc_b', 'Wg1', 'bg1', 'Wg2', 'bg2', 'Wg3', 'bg3', 'W1', 'b1', 'W2', 'b2', 'W3', 'b3', 'Wend', 'bend', 'Wsum', 'bsum')}
    del _L0_conv_all

    def _L0_ffn_setup():
        import math
        import jax, jax.numpy as jnp
        import numpy as np
        CAPACITY_FACTOR = 1.25
        TOP_K = 2
        LN_EPS = 1e-05

        def _layer_norm(x, gamma, beta):
            mu = jnp.mean(x, axis=-1, keepdims=True)
            var = jnp.var(x, axis=-1, keepdims=True)
            return (x - mu) * jax.lax.rsqrt(var + LN_EPS) * gamma + beta
        key = jax.random.key(seed)
        ks = jax.random.split(key, 4)
        B, S, D, F, E = (8, 2048, 128, 256, 8)
        x = jax.random.normal(ks[0], (B, S, D), dtype=jnp.float32)
        Wr = jax.random.normal(ks[1], (D, E), dtype=jnp.float32) / np.sqrt(D)
        br = jnp.zeros((E,), jnp.float32)
        W1 = jax.random.normal(ks[2], (E, D, F), dtype=jnp.float32) / np.sqrt(D)
        b1 = jnp.zeros((E, F), jnp.float32)
        W2 = jax.random.normal(ks[3], (E, F, D), dtype=jnp.float32) / np.sqrt(F)
        b2 = jnp.zeros((E, D), jnp.float32)
        gamma = jnp.ones((D,), jnp.float32)
        beta = jnp.zeros((D,), jnp.float32)
        return {'x': x, 'Wr': Wr, 'br': br, 'W1': W1, 'b1': b1, 'W2': W2, 'b2': b2, 'gamma': gamma, 'beta': beta}
    _L0_ffn_all = _L0_ffn_setup()
    _L0_ffn_in = {k: v for k, v in _L0_ffn_all.items() if k in ('Wr', 'br', 'W1', 'b1', 'W2', 'b2', 'gamma', 'beta')}
    del _L0_ffn_all
    return {'x': x, 'L0_conv_l_pair': _L0_conv_in['l_pair'], 'L0_conv_protein_pair': _L0_conv_in['protein_pair'], 'L0_conv_inter_pair': _L0_conv_in['inter_pair'], 'L0_conv_z_mask': _L0_conv_in['z_mask'], 'L0_conv_ln_g': _L0_conv_in['ln_g'], 'L0_conv_ln_b': _L0_conv_in['ln_b'], 'L0_conv_lnc_g': _L0_conv_in['lnc_g'], 'L0_conv_lnc_b': _L0_conv_in['lnc_b'], 'L0_conv_Wg1': _L0_conv_in['Wg1'], 'L0_conv_bg1': _L0_conv_in['bg1'], 'L0_conv_Wg2': _L0_conv_in['Wg2'], 'L0_conv_bg2': _L0_conv_in['bg2'], 'L0_conv_Wg3': _L0_conv_in['Wg3'], 'L0_conv_bg3': _L0_conv_in['bg3'], 'L0_conv_W1': _L0_conv_in['W1'], 'L0_conv_b1': _L0_conv_in['b1'], 'L0_conv_W2': _L0_conv_in['W2'], 'L0_conv_b2': _L0_conv_in['b2'], 'L0_conv_W3': _L0_conv_in['W3'], 'L0_conv_b3': _L0_conv_in['b3'], 'L0_conv_Wend': _L0_conv_in['Wend'], 'L0_conv_bend': _L0_conv_in['bend'], 'L0_conv_Wsum': _L0_conv_in['Wsum'], 'L0_conv_bsum': _L0_conv_in['bsum'], 'L0_ffn_Wr': _L0_ffn_in['Wr'], 'L0_ffn_br': _L0_ffn_in['br'], 'L0_ffn_W1': _L0_ffn_in['W1'], 'L0_ffn_b1': _L0_ffn_in['b1'], 'L0_ffn_W2': _L0_ffn_in['W2'], 'L0_ffn_b2': _L0_ffn_in['b2'], 'L0_ffn_gamma': _L0_ffn_in['gamma'], 'L0_ffn_beta': _L0_ffn_in['beta']}

def reference(x, L0_conv_l_pair, L0_conv_protein_pair, L0_conv_inter_pair, L0_conv_z_mask, L0_conv_ln_g, L0_conv_ln_b, L0_conv_lnc_g, L0_conv_lnc_b, L0_conv_Wg1, L0_conv_bg1, L0_conv_Wg2, L0_conv_bg2, L0_conv_Wg3, L0_conv_bg3, L0_conv_W1, L0_conv_b1, L0_conv_W2, L0_conv_b2, L0_conv_W3, L0_conv_b3, L0_conv_Wend, L0_conv_bend, L0_conv_Wsum, L0_conv_bsum, L0_ffn_Wr, L0_ffn_br, L0_ffn_W1, L0_ffn_b1, L0_ffn_W2, L0_ffn_b2, L0_ffn_gamma, L0_ffn_beta):
    import jax
    import jax.numpy as jnp

    def _L0_conv_ref(z, l_pair, protein_pair, inter_pair, z_mask, ln_g, ln_b, lnc_g, lnc_b, Wg1, bg1, Wg2, bg2, Wg3, bg3, W1, b1, W2, b2, W3, b3, Wend, bend, Wsum, bsum):
        import jax, jax.numpy as jnp
        import numpy as np
        EC = 128
        C = 64
        B, N = (1, 192)

        def _ln(x, g, b, eps=1e-05):
            m = x.mean(-1, keepdims=True)
            v = x.var(-1, keepdims=True)
            return (x - m) / jnp.sqrt(v + eps) * g + b
        zn = _ln(z, ln_g, ln_b)
        zm = z_mask[..., None]
        pp = _ln(protein_pair, ln_g, ln_b)
        lp = _ln(l_pair, ln_g, ln_b)
        ip = _ln(inter_pair, ln_g, ln_b)
        gate_proj = lambda x, Wg, bg, W, b: jax.nn.sigmoid(x @ Wg + bg) * (x @ W + b)
        ab1 = gate_proj(zn, Wg1, bg1, W1, b1) * zm
        ab2 = gate_proj(zn, Wg2, bg2, W2, b2) * zm
        ab3 = gate_proj(zn, Wg3, bg3, W3, b3) * zm
        pp = gate_proj(pp, Wg2, bg2, W2, b2)
        lp = gate_proj(lp, Wg1, bg1, W1, b1)
        ip = gate_proj(ip, Wg1, bg1, W1, b1)
        g = jax.nn.sigmoid(zn @ Wend + bend)
        block = jnp.einsum('bikc,bkjc->bijc', pp, ab1) + jnp.einsum('bikc,bjkc->bijc', ab2, lp) + ab3 * ip
        out = g * (_ln(block, lnc_g, lnc_b) @ Wsum + bsum) * zm
        return out

    def _L0_ffn_ref(x, Wr, br, W1, b1, W2, b2, gamma, beta):
        import math
        import jax, jax.numpy as jnp
        import numpy as np
        CAPACITY_FACTOR = 1.25
        TOP_K = 2
        LN_EPS = 1e-05

        def _layer_norm(x, gamma, beta):
            mu = jnp.mean(x, axis=-1, keepdims=True)
            var = jnp.var(x, axis=-1, keepdims=True)
            return (x - mu) * jax.lax.rsqrt(var + LN_EPS) * gamma + beta
        B, S, D = x.shape
        E = Wr.shape[1]
        N = B * S
        K = TOP_K
        logits = jnp.mean(x, axis=1) @ Wr + br
        routing_weights = jax.nn.softmax(logits, axis=-1)
        capacity = float(math.ceil(N * CAPACITY_FACTOR / E))
        expected_loads = routing_weights.sum(axis=0) * (N / B)
        scale = jnp.where(expected_loads > capacity, capacity / expected_loads, 1.0)
        routing_weights = jax.nn.softmax(routing_weights * scale, axis=-1)
        rw_tok = jnp.broadcast_to(routing_weights[:, None, :], (B, S, E)).reshape(N, E)
        top_w, top_i = jax.lax.top_k(rw_tok, K)
        top_w = jax.nn.softmax(top_w, axis=-1)
        xf = x.reshape(N, D)
        h = jax.nn.gelu(jnp.einsum('nd,edf->enf', xf, W1) + b1[:, None, :], approximate=False)
        y = jnp.einsum('enf,efd->end', h, W2) + b2[:, None, :]
        w_dense = jnp.zeros((N, E), x.dtype).at[jnp.arange(N)[:, None], top_i].add(top_w)
        out = jnp.einsum('ne,end->nd', w_dense, y).reshape(B, S, D)
        out = _layer_norm(out + x, gamma, beta)
        return out

    def _gn(v, G=32, eps=1e-05):
        B_, H_, W_, C_ = v.shape
        g = v.reshape(B_, H_, W_, G, C_ // G)
        m = jnp.mean(g, axis=(1, 2, 4), keepdims=True)
        s = jnp.var(g, axis=(1, 2, 4), keepdims=True)
        return ((g - m) / jnp.sqrt(s + eps)).reshape(v.shape)

    def _ln_c(v, eps=1e-06):
        m = jnp.mean(v, axis=-1, keepdims=True)
        s = jnp.var(v, axis=-1, keepdims=True)
        return (v - m) / jnp.sqrt(s + eps)

    def _ln_t(v, eps=1e-05):
        m = jnp.mean(v, axis=-1, keepdims=True)
        s = jnp.var(v, axis=-1, keepdims=True)
        return (v - m) / jnp.sqrt(s + eps)

    def _to_tokens(v):
        B_, H_, W_, C_ = v.shape
        return v.reshape(B_, H_ * W_, C_)

    def _from_tokens(t, like):
        return t.reshape(like.shape)
    x = x + _L0_conv_ref(_ln_c(x), L0_conv_l_pair, L0_conv_protein_pair, L0_conv_inter_pair, L0_conv_z_mask, L0_conv_ln_g, L0_conv_ln_b, L0_conv_lnc_g, L0_conv_lnc_b, L0_conv_Wg1, L0_conv_bg1, L0_conv_Wg2, L0_conv_bg2, L0_conv_Wg3, L0_conv_bg3, L0_conv_W1, L0_conv_b1, L0_conv_W2, L0_conv_b2, L0_conv_W3, L0_conv_b3, L0_conv_Wend, L0_conv_bend, L0_conv_Wsum, L0_conv_bsum)
    t = _to_tokens(x)
    t = t + _L0_ffn_ref(_ln_t(t), L0_ffn_Wr, L0_ffn_br, L0_ffn_W1, L0_ffn_b1, L0_ffn_W2, L0_ffn_b2, L0_ffn_gamma, L0_ffn_beta)
    x = _from_tokens(t, x)
    return x

_drawn_inputs = setup_inputs


def setup_inputs(seed=0):
    import zlib

    import numpy as np

    out = dict(_drawn_inputs(seed))
    spreads = {'L0_conv_ln_g': (1.0, 0.6),
     'L0_conv_ln_b': (0.0, 0.363),
     'L0_conv_lnc_g': (1.0, 0.6),
     'L0_conv_lnc_b': (0.0, 0.8),
     'L0_conv_bg1': (0.0, 2.0),
     'L0_conv_bg2': (0.0, 0.8),
     'L0_conv_bg3': (0.0, 2.0),
     'L0_conv_b1': (0.0, 0.1),
     'L0_conv_b2': (0.0, 0.1),
     'L0_conv_b3': (0.0, 2.0),
     'L0_conv_bend': (0.0, 0.8),
     'L0_conv_bsum': (0.0, 0.1),
     'L0_ffn_br': (0.0, 0.1),
     'L0_ffn_b1': (0.0, 0.369),
     'L0_ffn_b2': (0.0, 0.28),
     'L0_ffn_gamma': (1.0, 0.2),
     'L0_ffn_beta': (0.0, 0.1)}
    factors = {'L0_conv_l_pair': 3.866,
     'L0_conv_protein_pair': 4.023,
     'L0_conv_inter_pair': 8.0,
     'L0_conv_Wg1': 8.0,
     'L0_conv_Wg2': 8.0,
     'L0_conv_Wg3': 34.923,
     'L0_conv_W3': 21.996,
     'L0_conv_Wend': 5.034,
     'L0_ffn_Wr': 8.0}
    for name, (base, spread) in spreads.items():
        noise = np.random.default_rng([zlib.crc32(name.encode()), seed]).standard_normal(out[name].shape)
        drawn = base * np.exp(spread * noise) if base else spread * noise
        out[name] = jnp.asarray(drawn.astype(out[name].dtype))
    for name, factor in factors.items():
        out[name] = (out[name] * factor).astype(out[name].dtype)
    return out
```

```python
from contextlib import ExitStack

import concourse.bass as bass
from concourse import mybir

F32 = mybir.dt.float32
I32 = mybir.dt.int32
ALU = mybir.AluOpType
ACT = mybir.ActivationFunctionType
AX = mybir.AxisListType

P = 128
N = 192
CH = 128
HID = 64
BLOCK_A = 16
HALF_A = BLOCK_A // 2
NBLK = N // BLOCK_A
LOW = BLOCK_A
HIGH = HALF_A
TPB = LOW + HIGH
NB_HIGH = N - P
CC = 8
NCG = HID // CC
TOKENS = N * N
EXPERTS = 8
FF = 256
NCHUNK = 2 * FF // P
CAPACITY = -(-TOKENS * 5 // (4 * EXPERTS))
EPS5 = 1e-5
EPS6 = 1e-6
RSQRT_MAGIC = 0x5F3759DF
CHUNKS = ((0, 8), (8, 16), (16, 24))


def need(eng, sem, value):
    if isinstance(value, int) and value <= 0:
        return
    eng.wait_ge(sem, value)


LOAD_COUNT = 16 * (2 + 2)


class Chain:

    def __init__(self, eng, sem):
        self.eng, self.sem, self.base, self.count = eng, sem, 0, 0

    def start(self, base):
        self.base, self.count = base, 0

    def link(self, ins):
        self.count += 1
        ins.then_inc(self.sem, 1)
        self.eng.wait_ge(self.sem, self.base + self.count)


def load_tiles(eng, dst, src, n, sem, tiles=(0, TPB)):
    lo, hi = tiles
    for t in range(lo, min(hi, LOW), HALF_A):
        eng.dma_start(dst[:, t:t + HALF_A, :],
                      src[bass.ds(BLOCK_A * n + t, HALF_A), 0:P, :].rearrange("a b c -> b a c")).then_inc(sem, 16)
    if hi > LOW:
        for h in range(2):
            eng.dma_start(dst[64 * h:64 * h + 64, LOW:TPB, :],
                          src[bass.ds(BLOCK_A * n + HALF_A * h, HALF_A), P:N, :].rearrange("a b c -> b a c")
                          ).then_inc(sem, 16)


def wait_by_event(pool, sem, value, passed):
    pool.wait_ge(sem, value)
    pool.sem_inc(passed, 1)


def ln_coefs(nc, chain, stats, work, width, channels, mulv, addv, rstd, shift, plus=None):
    v = nc.vector
    both, diff, sq, var, y, t = (work[:, 0:2, 0:width], work[:, 2, 0:width], work[:, 3, 0:width],
                                 work[:, 4, 0:width], rstd, work[:, 5, 0:width])
    mean2, m2 = work[:, 0, 0:width], work[:, 1, 0:width]
    chain.link(v.tensor_tensor(both.rearrange("p k w -> p w k"), stats[:, :, 1:3], stats[:, :, 4:6], ALU.add))
    chain.link(v.tensor_tensor(diff, stats[:, :, 1], stats[:, :, 4], ALU.subtract))
    chain.link(v.scalar_tensor_tensor(sq, diff, 0.25 * mulv, diff, ALU.mult, ALU.mult))
    chain.link(v.scalar_tensor_tensor(var, m2, mulv / channels, sq, ALU.mult, ALU.add))
    chain.link(v.tensor_scalar(var, var, addv, None, ALU.add))
    chain.link(v.tensor_scalar(t.bitcast(I32), var.bitcast(I32), 1, None, ALU.arith_shift_right))
    chain.link(v.tensor_scalar(y.bitcast(I32), t.bitcast(I32), -1.0, float(RSQRT_MAGIC), ALU.mult, ALU.add))
    for _ in range(3):
        chain.link(v.tensor_tensor(t, y, y, ALU.mult))
        chain.link(v.scalar_tensor_tensor(t, t, -0.5, var, ALU.mult, ALU.mult))
        chain.link(v.scalar_tensor_tensor(y, t, 1.5, y, ALU.add, ALU.mult))
    last = v.scalar_tensor_tensor(shift, mean2, -0.5, y, ALU.mult, ALU.mult)
    if plus:
        chain.link(last)
        last = v.tensor_scalar(shift, shift, plus, None, ALU.add)
    return last


COEF_STEPS = 17


def setup_phase(nc, d, s):
    with ExitStack() as ctx:
        sb = lambda name, shape, dt=F32: ctx.enter_context(nc.sbuf_tensor(name, shape, dt))
        sem = lambda name: ctx.enter_context(nc.semaphore(name))
        zm_low = sb("zm_low", [P, N])
        zm_high = sb("zm_high", [64, N])
        ln_g, ln_b = sb("ln_g_col", [P, 1]), sb("ln_b_col", [P, 1])
        lnc_g, lnc_b = sb("lnc_g_col", [P, 1]), sb("lnc_b_col", [P, 1])
        fold = sb("fold", [P, P])
        foldc = sb("foldc", [HID, P])
        zeros = sb("zeros", [P, P])
        w_raw = sb("w_raw", [P, 512])
        ws_raw = sb("ws_raw", [P, CH])
        bias_row = sb("bias_row", [1, 640])
        ps = ctx.enter_context(nc.psum_tensor("ps_setup", [P, 6, 512], F32))
        loaded, ident_made, const_made = sem("setup_loaded"), sem("ident_made"), sem("const_made")
        folds_made, folded, zm_turned, own = sem("folds_made"), sem("folded"), sem("zm_turned"), sem("setup_own")
        block = ctx.enter_context(nc.Block())
        gate_order = ((0, "W1", "b1"), (64, "W2", "b2"), (128, "W3", "b3"),
                      (192, "Wg1", "bg1"), (256, "Wg2", "bg2"), (320, "Wg3", "bg3"))

        row = lambda ap: ap.rearrange("(o c) -> o c", o=1)
        col = lambda ap: ap.rearrange("(c o) -> c o", o=1)
        loads = [(zm_low[:], d["zm"][0:P, :]), (zm_high[:], d["zm"][P:N, :]),
                 (ln_g[:], col(d["ln_g"])), (ln_b[:], col(d["ln_b"])),
                 (w_raw[:, 384:512], d["Wend"]), (bias_row[:, 384:512], row(d["bend"])),
                 (bias_row[:, 512:640], row(d["bsum"]))]
        for off, w, b in gate_order:
            loads += [(w_raw[:, off:off + HID], d[w]), (bias_row[:, off:off + HID], row(d[b]))]
        for h in range(2):
            half = slice(HID * h, HID * h + HID)
            loads += [(lnc_g[half, :], col(d["lnc_g"])), (lnc_b[half, :], col(d["lnc_b"])), (ws_raw[half, :], d["Wsum"])]
        loads += [(s[k][:], row(d[k]).broadcast_to([P, CH])) for k in ("gamma", "beta")]
        n_loads = len(loads)

        @block.sync
        def _(sp):
            for dst, src in loads:
                sp.dma_start(dst, src).then_inc(loaded, 16)

        @block.gpsimd
        def _(pool):
            nc.gpsimd.memset(s["ident"][:], 0.0).then_inc(ident_made, 1)
            pool.wait_ge(ident_made, 1)
            nc.gpsimd.affine_select(out=s["ident"][:], in_=s["ident"][:], compare_op=ALU.not_equal, fill=1.0,
                                    base=0, pattern=[[-1, P]], channel_multiplier=1).then_inc(ident_made, 1)
            nc.gpsimd.memset(s["ones"][:], 1.0).then_inc(const_made, 1)
            nc.gpsimd.memset(zeros[:], 0.0).then_inc(const_made, 1)
            nc.gpsimd.memset(s["ws2"][:], 0.0).then_inc(const_made, 1)

        @block.vector
        def _(dve):
            dve.wait_ge(const_made, 3)
            dve.wait_ge(loaded, 16 * n_loads)
            chain = Chain(dve, own)
            v = nc.vector
            chain.link(v.tensor_tensor(ln_b[:], ln_b[:], ln_g[:], ALU.subtract))
            chain.link(v.tensor_tensor(lnc_b[:], lnc_b[:], lnc_g[:], ALU.subtract))
            v.tensor_scalar(fold[:], zeros[:], ln_b[:, 0:1], 1.0 / CH, ALU.add, ALU.mult).then_inc(folds_made, 1)
            v.tensor_scalar(foldc[:], zeros[0:HID, :], lnc_b[0:HID, 0:1], 1.0 / HID, ALU.add, ALU.mult).then_inc(folds_made, 1)
            chain.link(v.tensor_scalar(bias_row[:, 0:512], bias_row[:, 0:512], 1.0 / CH, None, ALU.mult))
            v.tensor_scalar(bias_row[:, 512:640], bias_row[:, 512:640], 1.0 / HID, None, ALU.mult).then_inc(folds_made, 1)
            dve.wait_ge(folded, 1)
            v.scalar_tensor_tensor(s["w_all"][:], w_raw[:], ln_g[:, 0:1], ps[:, 0, :], ALU.mult, ALU.add)
            dve.wait_ge(folded, 2)
            for h in range(2):
                half = slice(HID * h, HID * h + HID)
                v.scalar_tensor_tensor(s["ws2"][half, CH * h:CH * h + CH], ws_raw[half, :], lnc_g[half, 0:1],
                                       ps[half, 1, 0:CH], ALU.mult, ALU.add)
            dve.wait_ge(zm_turned, 3)
            zt = s["mask"][:].rearrange("p (n u) -> p n u", u=TPB)
            v.tensor_copy(zt[:, :, 0:LOW], ps[:, 2, 0:N].rearrange("p (n u) -> p n u", u=BLOCK_A))
            for h in range(2):
                src = ps[64 * h:64 * h + 64, 3 + h, 0:N].rearrange("p (n u) -> p n u", u=BLOCK_A)
                v.tensor_copy(zt[64 * h:64 * h + 64, :, LOW:TPB], src[:, :, HALF_A * h:HALF_A * h + HALF_A])

        @block.tensor
        def _(pe):
            pe.wait_ge(ident_made, 2)
            pe.wait_ge(loaded, 16 * n_loads)
            ident = s["ident"]
            for bank, cols in ((2, slice(0, P)), (3, slice(P, N)), (4, slice(64, N))):
                m = cols.stop - cols.start
                nc.tensor.transpose(ps[0:m, bank, 0:P], zm_low[:, cols], ident[:])
                nc.tensor.transpose(ps[0:m, bank, P:N], zm_high[:, cols], ident[0:64, 0:64]).then_inc(zm_turned, 1)
            pe.wait_ge(folds_made, 3)
            nc.tensor.matmul(ps[:, 0, :], fold[:], w_raw[:], start=True, stop=False)
            nc.tensor.matmul(ps[:, 0, :], s["ones"][0:1, :], bias_row[:, 0:512], start=False, stop=True).then_inc(folded, 1)
            nc.tensor.matmul(ps[:, 1, 0:CH], foldc[:], ws_raw[0:HID, :], start=True, stop=False)
            nc.tensor.matmul(ps[:, 1, 0:CH], s["ones"][0:1, :], bias_row[:, 512:640], start=False, stop=True).then_inc(folded, 1)


PASSES = (("x", 3, 2), ("pp", 1, 4), ("lp", 1, 4), ("ip", 1, 4))
GROUPS_A = []
for _s, (_name, _k, _size) in enumerate(PASSES):
    for _g in range(TPB // _size):
        GROUPS_A.append((_s, _g, _g * _size, _size))
NG_A = len(GROUPS_A)
PASS_END = [max(i for i, g in enumerate(GROUPS_A) if g[0] == s_) + 1 for s_ in range(len(PASSES))]


def project_phase(nc, d, s):
    with ExitStack() as ctx:
        sb = lambda name, shape, dt=F32: ctx.enter_context(nc.sbuf_tensor(name, shape, dt))
        sem = lambda name: ctx.enter_context(nc.semaphore(name))
        tiles_in = [sb(f"in_{name}", [P, TPB, CH]) for name, _, _ in PASSES]
        stats = [sb(f"stats_a{i}", [P, TPB, 6]) for i in range(len(PASSES))]
        work = sb("work_a", [P, 6, TPB])
        coef = [sb(f"coef_a{i}", [P, 2, TPB]) for i in range(len(PASSES))]
        xT = sb("xT_a", [P, 2, 4 * P])
        sig = sb("sig_a", [P, 2, 2 * 3 * HID])
        ab3 = sb("ab3_a", [P, TPB, HID])
        ip_prod = sb("ip_prod", [P, 2, 4 * HID])
        q_out = sb("q_out", [P, TPB, HID])
        low_out = [sb("low_ab", [P, 2 * NCG, LOW, CC]), sb("low_pp", [P, NCG, LOW, CC]), sb("low_lp", [P, NCG, LOW, CC])]
        high_out = [sb("high_ab", [P, 2 * NCG, HIGH, CC]), sb("high_pp", [P, NCG, HIGH, CC]), sb("high_lp", [P, NCG, HIGH, CC])]
        psT = ctx.enter_context(nc.psum_tensor("psT_a", [P, 2, 512], F32))
        psZ = ctx.enter_context(nc.psum_tensor("psZ_a", [P, 3, 2, 512], F32))
        loaded = [sem(f"loaded_{name}") for name, _, _ in PASSES]
        coefs_ready, own, pool_passed = sem("coefs_ready"), sem("dve_own_a"), sem("pool_passed_a")
        normed_act, normed_pool = sem("normed_act"), sem("normed_pool")
        turned, copied, projected = sem("turned"), sem("copied"), sem("projected")
        gated, masked, multiplied = sem("gated"), sem("masked"), sem("multiplied")
        stored = [sem("stored_ab"), sem("stored_pp"), sem("stored_lp"), sem("stored_q")]
        block = ctx.enter_context(nc.Block())
        srcs = [d[name] for name, _, _ in PASSES]

        def ahead(G, step, last):
            if G + step < NG_A:
                return G + step, GROUPS_A[G + step]
            return None if last else (G + step, GROUPS_A[G + step - NG_A])

        def act_tiles(t0, size):
            return [t0]

        def pool_tiles(t0, size):
            return list(range(t0 + 1, t0 + size))

        def loops(eng, body):
            body(0, False)
            with eng.Fori(1, NBLK - 1) as n:
                body(n, False)
            body(NBLK - 1, True)

        @block.sync
        def _(sp):
            for i in range(len(PASSES)):
                load_tiles(sp, tiles_in[i], srcs[i], 0, loaded[i])

            def body(n, last):
                for i in range(len(PASSES)):
                    if not last:
                        sp.wait_ge(turned, NG_A * n + PASS_END[i])
                        load_tiles(sp, tiles_in[i], srcs[i], n + 1, loaded[i])
                    sp.wait_ge(multiplied, NG_A * n + PASS_END[i])
                    if i < 3:
                        dst = (d["s_ab"], d["s_pp"], d["s_lp"])[i]
                        sp.dma_start(dst[0:P, :, bass.ds(CC * BLOCK_A * n, CC * BLOCK_A)],
                                     low_out[i][:].rearrange("p g a c -> p g (a c)")).then_inc(stored[i], 16)
                        for h in range(2):
                            sp.dma_start(dst[P:N, :, bass.ds(CC * BLOCK_A * n + CC * HALF_A * h, CC * HALF_A)],
                                         high_out[i][64 * h:64 * h + 64].rearrange("p g a c -> p g (a c)")
                                         ).then_inc(stored[i], 16)
                    else:
                        sp.dma_start(d["s_q"][bass.ds(n, 1)].rearrange("o p c -> (o p) c"),
                                     q_out[:].rearrange("p t c -> p (t c)")).then_inc(stored[3], 16)
            loops(sp, body)
            for i in range(3):
                sp.wait_ge(stored[i], 48 * NBLK)
            sp.wait_ge(stored[3], 16 * NBLK)

        def norm(wait, engine_op, sem_out, n, G, which, last):
            nxt = ahead(G, 2, last)
            if nxt is None:
                return
            count, (i, g, t0, size) = nxt
            wrap = count >= NG_A
            if g == 0:
                wait(coefs_ready, len(PASSES) * (n + (1 if wrap else 0)) + i + 1)
            ins = None
            for t in which(t0, size):
                ins = engine_op(tiles_in[i][:, t, :], coef[i][:, 0, t:t + 1], coef[i][:, 1, t:t + 1])
            ins.then_inc(sem_out, 1)

        @block.scalar
        def _(act):
            def op(x, r, b):
                return nc.scalar.activation(x, x, ACT.Identity, bias=b, scale=r)

            def copy_turned(n, count, grp):
                i, g, t0, size = grp
                act.wait_ge(turned, NG_A * n + count + 1)
                need(act, projected, NG_A * n + count - 1)
                nc.scalar.copy(xT[:, count % 2, 0:size * P], psT[:, count % 2, 0:size * P]).then_inc(copied, 1)

            def body(n, last):
                for G, (i, g, t0, size) in enumerate(GROUPS_A):
                    norm(act.wait_ge, op, normed_act, n, G, act_tiles, last)
                    nxt = ahead(G, 1, last)
                    if nxt:
                        copy_turned(n, *nxt)
                    k = PASSES[i][1]
                    act.wait_ge(projected, NG_A * n + G + 1)
                    if i == 0:
                        z = psZ[:, G % 3, :, 3 * HID:6 * HID]
                    else:
                        z = psZ[:, G % 3, 0, :].rearrange("p (t c) -> p t c", t=size)[:, :, HID:2 * HID]
                    need(act, multiplied, NG_A * n + G - 1)
                    nc.scalar.activation(sig[:, G % 2, 0:size * k * HID].rearrange("p (t c) -> p t c", t=size),
                                         z, ACT.Sigmoid).then_inc(gated, 1)

            for G in (-2, -1):
                norm(act.wait_ge, op, normed_act, 0, G, act_tiles, False)
            copy_turned(0, 0, GROUPS_A[0])
            loops(act, body)

        @block.gpsimd
        def _(pool):
            def op(x, r, b):
                return nc.gpsimd.tensor_scalar(x, x, r, b, ALU.mult, ALU.add)

            def wait(sem, value):
                wait_by_event(pool, sem, value, pool_passed)

            def body(n, last):
                for G, (i, g, t0, size) in enumerate(GROUPS_A):
                    norm(wait, op, normed_pool, n, G, pool_tiles, last)
                    if i == 0:
                        pool.wait_ge(gated, NG_A * n + G + 1)
                        gates = sig[:, G % 2, 0:size * 3 * HID].rearrange("p (t c) -> p t c", t=size)
                        zm = s["mask"][:, bass.ds(TPB * n + t0, size)].unsqueeze(2).broadcast_to([P, size, 3 * HID])
                        nc.gpsimd.tensor_tensor(gates, gates, zm, ALU.mult).then_inc(masked, 1)

            for G in (-2, -1):
                norm(wait, op, normed_pool, 0, G, pool_tiles, False)
            loops(pool, body)

        @block.tensor
        def _(pe):
            w = s["w_all"]
            pair1 = w[:, 0:6 * HID].rearrange("p (q k c) -> p q k c", q=2, k=3)
            rhs = [w[:, 0:6 * HID], pair1[:, :, 1, :], pair1[:, :, 0, :], pair1[:, :, 0, :]]

            def turn(n, count, grp):
                i, g, t0, size = grp
                pe.wait_ge(normed_act, NG_A * n + count + 1)
                pe.wait_ge(normed_pool, NG_A * n + count + 1)
                need(pe, copied, NG_A * n + count - 1)
                for j in range(size):
                    ins = nc.tensor.transpose(psT[:, count % 2, j * P:j * P + P], tiles_in[i][:, t0 + j, :], s["ident"][:])
                ins.then_inc(turned, 1)

            def body(n, last):
                for G, (i, g, t0, size) in enumerate(GROUPS_A):
                    nxt = ahead(G, 1, last)
                    if nxt:
                        turn(n, *nxt)
                    pe.wait_ge(copied, NG_A * n + G + 1)
                    need(pe, multiplied, NG_A * n + G - 2)
                    for j in range(size):
                        out = psZ[:, G % 3, j, 0:6 * HID] if i == 0 else psZ[:, G % 3, 0, j * P:j * P + P]
                        ins = nc.tensor.matmul(out, xT[:, G % 2, j * P:j * P + P], rhs[i], start=True, stop=True)
                    ins.then_inc(projected, 1)

            turn(0, 0, GROUPS_A[0])
            loops(pe, body)

        @block.vector
        def _(dve):
            chain = Chain(dve, own)
            v = nc.vector
            per_block = len(PASSES) * (COEF_STEPS + 1) + 1 + TPB // 4
            prologue = COEF_STEPS + 2

            def stats_of(n, i, tiles):
                for t in tiles:
                    v_ins = v.bn_stats(stats[i][:, t, :], tiles_in[i][:, t, :])
                return v_ins

            def coefs(n, i, last_stats):
                chain.link(last_stats)
                mulv, addv = (1.0 + EPS5, EPS5 * EPS6) if i == 0 else (1.0, EPS5)
                done = ln_coefs(nc, chain, stats[i], work, TPB, CH, mulv, addv, coef[i][:, 0, :], coef[i][:, 1, :], 1.0)
                if i == 0:
                    chain.link(done)
                    done = v.tensor_copy(s["coef_x"][:, :, bass.ds(TPB * n, TPB)], coef[0][:])
                done.then_inc(coefs_ready, 1)

            def body(n, last):
                chain.start(prologue + per_block * n)
                for G, (i, g, t0, size) in enumerate(GROUPS_A):
                    nxt_pass = (i + 1) % len(PASSES)
                    groups = TPB // size
                    stat_groups = groups * 2 // 3
                    if not (last and i == len(PASSES) - 1):
                        wrap = 1 if nxt_pass == 0 else 0
                        per = TPB // stat_groups
                        if g == 0:
                            dve.wait_ge(loaded[nxt_pass], LOAD_COUNT * (n + wrap + 1))
                        if g < stat_groups:
                            ins = stats_of(n, nxt_pass, range(g * per, g * per + per))
                            if g == stat_groups - 1:
                                coefs(n + wrap, nxt_pass, ins)
                    if i == 0:
                        dve.wait_ge(masked, (TPB // 2) * n + g + 1)
                    else:
                        dve.wait_ge(gated, NG_A * n + G + 1)
                    if g == 0 and i < 3:
                        need(dve, stored[i], 48 * n)
                    if g == 0 and i == 3:
                        need(dve, stored[3], 16 * n)
                    if i < 3:
                        out = low_out[i][:, :, t0:t0 + size, :] if t0 < LOW else high_out[i][:, :, t0 - LOW:t0 - LOW + size, :]
                        out = out.rearrange("p g a c -> p a g c")
                    gate = sig[:, G % 2, :]
                    if i == 0:
                        z = psZ[:, G % 3, :, :]
                        gate = gate.rearrange("p (t c) -> p t c", t=size)
                        v.tensor_tensor(out, z[:, :, 0:2 * HID].rearrange("p t (g c) -> p t g c", c=CC),
                                        gate[:, :, 0:2 * HID].rearrange("p t (g c) -> p t g c", c=CC), ALU.mult)
                        v.tensor_tensor(ab3[:, t0:t0 + size, :], z[:, :, 2 * HID:3 * HID], gate[:, :, 2 * HID:3 * HID],
                                        ALU.mult).then_inc(multiplied, 1)
                    else:
                        z = psZ[:, G % 3, 0, :].rearrange("p (t c) -> p t c", t=size)[:, :, 0:HID]
                        gate = gate[:, 0:size * HID].rearrange("p (t c) -> p t c", t=size)
                        if i < 3:
                            v.tensor_tensor(out, z.rearrange("p t (g c) -> p t g c", c=CC),
                                            gate.rearrange("p t (g c) -> p t g c", c=CC), ALU.mult).then_inc(multiplied, 1)
                        else:
                            prod = ip_prod[:, g % 2, :].rearrange("p (t c) -> p t c", t=size)
                            chain.link(v.tensor_tensor(prod, z, gate, ALU.mult))
                            v.tensor_tensor(q_out[:, t0:t0 + size, :], prod, ab3[:, t0:t0 + size, :], ALU.mult
                                            ).then_inc(multiplied, 1)

            dve.wait_ge(loaded[0], LOAD_COUNT)
            coefs(0, 0, stats_of(0, 0, range(TPB)))
            assert chain.count == prologue
            body(0, False)
            assert chain.count == per_block
            with dve.Fori(1, NBLK - 1) as n:
                body(n, False)
            body(NBLK - 1, True)


def triangle_phase(nc, d, s):
    with ExitStack() as ctx:
        sb = lambda name, shape, dt=F32: ctx.enter_context(nc.sbuf_tensor(name, shape, dt))
        sem = lambda name: ctx.enter_context(nc.semaphore(name))
        pp_low = [sb(f"pp_low{i}", [P, N, CC]) for i in range(2)]
        ab2_low = [sb(f"ab2_low{i}", [P, N, CC]) for i in range(2)]
        lp_low = [sb(f"lp_low{i}", [P, N, CC]) for i in range(2)]
        ab1_low = [sb(f"ab1_low{i}", [P, N, CC]) for i in range(2)]
        ab1_high = [sb(f"ab1_high{i}", [64, N, CC]) for i in range(2)]
        mov_high = [sb(f"mov_high{i}", [P, N, CC]) for i in range(2)]
        sta_high = [sb(f"sta_high{i}", [P, N, CC]) for i in range(2)]
        ab1T = sb("ab1T", [P, 2, N])
        psT = ctx.enter_context(nc.psum_tensor("psT_b", [P, 2, 512], F32))
        psO = ctx.enter_context(nc.psum_tensor("psO_b", [P, 4, 512], F32))
        loaded = [sem("loaded_even"), sem("loaded_odd")]
        turned, copied, summed, taken = sem("turned_b"), sem("copied_b"), sem("summed_b"), sem("taken_b")
        block = ctx.enter_context(nc.Block())
        N_LOADS = 8

        def loops(eng, body):
            body(0, False)
            with eng.Fori(1, NCG // 2 - 1) as m:
                body(m, False)
            body(NCG // 2 - 1, True)

        @block.sync
        def _(sp):
            def body(m, last):
                for par in range(2):
                    g = 2 * m + par
                    need(sp, summed, CC * (g - 2) + CC if not isinstance(m, int) or m > 0 else 0)
                    view = lambda src, lo, hi, k: src[lo:hi, bass.ds(g + k, 1), :].rearrange("b o c -> b (o c)")
                    flat = lambda t: t.rearrange("p a c -> p (a c)")
                    for dst, src in ((pp_low[par][:], view(d["s_pp"], 0, P, 0)), (ab1_low[par][:], view(d["s_ab"], 0, P, 0)),
                                     (ab1_high[par][:], view(d["s_ab"], P, N, 0)), (ab2_low[par][:], view(d["s_ab"], 0, P, NCG)),
                                     (lp_low[par][:], view(d["s_lp"], 0, P, 0)), (mov_high[par][0:64], view(d["s_pp"], P, N, 0)),
                                     (mov_high[par][64:P], view(d["s_ab"], P, N, NCG)),
                                     (sta_high[par][64:P], view(d["s_lp"], P, N, 0))):
                        sp.dma_start(flat(dst), src).then_inc(loaded[par], 16)
            loops(sp, body)

        @block.tensor
        def _(pe):
            ident = s["ident"]

            def turn(m, par, c):
                C = CC * par + c
                if c == 0:
                    pe.wait_ge(loaded[par], 16 * N_LOADS * (m + 1))
                need(pe, copied, 2 * CC * m + C - 1)
                lo, hi, t = ab1_low[par], ab1_high[par], psT[:, C % 2, :]
                nc.tensor.transpose(t[:, 0:P], lo[:, 0:P, c], ident[:])
                nc.tensor.transpose(t[:, P:N], hi[:, 0:P, c], ident[0:64, 0:64])
                nc.tensor.transpose(t[0:64, N:N + P], lo[:, P:N, c], ident[:])
                nc.tensor.transpose(t[0:64, N + P:2 * N], hi[:, P:N, c], ident[0:64, 0:64]).then_inc(turned, 1)

            def body(m, last):
                for C in range(2 * CC):
                    par, c = divmod(C, CC)
                    if C + 1 < 2 * CC:
                        turn(m, *divmod(C + 1, CC))
                    elif not last:
                        turn(m + 1, 0, 0)
                    pe.wait_ge(copied, 2 * CC * m + C + 1)
                    need(pe, taken, 2 * CC * m + C - 3)
                    out = psO[:, C % 4, :]
                    steps = ((ab1T[:, C % 2, :], pp_low[par][:, :, c]), (lp_low[par][:, :, c], ab2_low[par][:, :, c]),
                             (sta_high[par][:, :, c], mov_high[par][:, :, c]))
                    for k, (sta, mov) in enumerate(steps):
                        nc.tensor.matmul(out[:, 0:N], sta[:, 0:P], mov, start=(k == 0), stop=(k == 2))
                    for h in range(2):
                        for k, (sta, mov) in enumerate(steps):
                            part = mov.rearrange("p (n u) -> p n u", u=BLOCK_A)[:, :, HALF_A * h:HALF_A * h + HALF_A]
                            ins = nc.tensor.matmul(out[64 * h:64 * h + 64, N:N + N // 2], sta[:, P:N], part,
                                                   start=(k == 0), stop=(k == 2))
                    ins.then_inc(summed, 1)

            turn(0, 0, 0)
            loops(pe, body)

        @block.scalar
        def _(act):
            def body(m, last):
                for C in range(2 * CC):
                    par, c = divmod(C, CC)
                    act.wait_ge(turned, 2 * CC * m + C + 1)
                    need(act, summed, 2 * CC * m + C - 1)
                    nc.scalar.copy(ab1T[:, C % 2, :], psT[:, C % 2, 0:N])
                    nc.scalar.copy(sta_high[par][0:64, :, c], psT[0:64, C % 2, N:2 * N]).then_inc(copied, 1)
            loops(act, body)

        @block.vector
        def _(dve):
            tri = s["tri"][:].rearrange("p (n u) c -> p n u c", u=TPB)

            def body(m, last):
                for C in range(2 * CC):
                    dve.wait_ge(summed, 2 * CC * m + C + 1)
                    src = psO[:, C % 4, :]
                    at = bass.ds(2 * CC * m + C, 1)
                    nc.vector.tensor_copy(tri[:, :, 0:LOW, at].rearrange("p n u o -> p n (u o)"),
                                          src[:, 0:N].rearrange("p (n u) -> p n u", u=LOW))
                    nc.vector.tensor_copy(tri[:, :, LOW:TPB, at].rearrange("p n u o -> p n (u o)"),
                                          src[:, N:N + N // 2].rearrange("p (n u) -> p n u", u=HIGH)).then_inc(taken, 1)
            loops(dve, body)


PAIRS = TPB // 2
CHUNK_OF = [k for k, (lo, hi) in enumerate(CHUNKS) for _ in range(lo, hi)]
CHUNK_DMAS = (1, 1, 2)


def mix_phase(nc, d, s):
    with ExitStack() as ctx:
        sb = lambda name, shape, dt=F32: ctx.enter_context(nc.sbuf_tensor(name, shape, dt))
        sem = lambda name: ctx.enter_context(nc.semaphore(name))
        x_in, x_res, x2 = sb("x_in_c", [P, TPB, CH]), sb("x_res", [P, TPB, CH]), sb("x2_c", [P, TPB, CH])
        gate, q_in = sb("end_gate", [P, TPB, CH]), sb("q_in", [P, TPB, HID])
        coef_x = sb("coef_x_now", [P, 2, TPB])
        xh, xT = sb("xh_c", [P, 2, 2, CH]), sb("xT_c", [P, 2, 2 * P])
        tri_n, triT = sb("tri_n", [P, 2, 2, HID]), sb("triT", [P, 2, P])
        y = sb("y_c", [P, 2, 2, CH])
        stats_t, stats_x = sb("stats_t", [P, TPB, 6]), sb("stats_x2", [P, TPB, 6])
        work = sb("work_c", [P, 6, TPB])
        coef_t, coef_2 = sb("coef_t", [P, 2, TPB]), sb("coef_2_now", [P, 2, TPB])
        psT = ctx.enter_context(nc.psum_tensor("psT_c", [P, 2, 512], F32))
        psZ = ctx.enter_context(nc.psum_tensor("psZ_c", [P, 2, 512], F32))
        psB = ctx.enter_context(nc.psum_tensor("psB_c", [P, 512], F32))
        psW = ctx.enter_context(nc.psum_tensor("psW_c", [P, 2, 512], F32))
        chunk_sems = lambda name: [sem(f"{name}_{k}") for k in range(len(CHUNKS))]
        loaded_x, loaded_q, loaded_r, stored = (chunk_sems(k) for k in ("loaded_xc", "loaded_qc", "loaded_res", "stored_x2"))
        coefx_ready, normed_act, normed_pool = sem("coefx_ready"), sem("normed_act_c"), sem("normed_pool_c")
        turned, copied, projected, gated = (sem(f"{k}_c") for k in ("turned", "copied", "projected", "gated"))
        added, own, pool_passed = sem("added"), sem("dve_own_c"), sem("pool_passed_c")
        tri_normed, tri_turned, tri_copied, tri_projected = (sem(f"tri_{k}") for k in ("normed", "turned", "copied", "projected"))
        y_made, x2_made, coefs2_ready, routed = sem("y_made"), sem("x2_made"), sem("coefs2_ready"), sem("routed")
        block = ctx.enter_context(nc.Block())

        def loops(eng, body, chain=None, head=0, per=0):
            body(0, True, False, False, True)
            body(1, True, True, False, True)
            if chain:
                assert chain.count == head
            with eng.Fori(2, NBLK - 1) as n:
                if chain:
                    chain.start(head + per * (n - 2))
                body(n, True, True, True, True)
                if chain:
                    assert chain.count == per
            if chain:
                chain.start(head + per * (NBLK - 3))
            body(NBLK - 1, True, True, True, False)
            body(NBLK, False, True, True, False)
            body(NBLK + 1, False, False, True, False)

        @block.sync
        def _(sp):
            def load_q(n, k):
                lo, hi = CHUNKS[k]
                sp.dma_start(q_in[:, lo:hi, :].rearrange("p t c -> p (t c)"),
                             d["s_q"][bass.ds(n, 1), :, lo * HID:hi * HID].rearrange("o p c -> (o p) c")
                             ).then_inc(loaded_q[k], 16)

            for k, ch in enumerate(CHUNKS):
                load_tiles(sp, x_in, d["x"], 0, loaded_x[k], ch)
                load_q(0, k)
            for k, ch in enumerate(CHUNKS):
                load_tiles(sp, x_res, d["x"], 0, loaded_r[k], ch)

            def body(n, c1, c2, c3, more):
                for k, (lo, hi) in enumerate(CHUNKS):
                    if c2:
                        m = n - 1
                        sp.wait_ge(x2_made, PAIRS * m + hi // 2)
                        sp.dma_start(d["s_x2"][bass.ds(m, 1), :, lo * CH:hi * CH].rearrange("o p c -> (o p) c"),
                                     x2[:, lo:hi, :].rearrange("p t c -> p (t c)")).then_inc(stored[k], 16)
                        if c1:
                            load_tiles(sp, x_res, d["x"], n, loaded_r[k], (lo, hi))
                    if more:
                        sp.wait_ge(turned, PAIRS * n + hi // 2)
                        sp.wait_ge(added, PAIRS * n + hi // 2)
                        load_tiles(sp, x_in, d["x"], n + 1, loaded_x[k], (lo, hi))
                        load_q(n + 1, k)
            loops(sp, body)
            for k in range(len(CHUNKS)):
                sp.wait_ge(stored[k], 16 * NBLK)

        def norm_next(wait, op, sem_out, n, j, which, more):
            if j == PAIRS - 1:
                if not more:
                    return
                n, j = n + 1, -1
            nxt = j + 1
            t = 2 * nxt + which
            k = CHUNK_OF[t]
            if nxt % 6 == 0:
                wait(coefx_ready, 2 * n + nxt // 6 + 1)
            if t - which == CHUNKS[k][0]:
                wait(loaded_x[k], 16 * CHUNK_DMAS[k] * (n + 1))
            if not isinstance(n, int) or PAIRS * n + nxt > 1:
                wait(turned, PAIRS * n + nxt - 1)
            op(xh[:, nxt % 2, which, :], x_in[:, t, :], coef_x[:, 0, t:t + 1], coef_x[:, 1, t:t + 1]).then_inc(sem_out, 1)

        @block.scalar
        def _(act):
            def op(out, x, r, b):
                return nc.scalar.activation(out, x, ACT.Identity, bias=b, scale=r)

            def copy_turned(n, j):
                act.wait_ge(turned, PAIRS * n + j + 1)
                need(act, projected, PAIRS * n + j - 1)
                nc.scalar.copy(xT[:, j % 2, :], psT[:, j % 2, 0:2 * P]).then_inc(copied, 1)

            def body(n, c1, c2, c3, more):
                m = n - 1
                for j in range(PAIRS):
                    if c1:
                        norm_next(act.wait_ge, op, normed_act, n, j, 0, more)
                    if c2:
                        act.wait_ge(tri_turned, PAIRS * m + j + 1)
                        need(act, tri_projected, PAIRS * m + j - 1)
                        nc.scalar.copy(triT[:, j % 2, :], psB[:, 0:P]).then_inc(tri_copied, 1)
                    if c1:
                        if j + 1 < PAIRS:
                            copy_turned(n, j + 1)
                        elif more:
                            copy_turned(n + 1, 0)
                        act.wait_ge(projected, PAIRS * n + j + 1)
                        if c2:
                            act.wait_ge(y_made, PAIRS * m + j + 1)
                        nc.scalar.activation(gate[:, 2 * j:2 * j + 2, :],
                                             psZ[:, j % 2, 0:2 * CH].rearrange("p (t c) -> p t c", t=2),
                                             ACT.Sigmoid).then_inc(gated, 1)

            norm_next(act.wait_ge, op, normed_act, 0, -1, 0, True)
            copy_turned(0, 0)
            loops(act, body)

        @block.gpsimd
        def _(pool):
            def op(out, x, r, b):
                return nc.gpsimd.tensor_scalar(out, x, r, b, ALU.mult, ALU.add)

            def wait(sem, value):
                wait_by_event(pool, sem, value, pool_passed)

            def body(n, c1, c2, c3, more):
                m = n - 1
                for j in range(PAIRS):
                    if c1:
                        norm_next(wait, op, normed_pool, n, j, 1, more)
                    if c1:
                        k = CHUNK_OF[2 * j]
                        if 2 * j == CHUNKS[k][0]:
                            pool.wait_ge(loaded_q[k], 16 * (n + 1))
                        pair = s["tri"][:, bass.ds(TPB * n + 2 * j, 2), :]
                        nc.gpsimd.tensor_tensor(pair, pair, q_in[:, 2 * j:2 * j + 2, :], ALU.add).then_inc(added, 1)
                    if c2:
                        k = CHUNK_OF[2 * j]
                        pool.wait_ge(y_made, PAIRS * m + j + 1)
                        if 2 * j == CHUNKS[k][0]:
                            pool.wait_ge(loaded_r[k], 16 * CHUNK_DMAS[k] * (m + 1))
                            need(pool, stored[k], 16 * m)
                        if c3:
                            pool.wait_ge(routed, PAIRS * (n - 2) + j + 1)
                        nc.gpsimd.tensor_tensor(x2[:, 2 * j:2 * j + 2, :], y[:, j % 2], x_res[:, 2 * j:2 * j + 2, :],
                                                ALU.add).then_inc(x2_made, 1)

            norm_next(wait, op, normed_pool, 0, -1, 1, True)
            loops(pool, body)

        @block.tensor
        def _(pe):
            w_end = s["w_all"][:, 6 * HID:6 * HID + CH]

            def turn(n, j):
                pe.wait_ge(normed_act, PAIRS * n + j + 1)
                pe.wait_ge(normed_pool, PAIRS * n + j + 1)
                need(pe, copied, PAIRS * n + j - 1)
                for i in range(2):
                    ins = nc.tensor.transpose(psT[:, j % 2, i * P:i * P + P], xh[:, j % 2, i, :], s["ident"][:])
                ins.then_inc(turned, 1)

            def body(n, c1, c2, c3, more):
                m = n - 1
                for j in range(PAIRS):
                    if c3:
                        if j == 0:
                            pe.wait_ge(coefs2_ready, n - 1)
                        for t in (2 * j, 2 * j + 1):
                            ins = nc.tensor.matmul(s["psR"][0:1, 0:CH], coef_2[:, 0, t:t + 1], x2[:, t, :],
                                                   start=False, stop=False)
                        ins.then_inc(routed, 1)
                    if c2:
                        pe.wait_ge(tri_normed, PAIRS * m + j + 1)
                        need(pe, tri_copied, PAIRS * m + j)
                        nc.tensor.transpose(psB[:, 0:P], tri_n[:, j % 2].rearrange("p t c -> p (t c)"), s["ident"][:]
                                            ).then_inc(tri_turned, 1)
                    if c1:
                        if j + 1 < PAIRS:
                            turn(n, j + 1)
                        elif more:
                            turn(n + 1, 0)
                        pe.wait_ge(copied, PAIRS * n + j + 1)
                        need(pe, gated, PAIRS * n + j - 1)
                        for i in range(2):
                            ins = nc.tensor.matmul(psZ[:, j % 2, CH * i:CH * i + CH], xT[:, j % 2, i * P:i * P + P], w_end,
                                                   start=True, stop=True)
                        ins.then_inc(projected, 1)
                    if c2:
                        pe.wait_ge(tri_copied, PAIRS * m + j + 1)
                        need(pe, y_made, PAIRS * m + j - 1)
                        nc.tensor.matmul(psW[:, j % 2, 0:2 * CH], triT[:, j % 2, :], s["ws2"][:], start=True, stop=True
                                         ).then_inc(tri_projected, 1)

            nc.tensor.matmul(s["psR"][0:1, 0:CH], s["ones"][0:HID, 0:1], s["ws2"][0:HID, CH:2 * CH], start=True, stop=False)
            turn(0, 0)
            loops(pe, body)

        @block.vector
        def _(dve):
            chain = Chain(dve, own)
            v = nc.vector
            c1_links, c2_links = COEF_STEPS + 2, COEF_STEPS + 1
            tri_at = lambda n, t, size: s["tri"][:, bass.ds(TPB * n + t, size), :]

            def coef_x_next(n, half):
                lo, w = half * TPB // 2, TPB // 2
                v.tensor_copy(coef_x[:, :, lo:lo + w], s["coef_x"][:, :, bass.ds(TPB * n + lo, w)]).then_inc(coefx_ready, 1)

            def norm_tri(m, j):
                need(dve, tri_turned, PAIRS * m + j - 1)
                for i in range(2):
                    t = 2 * j + i
                    ins = v.tensor_scalar(tri_n[:, j % 2, i, :], s["tri"][:, bass.ds(TPB * m + t, 1), :].rearrange("p o c -> p (o c)"),
                                          coef_t[:, 0, t:t + 1], coef_t[:, 1, t:t + 1], ALU.mult, ALU.add)
                ins.then_inc(tri_normed, 1)

            def body(n, c1, c2, c3, more):
                m = n - 1
                stats_ins = None
                for j in range(PAIRS):
                    if c2:
                        if j == 0:
                            norm_tri(m, 0)
                        if j + 1 < PAIRS:
                            norm_tri(m, j + 1)
                    if more and j == PAIRS // 2 + 1:
                        dve.wait_ge(turned, PAIRS * n + PAIRS // 2)
                        coef_x_next(n + 1, 0)
                    if more and j == PAIRS - 1:
                        dve.wait_ge(turned, PAIRS * n + PAIRS)
                        coef_x_next(n + 1, 1)
                    if c1:
                        dve.wait_ge(added, PAIRS * n + j + 1)
                        for t in (2 * j, 2 * j + 1):
                            stats_ins = v.bn_stats(stats_t[:, t, :], tri_at(n, t, 1).rearrange("p o c -> p (o c)"))
                    if c2:
                        if j > 0:
                            dve.wait_ge(x2_made, PAIRS * m + j)
                            for t in (2 * j - 2, 2 * j - 1):
                                v.bn_stats(stats_x[:, t, :], x2[:, t, :])
                        dve.wait_ge(tri_projected, PAIRS * m + j + 1)
                        need(dve, x2_made, PAIRS * m + j - 1)
                        v.tensor_tensor(y[:, j % 2], psW[:, j % 2, 0:2 * CH].rearrange("p (t c) -> p t c", t=2),
                                        gate[:, 2 * j:2 * j + 2, :], ALU.mult).then_inc(y_made, 1)
                if c2:
                    dve.wait_ge(x2_made, PAIRS * m + PAIRS)
                    for t in (TPB - 2, TPB - 1):
                        stats_ins = v.bn_stats(stats_x[:, t, :], x2[:, t, :])
                if c1:
                    chain.link(stats_ins)
                    last = ln_coefs(nc, chain, stats_t, work, TPB, HID, 1.0, EPS5, coef_t[:, 0, :], coef_t[:, 1, :], 1.0)
                    chain.link(last)
                    zm = s["mask"][:, bass.ds(TPB * n, TPB)].unsqueeze(1).broadcast_to([P, 2, TPB])
                    chain.link(v.tensor_tensor(coef_t[:], coef_t[:], zm, ALU.mult))
                if c2:
                    if not c1:
                        chain.link(stats_ins)
                    if c3:
                        dve.wait_ge(routed, PAIRS * (n - 2) + PAIRS)
                    last = ln_coefs(nc, chain, stats_x, work, TPB, CH, 1.0, EPS5, coef_2[:, 0, :], coef_2[:, 1, :])
                    chain.link(last)
                    v.tensor_copy(s["coef_2"][:, :, bass.ds(TPB * m, TPB)], coef_2[:]).then_inc(coefs2_ready, 1)

            for half in range(2):
                coef_x_next(0, half)
            c1_links = 1 + COEF_STEPS + 2
            c2_links = COEF_STEPS
            loops(dve, body, chain, 2 * c1_links + c2_links, c1_links + c2_links)


def route_phase(nc, d, s):
    with ExitStack() as ctx:
        sb = lambda name, shape, dt=F32: ctx.enter_context(nc.sbuf_tensor(name, shape, dt))
        sem = lambda name: ctx.enter_context(nc.semaphore(name))
        E = EXPERTS
        wr, br = sb("wr", [CH, E]), sb("br", [1, E])
        shift_sum = sb("shift_sum", [P, 1])
        mean, mean_col = sb("mean_row", [1, CH]), sb("mean_col", [CH, 1])
        vec = sb("router_rows", [1, 12, E])
        scal = sb("router_scalars", [1, 16])
        sq = sb("router_squares", [1, 3, E, E])
        pick = sb("router_picks", [1, 2, E])
        pick_v = sb("router_pick_v", [1, 2, E])
        chosen, w_pair = sb("chosen", [1, 2], I32), sb("w_pair", [1, 2])
        chosen_f, val = sb("chosen_f", [1, 2]), sb("chosen_val", [1, 2])
        w_col = sb("w_col", [P, 2])
        w2_raw, b2_raw = sb("w2_raw", [P, NCHUNK, CH]), sb("b2_raw", [1, 2, CH])
        b2_row, b1_rows = sb("b2_row", [1, CH]), sb("b1_rows", [NCHUNK, P])
        ps = ctx.enter_context(nc.psum_tensor("ps_route", [P, 4, 512], F32))
        loaded, below_made, own, own_a = sem("route_loaded"), sem("below_made"), sem("dve_own_r"), sem("act_exp")
        summed_shift, summed_all, mean_made, turned, mean_kept, logits = (
            sem(k) for k in ("summed_shift", "summed_all", "mean_made", "mean_turned", "mean_kept", "logits"))
        max_made, probs_ready, gap_made, chosen_made, experts_loaded = (
            sem(k) for k in ("max_made", "probs_ready", "gap_made", "chosen_made", "experts_loaded"))
        weights_made, weights_spread, b1_turned, b2_made, b2_spread = (
            sem(k) for k in ("weights_made", "weights_spread", "b1_turned", "b2_made", "b2_spread"))
        block = ctx.enter_context(nc.Block())
        below = sq[:, 2]

        @block.gpsimd
        def _(pool):
            nc.gpsimd.memset(below, 1.0).then_inc(below_made, 1)
            pool.wait_ge(below_made, 1)
            nc.gpsimd.affine_select(out=below, in_=below, compare_op=ALU.is_gt, fill=0.0, base=0,
                                    pattern=[[1, E], [-1, E]], channel_multiplier=0).then_inc(below_made, 1)

        @block.sync
        def _(sp):
            sp.dma_start(wr[:], d["Wr"]).then_inc(loaded, 16)
            sp.dma_start(br[:], d["br"].rearrange("(o e) -> o e", o=1)).then_inc(loaded, 16)
            sp.wait_ge(chosen_made, 1)
            for k in range(2):
                e = sp.value_load(chosen[0:1, k:k + 1], min_val=0, max_val=E - 1)
                at = bass.ds(e, 1)
                half = slice(k * FF // P, (k + 1) * FF // P)
                sp.dma_start(s["w1"][:, k * FF:(k + 1) * FF], d["W1e"][at].rearrange("o c f -> (o c) f")).then_inc(experts_loaded, 16)
                sp.dma_start(w2_raw[:, half, :], d["W2e"][at].rearrange("o (c p) d -> p (o c) d", p=P)).then_inc(experts_loaded, 16)
                sp.dma_start(b1_rows[half, :], d["b1e"][at].rearrange("o (c p) -> (o c) p", p=P)).then_inc(experts_loaded, 16)
                sp.dma_start(b2_raw[0:1, k, :], d["b2e"][at]).then_inc(experts_loaded, 16)
            sp.wait_ge(experts_loaded, 8 * 16)

        @block.tensor
        def _(pe):
            ones = s["ones"]
            psR = s["psR"][0:1, 0:CH]
            pe.wait_ge(summed_shift, 1)
            nc.tensor.matmul(psR, shift_sum[:], ones[:], start=False, stop=True).then_inc(summed_all, 1)
            pe.wait_ge(mean_made, 1)
            nc.tensor.matmul(ps[:, 0, 0:1], mean[:], ones[0:1, 0:1], start=True, stop=True).then_inc(turned, 1)
            pe.wait_ge(mean_kept, 1)
            pe.wait_ge(loaded, 32)
            nc.tensor.matmul(ps[0:1, 1, 0:E], mean_col[:], wr[:], start=True, stop=False)
            nc.tensor.matmul(ps[0:1, 1, 0:E], ones[0:1, 0:1], br[:], start=False, stop=True).then_inc(logits, 1)
            pe.wait_ge(weights_made, 1)
            nc.tensor.matmul(ps[:, 2, 0:2], ones[0:1, :], w_pair[:], start=True, stop=True).then_inc(weights_spread, 1)
            pe.wait_ge(experts_loaded, 8 * 16)
            nc.tensor.transpose(ps[:, 0, 0:NCHUNK], b1_rows[:], s["ident"][0:NCHUNK, 0:NCHUNK]).then_inc(b1_turned, 1)
            pe.wait_ge(b2_made, 1)
            nc.tensor.matmul(ps[:, 3, 0:CH], ones[0:1, :], b2_row[:], start=True, stop=True).then_inc(b2_spread, 1)

        @block.scalar
        def _(act):
            act.wait_ge(max_made, 1)
            nc.scalar.activation(vec[:, 0], ps[0:1, 1, 0:E], ACT.Exp, bias=scal[:, 0:1], accum_out=scal[:, 1:2]).then_inc(own_a, 1)
            act.wait_ge(probs_ready, 1)
            nc.scalar.activation(vec[:, 3], vec[:, 2], ACT.Exp, bias=scal[:, 3:4], accum_out=scal[:, 4:5]).then_inc(own_a, 1)
            act.wait_ge(gap_made, 1)
            nc.scalar.activation(scal[:, 6:7], scal[:, 5:6], ACT.Exp).then_inc(own_a, 1)

        @block.vector
        def _(dve):
            chain = Chain(dve, own)
            v = nc.vector
            L = chain.link
            v.reduce_sum(shift_sum[:], s["coef_2"][:, 1, :], AX.X).then_inc(summed_shift, 1)
            dve.wait_ge(summed_all, 1)
            v.tensor_scalar(mean[:], s["psR"][0:1, 0:CH], 1.0 / TOKENS, None, ALU.mult).then_inc(mean_made, 1)
            dve.wait_ge(turned, 1)
            v.tensor_copy(mean_col[:], ps[:, 0, 0:1]).then_inc(mean_kept, 1)
            dve.wait_ge(logits, 1)
            L(v.reduce_max(scal[:, 2:3], ps[0:1, 1, 0:E], AX.X))
            v.tensor_scalar(scal[:, 0:1], scal[:, 2:3], -1.0, None, ALU.mult).then_inc(max_made, 1)
            dve.wait_ge(own_a, 1)
            L(v.reciprocal(scal[:, 7:8], scal[:, 1:2]))
            L(v.tensor_scalar(vec[:, 1], vec[:, 0], scal[:, 7:8], None, ALU.mult))
            L(v.tensor_scalar(vec[:, 2], vec[:, 1], CAPACITY / TOKENS, None, ALU.min))
            L(v.reduce_max(scal[:, 2:3], vec[:, 2], AX.X))
            v.tensor_scalar(scal[:, 3:4], scal[:, 2:3], -1.0, None, ALU.mult).then_inc(probs_ready, 1)
            by_f = vec[:, 2].unsqueeze(1).broadcast_to([1, E, E])
            by_e = vec[:, 2].unsqueeze(2).broadcast_to([1, E, E])
            dve.wait_ge(below_made, 2)
            v.tensor_tensor(sq[:, 0], by_f, by_e, ALU.is_gt)
            L(v.tensor_tensor(sq[:, 1], by_f, by_e, ALU.is_equal))
            L(v.tensor_tensor(sq[:, 1], sq[:, 1], below, ALU.mult))
            L(v.tensor_tensor(sq[:, 0], sq[:, 0], sq[:, 1], ALU.add))
            v.reduce_sum(vec[:, 4], sq[:, 0], AX.X)
            L(v.reduce_sum(vec[:, 5], below, AX.X))
            for k in range(2):
                ins = v.tensor_scalar(pick[:, k], vec[:, 4], float(k), None, ALU.is_equal)
            L(ins)
            L(v.tensor_tensor(pick_v[:], pick[:], vec[:, 5].unsqueeze(1).broadcast_to([1, 2, E]), ALU.mult))
            L(v.reduce_sum(chosen_f[:], pick_v[:], AX.X))
            v.tensor_copy(chosen[:], chosen_f[:]).then_inc(chosen_made, 1)
            dve.wait_ge(own_a, 2)
            L(v.reciprocal(scal[:, 8:9], scal[:, 4:5]))
            L(v.tensor_scalar(vec[:, 6], vec[:, 3], scal[:, 8:9], None, ALU.mult))
            L(v.tensor_tensor(pick_v[:], pick[:], vec[:, 6].unsqueeze(1).broadcast_to([1, 2, E]), ALU.mult))
            L(v.reduce_sum(val[:], pick_v[:], AX.X))
            v.tensor_tensor(scal[:, 5:6], val[:, 1:2], val[:, 0:1], ALU.subtract).then_inc(gap_made, 1)
            dve.wait_ge(own_a, 3)
            L(v.tensor_scalar(scal[:, 9:10], scal[:, 6:7], 1.0, None, ALU.add))
            L(v.reciprocal(w_pair[:, 0:1], scal[:, 9:10]))
            v.tensor_tensor(w_pair[:, 1:2], scal[:, 6:7], w_pair[:, 0:1], ALU.mult).then_inc(weights_made, 1)
            dve.wait_ge(weights_spread, 1)
            L(v.tensor_copy(w_col[:], ps[:, 2, 0:2]))
            dve.wait_ge(experts_loaded, 8 * 16)
            L(v.tensor_scalar(b2_raw[:, 1, :], b2_raw[:, 1, :], w_col[0:1, 1:2], None, ALU.mult))
            v.scalar_tensor_tensor(b2_row[:], b2_raw[:, 0, :], w_col[0:1, 0:1], b2_raw[:, 1, :], ALU.mult, ALU.add).then_inc(b2_made, 1)
            for k in range(2):
                half = slice(k * FF // P, (k + 1) * FF // P)
                v.tensor_scalar(s["w2"][:, half, :], w2_raw[:, half, :], w_col[:, k:k + 1], None, ALU.mult)
            dve.wait_ge(b2_spread, 1)
            v.tensor_copy(s["b2"][:], ps[:, 3, 0:CH])
            dve.wait_ge(b1_turned, 1)
            v.tensor_copy(s["b1"][:], ps[:, 0, 0:NCHUNK])


GROUPS_D = TPB // 4


def ffn_phase(nc, d, s):
    with ExitStack() as ctx:
        sb = lambda name, shape, dt=F32: ctx.enter_context(nc.sbuf_tensor(name, shape, dt))
        sem = lambda name: ctx.enter_context(nc.semaphore(name))
        G4 = 4 * CH
        x2 = sb("x2_d", [P, TPB, CH])
        x2b, vv, o_buf = sb("x2_beta", [P, TPB, CH]), sb("ffn_sum", [P, TPB, CH]), sb("out_buf", [P, TPB, CH])
        xh, xb, u = sb("xh_d", [P, 2, 4, CH]), sb("xh_b2", [P, 2, 4, CH]), sb("u_d", [P, 2, 4, CH])
        xT, hT = sb("xT_d", [P, 2, G4]), sb("hT", [P, 2, NCHUNK, G4])
        stats, work, coef = sb("stats_d", [P, TPB, 6]), sb("work_d", [P, 6, TPB]), sb("coef_d", [P, 2, TPB])
        psT = ctx.enter_context(nc.psum_tensor("psT_d", [P, 2, 512], F32))
        psH = ctx.enter_context(nc.psum_tensor("psH_d", [P, NCHUNK, 512], F32))
        psY = ctx.enter_context(nc.psum_tensor("psY_d", [P, 2, 512], F32))
        loaded, stored = [[sem(f"{k}_{i}") for i in range(len(CHUNKS))] for k in ("loaded_d", "stored_out")]
        normed, turned, copied, raised, gelued, lowered = (sem(f"{k}_d") for k in ("normed", "turned", "copied", "raised", "gelued", "lowered"))
        xb_made, x2b_made, v_made, u_made, scaled, final, own = (
            sem(k) for k in ("xb_made", "x2b_made", "v_made", "u_made", "scaled", "final", "dve_own_d"))
        block = ctx.enter_context(nc.Block())
        NG = GROUPS_D

        def loops(eng, body, chain=None, per=0):
            body(0, True, False, True)
            body(1, True, True, True)
            if chain:
                assert chain.count == 2 * per
            with eng.Fori(2, NBLK - 1) as n:
                if chain:
                    chain.start(per * n)
                body(n, True, True, True)
                if chain:
                    assert chain.count == per
            if chain:
                chain.start(per * (NBLK - 1))
            body(NBLK - 1, True, True, False)
            body(NBLK, False, True, False)

        @block.sync
        def _(sp):
            def load(n, k):
                lo, hi = CHUNKS[k]
                sp.dma_start(x2[:, lo:hi, :].rearrange("p t c -> p (t c)"),
                             d["s_x2"][bass.ds(n, 1), :, lo * CH:hi * CH].rearrange("o p c -> (o p) c")).then_inc(loaded[k], 16)

            for k in range(len(CHUNKS)):
                load(0, k)

            def body(n, d1, d2, more):
                for k, (lo, hi) in enumerate(CHUNKS):
                    if d2:
                        m = n - 1
                        sp.wait_ge(final, NG * m + hi // 4)
                        if hi <= LOW:
                            sp.dma_start(d["out"][bass.ds(BLOCK_A * m + lo, hi - lo), 0:P, :].rearrange("a b c -> b a c"),
                                         o_buf[:, lo:hi, :]).then_inc(stored[k], 16)
                        else:
                            for h in range(2):
                                sp.dma_start(d["out"][bass.ds(BLOCK_A * m + HALF_A * h, HALF_A), P:N, :].rearrange("a b c -> b a c"),
                                             o_buf[64 * h:64 * h + 64, lo:hi, :]).then_inc(stored[k], 16)
                    if more:
                        sp.wait_ge(normed, NG * n + hi // 4)
                        sp.wait_ge(x2b_made, NG * n + hi // 4)
                        load(n + 1, k)
            loops(sp, body)
            for k in range(len(CHUNKS)):
                sp.wait_ge(stored[k], 16 * CHUNK_DMAS[k] * NBLK)

        @block.scalar
        def _(act):
            def copy_turned(n, g):
                act.wait_ge(turned, NG * n + g + 1)
                need(act, raised, NCHUNK * (NG * n + g - 1))
                nc.scalar.copy(xT[:, g % 2, :], psT[:, g % 2, :]).then_inc(copied, 1)

            def body(n, d1, d2, more):
                if not d1:
                    return
                for g in range(NG):
                    for f in range(NCHUNK):
                        act.wait_ge(raised, NCHUNK * (NG * n + g) + f + 1)
                        if f == 0:
                            need(act, lowered, NG * n + g - 1)
                        nc.scalar.activation(hT[:, g % 2, f, :], psH[:, f, :], ACT.Gelu, bias=s["b1"][:, f:f + 1]).then_inc(gelued, 1)
                    if g + 1 < NG:
                        copy_turned(n, g + 1)
                    elif more:
                        copy_turned(n + 1, 0)
            copy_turned(0, 0)
            loops(act, body)

        @block.tensor
        def _(pe):
            def turn(n, g):
                pe.wait_ge(normed, NG * n + g + 1)
                need(pe, copied, NG * n + g - 1)
                for i in range(4):
                    ins = nc.tensor.transpose(psT[:, g % 2, i * P:i * P + P], xh[:, g % 2, i, :], s["ident"][:])
                ins.then_inc(turned, 1)

            def body(n, d1, d2, more):
                if not d1:
                    return
                for g in range(NG):
                    pe.wait_ge(copied, NG * n + g + 1)
                    for f in range(NCHUNK):
                        need(pe, gelued, NCHUNK * (NG * n + g - 1) + f + 1)
                        nc.tensor.matmul(psH[:, f, :], s["w1"][:, f * P:f * P + P], xT[:, g % 2, :], start=True, stop=True
                                         ).then_inc(raised, 1)
                    if g + 1 < NG:
                        turn(n, g + 1)
                    elif more:
                        turn(n + 1, 0)
                    pe.wait_ge(gelued, NCHUNK * (NG * n + g) + NCHUNK)
                    need(pe, v_made, NG * n + g - 1)
                    for i in range(4):
                        for f in range(NCHUNK):
                            ins = nc.tensor.matmul(psY[:, g % 2, i * CH:i * CH + CH], hT[:, g % 2, f, i * P:i * P + P],
                                                   s["w2"][:, f, :], start=(f == 0), stop=(f == NCHUNK - 1))
                    ins.then_inc(lowered, 1)
            turn(0, 0)
            loops(pe, body)

        @block.gpsimd
        def _(pool):
            def spread(row):
                return row.unsqueeze(1).broadcast_to([P, 4, CH])

            def body(n, d1, d2, more):
                m = n - 1
                for g in range(NG):
                    if d2:
                        pool.wait_ge(u_made, NG * m + g + 1)
                        nc.gpsimd.tensor_tensor(u[:, g % 2], u[:, g % 2], spread(s["gamma"][:]), ALU.mult).then_inc(scaled, 1)
                    if d1:
                        k = CHUNK_OF[4 * g]
                        pool.wait_ge(normed, NG * n + g + 1)
                        need(pool, v_made, NG * n + g - 1)
                        nc.gpsimd.tensor_tensor(xb[:, g % 2], xh[:, g % 2], spread(s["b2"][:]), ALU.add).then_inc(xb_made, 1)
                        if 4 * g == CHUNKS[k][0]:
                            pool.wait_ge(loaded[k], 16 * (n + 1))
                        if d2:
                            pool.wait_ge(final, NG * m + g + 1)
                        nc.gpsimd.tensor_tensor(x2b[:, 4 * g:4 * g + 4, :], x2[:, 4 * g:4 * g + 4, :], spread(s["beta"][:]),
                                                ALU.add).then_inc(x2b_made, 1)
            loops(pool, body)

        @block.vector
        def _(dve):
            chain = Chain(dve, own)
            v = nc.vector

            def norm(n, g):
                k = CHUNK_OF[4 * g]
                if 4 * g == CHUNKS[k][0]:
                    dve.wait_ge(loaded[k], 16 * (n + 1))
                need(dve, turned, NG * n + g - 1)
                need(dve, xb_made, NG * n + g - 1)
                for i in range(4):
                    t = 4 * g + i
                    r, b = (s["coef_2"][:, q, bass.ds(TPB * n + t, 1)] for q in range(2))
                    ins = v.tensor_scalar(xh[:, g % 2, i, :], x2[:, t, :], r, b, ALU.mult, ALU.add)
                ins.then_inc(normed, 1)

            def stats_of(n, g):
                dve.wait_ge(v_made, NG * n + g + 1)
                for t in range(4 * g, 4 * g + 4):
                    ins = v.bn_stats(stats[:, t, :], vv[:, t, :])
                return ins

            def body(n, d1, d2, more):
                m = n - 1
                for g in range(NG):
                    tiles = slice(4 * g, 4 * g + 4)
                    if d2:
                        need(dve, scaled, NG * m + g - 1)
                        for i in range(4):
                            t = 4 * g + i
                            ins = v.tensor_scalar(u[:, g % 2, i, :], vv[:, t, :], coef[:, 0, t:t + 1], coef[:, 1, t:t + 1],
                                                  ALU.mult, ALU.add)
                        ins.then_inc(u_made, 1)
                    if d1 and g + 1 < NG:
                        norm(n, g + 1)
                    elif more:
                        norm(n + 1, 0)
                    if d2:
                        k = CHUNK_OF[4 * g]
                        dve.wait_ge(scaled, NG * m + g + 1)
                        if 4 * g == CHUNKS[k][0]:
                            need(dve, stored[k], 16 * CHUNK_DMAS[k] * m)
                        v.tensor_tensor(o_buf[:, tiles, :], u[:, g % 2], x2b[:, tiles, :], ALU.add).then_inc(final, 1)
                    if d1:
                        if g > 0:
                            stats_of(n, g - 1)
                        dve.wait_ge(lowered, NG * n + g + 1)
                        dve.wait_ge(xb_made, NG * n + g + 1)
                        v.tensor_tensor(vv[:, tiles, :], psY[:, g % 2, :].rearrange("p (t c) -> p t c", t=4), xb[:, g % 2],
                                        ALU.add).then_inc(v_made, 1)
                if d1:
                    chain.link(stats_of(n, NG - 1))
                    chain.link(ln_coefs(nc, chain, stats, work, TPB, CH, 1.0, EPS5, coef[:, 0, :], coef[:, 1, :]))

            norm(0, 0)
            loops(dve, body, chain, COEF_STEPS + 1)


def metaformer_kernel(nc, x, l_pair, protein_pair, inter_pair, z_mask, ln_g, ln_b, lnc_g, lnc_b, Wg1, bg1, Wg2, bg2,
                      Wg3, bg3, W1, b1, W2, b2, W3, b3, Wend, bend, Wsum, bsum, Wr, br, W1e, b1e, W2e, b2e, gamma, beta, out):
    grid = lambda ap: ap.rearrange("o a b c -> (o a) b c")
    d = dict(x=grid(x), lp=grid(l_pair), pp=grid(protein_pair), ip=grid(inter_pair), zm=z_mask.rearrange("o a b -> (o a) b"),
             ln_g=ln_g, ln_b=ln_b, lnc_g=lnc_g, lnc_b=lnc_b, Wg1=Wg1, bg1=bg1, Wg2=Wg2, bg2=bg2, Wg3=Wg3, bg3=bg3,
             W1=W1, b1=b1, W2=W2, b2=b2, W3=W3, b3=b3, Wend=Wend, bend=bend, Wsum=Wsum, bsum=bsum,
             Wr=Wr, br=br, W1e=W1e, b1e=b1e, W2e=W2e, b2e=b2e, gamma=gamma, beta=beta, out=grid(out))
    scratch = lambda name, shape: nc.dram_tensor(name, shape, F32, kind="Internal").ap()
    d["s_ab"] = scratch("scratch_ab", (N, 2 * NCG, N * CC))
    d["s_pp"] = scratch("scratch_pp", (N, NCG, N * CC))
    d["s_lp"] = scratch("scratch_lp", (N, NCG, N * CC))
    d["s_q"] = scratch("scratch_q", (NBLK, P, TPB * HID))
    d["s_x2"] = scratch("scratch_x2", (NBLK, P, TPB * CH))
    with ExitStack() as ctx:
        s = {}
        for name, shape in (("ident", [P, P]), ("ones", [P, P]), ("w_all", [P, 6 * HID + CH]), ("ws2", [P, 2 * CH]),
                            ("mask", [P, NBLK * TPB]), ("coef_x", [P, 2, NBLK * TPB]), ("coef_2", [P, 2, NBLK * TPB]),
                            ("w1", [P, 2 * FF]), ("w2", [P, NCHUNK, CH]), ("b1", [P, NCHUNK]), ("b2", [P, CH]),
                            ("gamma", [P, CH]), ("beta", [P, CH])):
            s[name] = ctx.enter_context(nc.sbuf_tensor(name, shape, F32))
        setup_phase(nc, d, s)
        project_phase(nc, d, s)
        with nc.sbuf_tensor("tri", [P, NBLK * TPB, HID], F32) as tri:
            s["tri"] = tri
            triangle_phase(nc, d, s)
            with nc.psum_tensor("psR", [P, 512], F32) as psR:
                s["psR"] = psR
                mix_phase(nc, d, s)
                route_phase(nc, d, s)
        ffn_phase(nc, d, s)


_CONV = ['l_pair', 'protein_pair', 'inter_pair', 'z_mask', 'ln_g', 'ln_b', 'lnc_g', 'lnc_b', 'Wg1', 'bg1', 'Wg2', 'bg2',
         'Wg3', 'bg3', 'W1', 'b1', 'W2', 'b2', 'W3', 'b3', 'Wend', 'bend', 'Wsum', 'bsum']
_FFN = ['Wr', 'br', 'W1', 'b1', 'W2', 'b2', 'gamma', 'beta']
_INS = ['x'] + ['L0_conv_' + n for n in _CONV] + ['L0_ffn_' + n for n in _FFN]


def kernel(**inputs):
    import numpy as _np
    import concourse.bacc as _bacc
    from concourse import mybir as _mybir
    from concourse.bass_utils import run_bass_kernel_spmd as _run

    nc = _bacc.Bacc("TRN2", target_bir_lowering=False, num_devices=1)
    arrays, args = {}, []
    for name in _INS:
        a = _np.ascontiguousarray(inputs[name])
        arrays[f"in_{name}_dram"] = a
        args.append(nc.dram_tensor(f"in_{name}_dram", a.shape, _mybir.dt.from_np(a.dtype), kind="ExternalInput").ap())
    out = nc.dram_tensor("out_0_dram", (1, N, N, CH), F32, kind="ExternalOutput").ap()
    metaformer_kernel(nc, *args, out)
    r = _run(nc, [arrays], core_ids=[0])
    return r.results[0]["out_0_dram"]
```

```python
from contextlib import ExitStack

import concourse.bass as bass
from concourse import mybir

F32 = mybir.dt.float32
I32 = mybir.dt.int32
ALU = mybir.AluOpType
ACT = mybir.ActivationFunctionType
AX = mybir.AxisListType

P = 128
N = 192
CH = 128
HID = 64
BLOCK_A = 16
HALF_A = BLOCK_A // 2
NBLK = N // BLOCK_A
LOW = BLOCK_A
HIGH = HALF_A
TPB = LOW + HIGH
NB_HIGH = N - P
CC = 8
NCG = HID // CC
TOKENS = N * N
EXPERTS = 8
FF = 256
NCHUNK = 2 * FF // P
CAPACITY = -(-TOKENS * 5 // (4 * EXPERTS))
EPS5 = 1e-5
EPS6 = 1e-6
RSQRT_MAGIC = 0x5F3759DF
CHUNKS = ((0, 8), (8, 16), (16, 24))


def need(eng, sem, value):
    if isinstance(value, int) and value <= 0:
        return
    eng.wait_ge(sem, value)


LOAD_COUNT = 16 * (2 + 2)


class Chain:

    def __init__(self, eng, sem):
        self.eng, self.sem, self.count = eng, sem, 0

    def link(self, ins):
        self.count += 1
        ins.then_inc(self.sem, 1)
        self.eng.wait_ge(self.sem, self.count)


def load_tiles(eng, dst, src, n, sem, tiles=(0, TPB)):
    lo, hi = tiles
    for t in range(lo, min(hi, LOW), HALF_A):
        eng.dma_start(dst[:, t:t + HALF_A, :],
                      src[bass.ds(BLOCK_A * n + t, HALF_A), 0:P, :].rearrange("a b c -> b a c")).then_inc(sem, 16)
    if hi > LOW:
        for h in range(2):
            eng.dma_start(dst[64 * h:64 * h + 64, LOW:TPB, :],
                          src[bass.ds(BLOCK_A * n + HALF_A * h, HALF_A), P:N, :].rearrange("a b c -> b a c")
                          ).then_inc(sem, 16)


def wait_by_event(pool, sem, value, passed):
    pool.wait_ge(sem, value)
    pool.sem_inc(passed, 1)


LN_STEPS = 17


def ln_step(nc, dve, step, stepped, before, stats, work, channels, mulv, addv, rstd, shift, plus=0.0):
    v = nc.vector
    mean2, m2, diff, sq, var, t = (work[:, k, :] for k in range(6))
    y = rstd
    if step > 0:
        dve.wait_ge(stepped, before + step)
    if step == 0:
        ins = v.tensor_tensor(work[:, 0:2, :].rearrange("p k w -> p w k"), stats[:, :, 1:3], stats[:, :, 4:6], ALU.add)
    elif step == 1:
        ins = v.tensor_tensor(diff, stats[:, :, 1], stats[:, :, 4], ALU.subtract)
    elif step == 2:
        ins = v.scalar_tensor_tensor(sq, diff, 0.25 * mulv, diff, ALU.mult, ALU.mult)
    elif step == 3:
        ins = v.scalar_tensor_tensor(var, m2, mulv / channels, sq, ALU.mult, ALU.add)
    elif step == 4:
        ins = v.tensor_scalar(var, var, addv, None, ALU.add)
    elif step == 5:
        ins = v.tensor_scalar(t.bitcast(I32), var.bitcast(I32), 1, None, ALU.arith_shift_right)
    elif step == 6:
        ins = v.tensor_scalar(y.bitcast(I32), t.bitcast(I32), -1.0, float(RSQRT_MAGIC), ALU.mult, ALU.add)
    elif step < 16:
        if step % 3 == 1:
            ins = v.tensor_tensor(t, y, y, ALU.mult)
        elif step % 3 == 2:
            ins = v.scalar_tensor_tensor(t, t, -0.5, var, ALU.mult, ALU.mult)
        else:
            ins = v.scalar_tensor_tensor(y, t, 1.5, y, ALU.add, ALU.mult)
    else:
        ins = v.scalar_tensor_tensor(shift, mean2, -0.5, y, ALU.mult, ALU.mult)
    ins.then_inc(stepped, 1)


def setup_phase(nc, d, s):
    with ExitStack() as ctx:
        sb = lambda name, shape, dt=F32: ctx.enter_context(nc.sbuf_tensor(name, shape, dt))
        sem = lambda name: ctx.enter_context(nc.semaphore(name))
        zm_low = sb("zm_low", [P, N])
        zm_high = sb("zm_high", [64, N])
        ln_g, ln_b = sb("ln_g_col", [P, 1]), sb("ln_b_col", [P, 1])
        lnc_g, lnc_b = sb("lnc_g_col", [P, 1]), sb("lnc_b_col", [P, 1])
        fold = sb("fold", [P, P])
        foldc = sb("foldc", [HID, P])
        zeros = sb("zeros", [P, P])
        w_raw = sb("w_raw", [P, 512])
        ws_raw = sb("ws_raw", [P, CH])
        bias_row = sb("bias_row", [1, 640])
        ps = ctx.enter_context(nc.psum_tensor("ps_setup", [P, 6, 512], F32))
        loaded, ident_made, const_made = sem("setup_loaded"), sem("ident_made"), sem("const_made")
        folds_made, folded, zm_turned, own = sem("folds_made"), sem("folded"), sem("zm_turned"), sem("setup_own")
        block = ctx.enter_context(nc.Block())
        gate_order = ((0, "W1", "b1"), (64, "W2", "b2"), (128, "W3", "b3"),
                      (192, "Wg1", "bg1"), (256, "Wg2", "bg2"), (320, "Wg3", "bg3"))

        row = lambda ap: ap.rearrange("(o c) -> o c", o=1)
        col = lambda ap: ap.rearrange("(c o) -> c o", o=1)
        loads = [(zm_low[:], d["zm"][0:P, :]), (zm_high[:], d["zm"][P:N, :]),
                 (ln_g[:], col(d["ln_g"])), (ln_b[:], col(d["ln_b"])),
                 (w_raw[:, 384:512], d["Wend"]), (bias_row[:, 384:512], row(d["bend"])),
                 (bias_row[:, 512:640], row(d["bsum"]))]
        for off, w, b in gate_order:
            loads += [(w_raw[:, off:off + HID], d[w]), (bias_row[:, off:off + HID], row(d[b]))]
        for h in range(2):
            half = slice(HID * h, HID * h + HID)
            loads += [(lnc_g[half, :], col(d["lnc_g"])), (lnc_b[half, :], col(d["lnc_b"])), (ws_raw[half, :], d["Wsum"])]
        loads += [(s[k][:], row(d[k]).broadcast_to([P, CH])) for k in ("gamma", "beta")]
        n_loads = len(loads)

        @block.sync
        def _(sp):
            for dst, src in loads:
                sp.dma_start(dst, src).then_inc(loaded, 16)

        @block.gpsimd
        def _(pool):
            nc.gpsimd.memset(s["ident"][:], 0.0).then_inc(ident_made, 1)
            pool.wait_ge(ident_made, 1)
            nc.gpsimd.affine_select(out=s["ident"][:], in_=s["ident"][:], compare_op=ALU.not_equal, fill=1.0,
                                    base=0, pattern=[[-1, P]], channel_multiplier=1).then_inc(ident_made, 1)
            nc.gpsimd.memset(s["ones"][:], 1.0).then_inc(const_made, 1)
            nc.gpsimd.memset(zeros[:], 0.0).then_inc(const_made, 1)
            nc.gpsimd.memset(s["ws2"][:], 0.0).then_inc(const_made, 1)

        @block.vector
        def _(dve):
            dve.wait_ge(const_made, 3)
            dve.wait_ge(loaded, 16 * n_loads)
            chain = Chain(dve, own)
            v = nc.vector
            chain.link(v.tensor_tensor(ln_b[:], ln_b[:], ln_g[:], ALU.subtract))
            chain.link(v.tensor_tensor(lnc_b[:], lnc_b[:], lnc_g[:], ALU.subtract))
            v.tensor_scalar(fold[:], zeros[:], ln_b[:, 0:1], 1.0 / CH, ALU.add, ALU.mult).then_inc(folds_made, 1)
            v.tensor_scalar(foldc[:], zeros[0:HID, :], lnc_b[0:HID, 0:1], 1.0 / HID, ALU.add, ALU.mult).then_inc(folds_made, 1)
            chain.link(v.tensor_scalar(bias_row[:, 0:512], bias_row[:, 0:512], 1.0 / CH, None, ALU.mult))
            v.tensor_scalar(bias_row[:, 512:640], bias_row[:, 512:640], 1.0 / HID, None, ALU.mult).then_inc(folds_made, 1)
            dve.wait_ge(folded, 1)
            v.scalar_tensor_tensor(s["w_all"][:], w_raw[:], ln_g[:, 0:1], ps[:, 0, :], ALU.mult, ALU.add)
            dve.wait_ge(folded, 2)
            for h in range(2):
                half = slice(HID * h, HID * h + HID)
                v.scalar_tensor_tensor(s["ws2"][half, CH * h:CH * h + CH], ws_raw[half, :], lnc_g[half, 0:1],
                                       ps[half, 1, 0:CH], ALU.mult, ALU.add)
            dve.wait_ge(zm_turned, 3)
            zt = s["mask"][:].rearrange("p (n u) -> p n u", u=TPB)
            v.tensor_copy(zt[:, :, 0:LOW], ps[:, 2, 0:N].rearrange("p (n u) -> p n u", u=BLOCK_A))
            for h in range(2):
                src = ps[64 * h:64 * h + 64, 3 + h, 0:N].rearrange("p (n u) -> p n u", u=BLOCK_A)
                v.tensor_copy(zt[64 * h:64 * h + 64, :, LOW:TPB], src[:, :, HALF_A * h:HALF_A * h + HALF_A])

        @block.tensor
        def _(pe):
            pe.wait_ge(ident_made, 2)
            pe.wait_ge(loaded, 16 * n_loads)
            ident = s["ident"]
            for bank, cols in ((2, slice(0, P)), (3, slice(P, N)), (4, slice(64, N))):
                m = cols.stop - cols.start
                nc.tensor.transpose(ps[0:m, bank, 0:P], zm_low[:, cols], ident[:])
                nc.tensor.transpose(ps[0:m, bank, P:N], zm_high[:, cols], ident[0:64, 0:64]).then_inc(zm_turned, 1)
            pe.wait_ge(folds_made, 3)
            nc.tensor.matmul(ps[:, 0, :], fold[:], w_raw[:], start=True, stop=False)
            nc.tensor.matmul(ps[:, 0, :], s["ones"][0:1, :], bias_row[:, 0:512], start=False, stop=True).then_inc(folded, 1)
            nc.tensor.matmul(ps[:, 1, 0:CH], foldc[:], ws_raw[0:HID, :], start=True, stop=False)
            nc.tensor.matmul(ps[:, 1, 0:CH], s["ones"][0:1, :], bias_row[:, 512:640], start=False, stop=True).then_inc(folded, 1)


PASSES = (("x", 3, 2), ("pp", 1, 4), ("lp", 1, 4), ("ip", 1, 4))
GROUPS_A = []
for _s, (_name, _k, _size) in enumerate(PASSES):
    for _g in range(TPB // _size):
        GROUPS_A.append((_s, _g, _g * _size, _size))
NG_A = len(GROUPS_A)
PASS_END = [max(i for i, g in enumerate(GROUPS_A) if g[0] == s_) + 1 for s_ in range(len(PASSES))]


def project_phase(nc, d, s):
    with ExitStack() as ctx:
        sb = lambda name, shape, dt=F32: ctx.enter_context(nc.sbuf_tensor(name, shape, dt))
        sem = lambda name: ctx.enter_context(nc.semaphore(name))
        tiles_in = [sb(f"in_{name}", [P, TPB, CH]) for name, _, _ in PASSES]
        stats = [sb(f"stats_a{i}", [P, TPB, 6]) for i in range(len(PASSES))]
        work = sb("work_a", [P, 6, TPB])
        coef = [sb(f"coef_a{i}", [P, 2, TPB]) for i in range(len(PASSES))]
        coef_spare = sb("coef_spare", [P, 2, TPB])
        xT = sb("xT_a", [P, 2, 4 * P])
        sig = sb("sig_a", [P, 2, 2 * 3 * HID])
        ab3 = sb("ab3_a", [P, TPB, HID])
        ip_prod = sb("ip_prod", [P, 2, 4 * HID])
        q_out = sb("q_out", [P, TPB, HID])
        low_out = [sb("low_ab", [P, 2 * NCG, LOW, CC]), sb("low_pp", [P, NCG, LOW, CC]), sb("low_lp", [P, NCG, LOW, CC])]
        high_out = [sb("high_ab", [P, 2 * NCG, HIGH, CC]), sb("high_pp", [P, NCG, HIGH, CC]), sb("high_lp", [P, NCG, HIGH, CC])]
        psT = ctx.enter_context(nc.psum_tensor("psT_a", [P, 2, 512], F32))
        psZ = ctx.enter_context(nc.psum_tensor("psZ_a", [P, 3, 2, 512], F32))
        loaded = [sem(f"loaded_{name}") for name, _, _ in PASSES]
        statted, coefs_ready, own, pool_passed = sem("statted"), sem("coefs_ready"), sem("coef_stepped_a"), sem("pool_passed_a")
        ip_made = sem("ip_made")
        normed_act, normed_pool = sem("normed_act"), sem("normed_pool")
        turned, copied, projected = sem("turned"), sem("copied"), sem("projected")
        gated, masked, multiplied = sem("gated"), sem("masked"), sem("multiplied")
        stored = [sem("stored_ab"), sem("stored_pp"), sem("stored_lp"), sem("stored_q")]
        block = ctx.enter_context(nc.Block())
        srcs = [d[name] for name, _, _ in PASSES]

        def ahead(G, step, last):
            if G + step < NG_A:
                return G + step, GROUPS_A[G + step]
            return None if last else (G + step, GROUPS_A[G + step - NG_A])

        def act_tiles(t0, size):
            return [t0]

        def pool_tiles(t0, size):
            return list(range(t0 + 1, t0 + size))

        def loops(eng, body):
            body(0, False)
            with eng.Fori(1, NBLK - 1) as n:
                body(n, False)
            body(NBLK - 1, True)

        @block.sync
        def _(sp):
            for i in range(len(PASSES)):
                load_tiles(sp, tiles_in[i], srcs[i], 0, loaded[i])

            def body(n, last):
                for i in range(len(PASSES)):
                    if not last:
                        sp.wait_ge(turned, NG_A * n + PASS_END[i])
                        load_tiles(sp, tiles_in[i], srcs[i], n + 1, loaded[i])
                    sp.wait_ge(multiplied, NG_A * n + PASS_END[i])
                    if i < 3:
                        dst = (d["s_ab"], d["s_pp"], d["s_lp"])[i]
                        sp.dma_start(dst[0:P, :, bass.ds(CC * BLOCK_A * n, CC * BLOCK_A)],
                                     low_out[i][:].rearrange("p g a c -> p g (a c)")).then_inc(stored[i], 16)
                        for h in range(2):
                            sp.dma_start(dst[P:N, :, bass.ds(CC * BLOCK_A * n + CC * HALF_A * h, CC * HALF_A)],
                                         high_out[i][64 * h:64 * h + 64].rearrange("p g a c -> p g (a c)")
                                         ).then_inc(stored[i], 16)
                    else:
                        sp.dma_start(d["s_q"][bass.ds(n, 1)].rearrange("o p c -> (o p) c"),
                                     q_out[:].rearrange("p t c -> p (t c)")).then_inc(stored[3], 16)
            loops(sp, body)
            for i in range(3):
                sp.wait_ge(stored[i], 48 * NBLK)
            sp.wait_ge(stored[3], 16 * NBLK)

        def norm(wait, engine_op, sem_out, n, G, which, last):
            nxt = ahead(G, 2, last)
            if nxt is None:
                return
            count, (i, g, t0, size) = nxt
            wrap = count >= NG_A
            if g == 0:
                wait(coefs_ready, len(PASSES) * (n + (1 if wrap else 0)) + i + 1)
            ins = None
            for t in which(t0, size):
                ins = engine_op(tiles_in[i][:, t, :], coef[i][:, 0, t:t + 1], coef[i][:, 1, t:t + 1])
            ins.then_inc(sem_out, 1)

        @block.scalar
        def _(act):
            def op(x, r, b):
                return nc.scalar.activation(x, x, ACT.Identity, bias=b, scale=r)

            def copy_turned(n, count, grp):
                i, g, t0, size = grp
                act.wait_ge(turned, NG_A * n + count + 1)
                need(act, projected, NG_A * n + count - 1)
                nc.scalar.copy(xT[:, count % 2, 0:size * P], psT[:, count % 2, 0:size * P]).then_inc(copied, 1)

            def body(n, last):
                for G, (i, g, t0, size) in enumerate(GROUPS_A):
                    norm(act.wait_ge, op, normed_act, n, G, act_tiles, last)
                    nxt = ahead(G, 1, last)
                    if nxt:
                        copy_turned(n, *nxt)
                    k = PASSES[i][1]
                    act.wait_ge(projected, NG_A * n + G + 1)
                    if i == 0:
                        z = psZ[:, G % 3, :, 3 * HID:6 * HID]
                    else:
                        z = psZ[:, G % 3, 0, :].rearrange("p (t c) -> p t c", t=size)[:, :, HID:2 * HID]
                    need(act, multiplied, NG_A * n + G - 1)
                    nc.scalar.activation(sig[:, G % 2, 0:size * k * HID].rearrange("p (t c) -> p t c", t=size),
                                         z, ACT.Sigmoid).then_inc(gated, 1)

            for G in (-2, -1):
                norm(act.wait_ge, op, normed_act, 0, G, act_tiles, False)
            copy_turned(0, 0, GROUPS_A[0])
            loops(act, body)

        @block.gpsimd
        def _(pool):
            def op(x, r, b):
                return nc.gpsimd.tensor_scalar(x, x, r, b, ALU.mult, ALU.add)

            def wait(sem, value):
                wait_by_event(pool, sem, value, pool_passed)

            def body(n, last):
                for G, (i, g, t0, size) in enumerate(GROUPS_A):
                    norm(wait, op, normed_pool, n, G, pool_tiles, last)
                    if i == 0:
                        pool.wait_ge(gated, NG_A * n + G + 1)
                        gates = sig[:, G % 2, 0:size * 3 * HID].rearrange("p (t c) -> p t c", t=size)
                        zm = s["mask"][:, bass.ds(TPB * n + t0, size)].unsqueeze(2).broadcast_to([P, size, 3 * HID])
                        nc.gpsimd.tensor_tensor(gates, gates, zm, ALU.mult).then_inc(masked, 1)

            for G in (-2, -1):
                norm(wait, op, normed_pool, 0, G, pool_tiles, False)
            loops(pool, body)

        @block.tensor
        def _(pe):
            w = s["w_all"]
            pair1 = w[:, 0:6 * HID].rearrange("p (q k c) -> p q k c", q=2, k=3)
            rhs = [w[:, 0:6 * HID], pair1[:, :, 1, :], pair1[:, :, 0, :], pair1[:, :, 0, :]]

            def turn(n, count, grp):
                i, g, t0, size = grp
                pe.wait_ge(normed_act, NG_A * n + count + 1)
                pe.wait_ge(normed_pool, NG_A * n + count + 1)
                need(pe, copied, NG_A * n + count - 1)
                for j in range(size):
                    ins = nc.tensor.transpose(psT[:, count % 2, j * P:j * P + P], tiles_in[i][:, t0 + j, :], s["ident"][:])
                ins.then_inc(turned, 1)

            def body(n, last):
                for G, (i, g, t0, size) in enumerate(GROUPS_A):
                    nxt = ahead(G, 1, last)
                    if nxt:
                        turn(n, *nxt)
                    pe.wait_ge(copied, NG_A * n + G + 1)
                    need(pe, multiplied, NG_A * n + G - 2)
                    for j in range(size):
                        out = psZ[:, G % 3, j, 0:6 * HID] if i == 0 else psZ[:, G % 3, 0, j * P:j * P + P]
                        ins = nc.tensor.matmul(out, xT[:, G % 2, j * P:j * P + P], rhs[i], start=True, stop=True)
                    ins.then_inc(projected, 1)

            turn(0, 0, GROUPS_A[0])
            loops(pe, body)

        @block.vector
        def _(dve):
            v = nc.vector
            NP = len(PASSES)
            steps = LN_STEPS + 1

            def stats_of(n, i, tiles):
                if tiles[0] == 0:
                    dve.wait_ge(loaded[i], LOAD_COUNT * (n + 1))
                for t in tiles:
                    ins = v.bn_stats(stats[i][:, t, :], tiles_in[i][:, t, :])
                if tiles[-1] == TPB - 1:
                    ins.then_inc(statted, 1)

            def coef_step(n, i, step):
                before = steps * (NP * n + i)
                mulv, addv = (1.0 + EPS5, EPS5 * EPS6) if i == 0 else (1.0, EPS5)
                if step == 0:
                    dve.wait_ge(statted, NP * n + i + 1)
                    if i == 0:
                        need(dve, turned, NG_A * (n - 1) + PASS_END[0])
                if step < LN_STEPS:
                    ln_step(nc, dve, step, own, before, stats[i], work, CH, mulv, addv, coef[i][:, 0, :], coef[i][:, 1, :])
                elif step == LN_STEPS:
                    dve.wait_ge(own, before + LN_STEPS)
                    v.tensor_scalar(coef[i][:, 1, :], coef[i][:, 1, :], 1.0, None, ALU.add).then_inc(own, 1)
                else:
                    dve.wait_ge(own, before + steps)
                    v.tensor_copy(s["coef_x"][:, :, bass.ds(TPB * n, TPB)] if i == 0 else coef_spare[:],
                                  coef[i][:]).then_inc(coefs_ready, 1)

            def body(n, last):
                for G, (i, g, t0, size) in enumerate(GROUPS_A):
                    groups = TPB // size
                    per = -(-(steps + 1) // (groups - 2))
                    share = [k for k in range(per * g, per * g + per) if k <= steps]
                    todo_stats = list(range(t0, t0 + size))
                    if last and i + 1 >= NP:
                        share = []
                    if last and i + 2 >= NP:
                        todo_stats = []
                    wrap1, wrap2 = (i + 1) // NP, (i + 2) // NP
                    for k in range(max(len(share), len(todo_stats))):
                        if k < len(share):
                            coef_step(n + wrap1, (i + 1) % NP, share[k])
                        if k < len(todo_stats):
                            stats_of(n + wrap2, (i + 2) % NP, todo_stats[k:k + 1])
                    if i == 0:
                        dve.wait_ge(masked, (TPB // 2) * n + g + 1)
                    else:
                        dve.wait_ge(gated, NG_A * n + G + 1)
                    if g == 0:
                        need(dve, stored[i], (48 if i < 3 else 16) * n)
                    if i < 3:
                        out = low_out[i][:, :, t0:t0 + size, :] if t0 < LOW else high_out[i][:, :, t0 - LOW:t0 - LOW + size, :]
                        out = out.rearrange("p g a c -> p a g c")
                    gate = sig[:, G % 2, :]
                    if i == 0:
                        z = psZ[:, G % 3, :, :]
                        gate = gate.rearrange("p (t c) -> p t c", t=size)
                        v.tensor_tensor(out, z[:, :, 0:2 * HID].rearrange("p t (g c) -> p t g c", c=CC),
                                        gate[:, :, 0:2 * HID].rearrange("p t (g c) -> p t g c", c=CC), ALU.mult)
                        v.tensor_tensor(ab3[:, t0:t0 + size, :], z[:, :, 2 * HID:3 * HID], gate[:, :, 2 * HID:3 * HID],
                                        ALU.mult).then_inc(multiplied, 1)
                    else:
                        z = psZ[:, G % 3, 0, :].rearrange("p (t c) -> p t c", t=size)[:, :, 0:HID]
                        gate = gate[:, 0:size * HID].rearrange("p (t c) -> p t c", t=size)
                        if i < 3:
                            v.tensor_tensor(out, z.rearrange("p t (g c) -> p t g c", c=CC),
                                            gate.rearrange("p t (g c) -> p t g c", c=CC), ALU.mult).then_inc(multiplied, 1)
                        else:
                            prod = ip_prod[:, g % 2, :].rearrange("p (t c) -> p t c", t=size)
                            v.tensor_tensor(prod, z, gate, ALU.mult).then_inc(ip_made, 1)
                            dve.wait_ge(ip_made, (TPB // 4) * n + g + 1)
                            v.tensor_tensor(q_out[:, t0:t0 + size, :], prod, ab3[:, t0:t0 + size, :], ALU.mult
                                            ).then_inc(multiplied, 1)

            stats_of(0, 0, list(range(TPB)))
            for k in range(steps + 1):
                coef_step(0, 0, k)
            stats_of(0, 1, list(range(TPB)))
            loops(dve, body)


def triangle_phase(nc, d, s):
    with ExitStack() as ctx:
        sb = lambda name, shape, dt=F32: ctx.enter_context(nc.sbuf_tensor(name, shape, dt))
        sem = lambda name: ctx.enter_context(nc.semaphore(name))
        pp_low = [sb(f"pp_low{i}", [P, N, CC]) for i in range(2)]
        ab2_low = [sb(f"ab2_low{i}", [P, N, CC]) for i in range(2)]
        lp_low = [sb(f"lp_low{i}", [P, N, CC]) for i in range(2)]
        ab1_low = [sb(f"ab1_low{i}", [P, N, CC]) for i in range(2)]
        ab1_high = [sb(f"ab1_high{i}", [64, N, CC]) for i in range(2)]
        mov_high = [sb(f"mov_high{i}", [P, N, CC]) for i in range(2)]
        sta_high = [sb(f"sta_high{i}", [P, N, CC]) for i in range(2)]
        ab1T = sb("ab1T", [P, 2, N])
        psT = ctx.enter_context(nc.psum_tensor("psT_b", [P, 2, 512], F32))
        psO = ctx.enter_context(nc.psum_tensor("psO_b", [P, 4, 512], F32))
        loaded = [sem("loaded_even"), sem("loaded_odd")]
        turned, copied, summed, taken = sem("turned_b"), sem("copied_b"), sem("summed_b"), sem("taken_b")
        block = ctx.enter_context(nc.Block())
        N_LOADS = 8

        def loops(eng, body):
            body(0, False)
            with eng.Fori(1, NCG // 2 - 1) as m:
                body(m, False)
            body(NCG // 2 - 1, True)

        @block.sync
        def _(sp):
            def body(m, last):
                for par in range(2):
                    g = 2 * m + par
                    need(sp, summed, CC * (g - 2) + CC if not isinstance(m, int) or m > 0 else 0)
                    view = lambda src, lo, hi, k: src[lo:hi, bass.ds(g + k, 1), :].rearrange("b o c -> b (o c)")
                    flat = lambda t: t.rearrange("p a c -> p (a c)")
                    for dst, src in ((pp_low[par][:], view(d["s_pp"], 0, P, 0)), (ab1_low[par][:], view(d["s_ab"], 0, P, 0)),
                                     (ab1_high[par][:], view(d["s_ab"], P, N, 0)), (ab2_low[par][:], view(d["s_ab"], 0, P, NCG)),
                                     (lp_low[par][:], view(d["s_lp"], 0, P, 0)), (mov_high[par][0:64], view(d["s_pp"], P, N, 0)),
                                     (mov_high[par][64:P], view(d["s_ab"], P, N, NCG)),
                                     (sta_high[par][64:P], view(d["s_lp"], P, N, 0))):
                        sp.dma_start(flat(dst), src).then_inc(loaded[par], 16)
            loops(sp, body)

        @block.tensor
        def _(pe):
            ident = s["ident"]

            def turn(m, par, c):
                C = CC * par + c
                if c == 0:
                    pe.wait_ge(loaded[par], 16 * N_LOADS * (m + 1))
                need(pe, copied, 2 * CC * m + C - 1)
                lo, hi, t = ab1_low[par], ab1_high[par], psT[:, C % 2, :]
                nc.tensor.transpose(t[:, 0:P], lo[:, 0:P, c], ident[:])
                nc.tensor.transpose(t[:, P:N], hi[:, 0:P, c], ident[0:64, 0:64])
                nc.tensor.transpose(t[0:64, N:N + P], lo[:, P:N, c], ident[:])
                nc.tensor.transpose(t[0:64, N + P:2 * N], hi[:, P:N, c], ident[0:64, 0:64]).then_inc(turned, 1)

            def body(m, last):
                for C in range(2 * CC):
                    par, c = divmod(C, CC)
                    if C + 1 < 2 * CC:
                        turn(m, *divmod(C + 1, CC))
                    elif not last:
                        turn(m + 1, 0, 0)
                    pe.wait_ge(copied, 2 * CC * m + C + 1)
                    need(pe, taken, 2 * CC * m + C - 3)
                    out = psO[:, C % 4, :]
                    steps = ((ab1T[:, C % 2, :], pp_low[par][:, :, c]), (lp_low[par][:, :, c], ab2_low[par][:, :, c]),
                             (sta_high[par][:, :, c], mov_high[par][:, :, c]))
                    for k, (sta, mov) in enumerate(steps):
                        nc.tensor.matmul(out[:, 0:N], sta[:, 0:P], mov, start=(k == 0), stop=(k == 2))
                    for h in range(2):
                        for k, (sta, mov) in enumerate(steps):
                            part = mov.rearrange("p (n u) -> p n u", u=BLOCK_A)[:, :, HALF_A * h:HALF_A * h + HALF_A]
                            ins = nc.tensor.matmul(out[64 * h:64 * h + 64, N:N + N // 2], sta[:, P:N], part,
                                                   start=(k == 0), stop=(k == 2))
                    ins.then_inc(summed, 1)

            turn(0, 0, 0)
            loops(pe, body)

        @block.scalar
        def _(act):
            def body(m, last):
                for C in range(2 * CC):
                    par, c = divmod(C, CC)
                    act.wait_ge(turned, 2 * CC * m + C + 1)
                    need(act, summed, 2 * CC * m + C - 1)
                    nc.scalar.copy(ab1T[:, C % 2, :], psT[:, C % 2, 0:N])
                    nc.scalar.copy(sta_high[par][0:64, :, c], psT[0:64, C % 2, N:2 * N]).then_inc(copied, 1)
            loops(act, body)

        @block.vector
        def _(dve):
            tri = s["tri"][:].rearrange("p (n u) c -> p n u c", u=TPB)

            def body(m, last):
                for C in range(2 * CC):
                    dve.wait_ge(summed, 2 * CC * m + C + 1)
                    src = psO[:, C % 4, :]
                    at = bass.ds(2 * CC * m + C, 1)
                    nc.vector.tensor_copy(tri[:, :, 0:LOW, at].rearrange("p n u o -> p n (u o)"),
                                          src[:, 0:N].rearrange("p (n u) -> p n u", u=LOW))
                    nc.vector.tensor_copy(tri[:, :, LOW:TPB, at].rearrange("p n u o -> p n (u o)"),
                                          src[:, N:N + N // 2].rearrange("p (n u) -> p n u", u=HIGH)).then_inc(taken, 1)
            loops(dve, body)


PAIRS = TPB // 2
CHUNK_OF = [k for k, (lo, hi) in enumerate(CHUNKS) for _ in range(lo, hi)]
CHUNK_DMAS = (1, 1, 2)


def mix_phase(nc, d, s):
    with ExitStack() as ctx:
        sb = lambda name, shape, dt=F32: ctx.enter_context(nc.sbuf_tensor(name, shape, dt))
        sem = lambda name: ctx.enter_context(nc.semaphore(name))
        x_in, x2 = sb("x_in_c", [P, 2, TPB, CH]), sb("x2_c", [P, 2, TPB, CH])
        q_in = sb("q_in", [P, TPB, HID])
        coef_x, coef_t = sb("coef_x_now", [P, 2, 2, TPB]), sb("coef_t", [P, 2, 2, TPB])
        coef_2 = sb("coef_2_now", [P, 2, TPB])
        xh, tri_n = sb("xh_c", [P, 3, 2, CH]), sb("tri_n", [P, 3, 2, HID])
        xT, gate, y = sb("xT_c", [P, 2, 3 * P]), sb("end_gate", [P, 2, 2, CH]), sb("y_c", [P, 2, 2, CH])
        stats_t, stats_x = sb("stats_t", [P, TPB, 6]), sb("stats_x2", [P, 2, TPB, 6])
        work = sb("work_c", [P, 6, TPB])
        psT = ctx.enter_context(nc.psum_tensor("psT_c", [P, 2, 512], F32))
        psZ = ctx.enter_context(nc.psum_tensor("psZ_c", [P, 2, 512], F32))
        psW = ctx.enter_context(nc.psum_tensor("psW_c", [P, 2, 512], F32))
        chunk_sems = lambda name: [sem(f"{name}_{k}") for k in range(len(CHUNKS))]
        loaded_q = chunk_sems("loaded_qc")
        loaded_x = [chunk_sems(f"loaded_xc{par}") for par in range(2)]
        stored = [chunk_sems(f"stored_x2{par}") for par in range(2)]
        coefx_ready, normed_act, normed_pool = sem("coefx_ready"), sem("normed_act_c"), sem("normed_pool_c")
        tri_normed, turned, copied, projected, gated, tri_projected = (
            sem(k) for k in ("tri_normed", "turned_c", "copied_c", "projected_c", "gated_c", "tri_projected"))
        added, statted_t, statted_x, pool_passed = sem("added"), sem("statted_t"), sem("statted_x"), sem("pool_passed_c")
        stepped_t, stepped_x, coefst_ready, coefs2_ready = (
            sem(k) for k in ("stepped_t", "stepped_x2", "coefst_ready", "coefs2_ready"))
        y_made, x2_made, routed = sem("y_made"), sem("x2_made"), sem("routed")
        block = ctx.enter_context(nc.Block())
        T0_SLOTS = TPB // 4
        ROUTE_SLOTS = range(PAIRS - TPB // 4, PAIRS)

        def loops(eng, slot, tail=False):
            for par in range(2):
                for j in range(PAIRS):
                    slot(0, par, j)
            with eng.Fori(1, NBLK // 2 - 1) as m:
                for par in range(2):
                    for j in range(PAIRS):
                        slot(m, par, j)
            for par in range(2):
                for j in range(PAIRS):
                    slot(NBLK // 2 - 1, par, j)
            if tail:
                for j in range(PAIRS):
                    slot(NBLK // 2, 0, j)

        def there(m, par):
            return not isinstance(m, int) or 0 <= 2 * m + par < NBLK

        def after(m, par, j, k):
            if j + k >= PAIRS:
                m, par, j = (m, 1, j - PAIRS) if par == 0 else (m + 1, 0, j - PAIRS)
            return (m, par, j + k) if there(m, par) else None

        def next_block(m, par):
            return (m, 1) if par == 0 else (m + 1, 0)

        def last_block(m, par):
            return (m, 0) if par == 1 else (m - 1, 1)

        @block.sync
        def _(sp):
            def load_q(n, k):
                lo, hi = CHUNKS[k]
                sp.dma_start(q_in[:, lo:hi, :].rearrange("p t c -> p (t c)"),
                             d["s_q"][bass.ds(n, 1), :, lo * HID:hi * HID].rearrange("o p c -> (o p) c")
                             ).then_inc(loaded_q[k], 16)

            for par in range(2):
                for k, ch in enumerate(CHUNKS):
                    if par == 0:
                        load_q(0, k)
                    load_tiles(sp, x_in[:, par], d["x"], par, loaded_x[par][k], ch)
            for k, (lo, hi) in enumerate(CHUNKS):
                sp.wait_ge(added, hi // 4)
                load_q(1, k)

            def slot(m, par, j):
                n = 2 * m + par
                for k, (lo, hi) in enumerate(CHUNKS):
                    if j == hi // 4 - 1 and there(m + 1, par):
                        sp.wait_ge(added, T0_SLOTS * (n + 1) + hi // 4)
                        load_q(n + 2, k)
                    if j == hi // 2 - 1:
                        sp.wait_ge(x2_made, PAIRS * n + hi // 2)
                        sp.dma_start(d["s_x2"][bass.ds(n, 1), :, lo * CH:hi * CH].rearrange("o p c -> (o p) c"),
                                     x2[:, par, lo:hi, :].rearrange("p t c -> p (t c)")).then_inc(stored[par][k], 16)
                        if there(m + 1, par):
                            load_tiles(sp, x_in[:, par], d["x"], n + 2, loaded_x[par][k], (lo, hi))
            loops(sp, slot)
            for par in range(2):
                for k in range(len(CHUNKS)):
                    sp.wait_ge(stored[par][k], 16 * NBLK // 2)

        def norm_x(wait, op, sem_out, m, par, j, which):
            n, t = 2 * m + par, 2 * j + which
            k = CHUNK_OF[t]
            if j == 0:
                wait(coefx_ready, n + 1)
            if 2 * j == CHUNKS[k][0]:
                wait(loaded_x[par][k], 16 * CHUNK_DMAS[k] * (m + 1))
            if not isinstance(m, int) or PAIRS * n + j > 2:
                wait(turned, PAIRS * n + j - 2)
            op(xh[:, j % 3, which, :], x_in[:, par, t, :], coef_x[:, par, 0, t:t + 1], coef_x[:, par, 1, t:t + 1]
               ).then_inc(sem_out, 1)

        @block.scalar
        def _(act):
            def op(out, x, r, b):
                return nc.scalar.activation(out, x, ACT.Identity, bias=b, scale=r)

            def copy_turned(m, par, j):
                c = PAIRS * (2 * m + par) + j
                act.wait_ge(turned, c + 1)
                need(act, tri_projected, c - 1)
                nc.scalar.copy(xT[:, j % 2, :], psT[:, j % 2, 0:3 * P]).then_inc(copied, 1)

            def slot(m, par, j):
                c = PAIRS * (2 * m + par) + j
                two, one = after(m, par, j, 2), after(m, par, j, 1)
                if two:
                    norm_x(act.wait_ge, op, normed_act, *two, 0)
                if one:
                    copy_turned(*one)
                act.wait_ge(projected, c + 1)
                need(act, y_made, c - 1)
                nc.scalar.activation(gate[:, j % 2], psZ[:, j % 2, 0:2 * CH].rearrange("p (t c) -> p t c", t=2),
                                     ACT.Sigmoid).then_inc(gated, 1)

            for j in range(2):
                norm_x(act.wait_ge, op, normed_act, 0, 0, j, 0)
            copy_turned(0, 0, 0)
            loops(act, slot)

        @block.gpsimd
        def _(pool):
            def op(out, x, r, b):
                return nc.gpsimd.tensor_scalar(out, x, r, b, ALU.mult, ALU.add)

            def wait(sem, value):
                wait_by_event(pool, sem, value, pool_passed)

            def add_q(m, par, g):
                n, k = 2 * m + par, CHUNK_OF[4 * g]
                if 4 * g == CHUNKS[k][0]:
                    pool.wait_ge(loaded_q[k], 16 * (n + 1))
                tiles = s["tri"][:, bass.ds(TPB * n + 4 * g, 4), :]
                nc.gpsimd.tensor_tensor(tiles, tiles, q_in[:, 4 * g:4 * g + 4, :], ALU.add).then_inc(added, 1)

            def slot(m, par, j):
                n = 2 * m + par
                two = after(m, par, j, 2)
                if two:
                    norm_x(wait, op, normed_pool, *two, 1)
                if j < T0_SLOTS and there(*next_block(m, par)):
                    add_q(*next_block(m, par), j)
                k = CHUNK_OF[2 * j]
                pool.wait_ge(y_made, PAIRS * n + j + 1)
                if 2 * j == CHUNKS[k][0]:
                    need(pool, stored[par][k], 16 * m)
                if j == 0:
                    need(pool, routed, len(ROUTE_SLOTS) * (n - 1))
                nc.gpsimd.tensor_tensor(x2[:, par, 2 * j:2 * j + 2, :], y[:, j % 2], x_in[:, par, 2 * j:2 * j + 2, :],
                                        ALU.add).then_inc(x2_made, 1)

            for g in range(T0_SLOTS):
                add_q(0, 0, g)
            for j in range(2):
                norm_x(wait, op, normed_pool, 0, 0, j, 1)
            loops(pool, slot)

        @block.tensor
        def _(pe):
            w_end = s["w_all"][:, 6 * HID:6 * HID + CH]

            def turn(m, par, j):
                c = PAIRS * (2 * m + par) + j
                pe.wait_ge(normed_act, c + 1)
                pe.wait_ge(normed_pool, c + 1)
                need(pe, copied, c - 1)
                for i in range(2):
                    nc.tensor.transpose(psT[:, j % 2, i * P:i * P + P], xh[:, j % 3, i, :], s["ident"][:])
                pe.wait_ge(tri_normed, c + 1)
                nc.tensor.transpose(psT[:, j % 2, 2 * P:3 * P], tri_n[:, j % 3].rearrange("p t c -> p (t c)"), s["ident"][:]
                                    ).then_inc(turned, 1)

            def slot(m, par, j):
                n = 2 * m + par
                c = PAIRS * n + j
                if there(m, par):
                    one = after(m, par, j, 1)
                    if one:
                        turn(*one)
                    pe.wait_ge(copied, c + 1)
                    need(pe, gated, c - 1)
                    for i in range(2):
                        ins = nc.tensor.matmul(psZ[:, j % 2, CH * i:CH * i + CH], xT[:, j % 2, i * P:i * P + P], w_end,
                                               start=True, stop=True)
                    ins.then_inc(projected, 1)
                    need(pe, y_made, c - 1)
                    nc.tensor.matmul(psW[:, j % 2, 0:2 * CH], xT[:, j % 2, 2 * P:3 * P], s["ws2"][:], start=True, stop=True
                                     ).then_inc(tri_projected, 1)
                if j in ROUTE_SLOTS and there(*last_block(m, par)):
                    if j == ROUTE_SLOTS[0]:
                        pe.wait_ge(coefs2_ready, n)
                    for t in range(4 * (j - ROUTE_SLOTS[0]), 4 * (j - ROUTE_SLOTS[0]) + 4):
                        ins = nc.tensor.matmul(s["psR"][0:1, 0:CH], coef_2[:, 0, t:t + 1], x2[:, 1 - par, t, :],
                                               start=False, stop=False)
                    ins.then_inc(routed, 1)

            nc.tensor.matmul(s["psR"][0:1, 0:CH], s["ones"][0:HID, 0:1], s["ws2"][0:HID, CH:2 * CH], start=True, stop=False)
            turn(0, 0, 0)
            loops(pe, slot, True)

        @block.vector
        def _(dve):
            v = nc.vector
            steps_t, steps_x = LN_STEPS + 2, LN_STEPS + 1

            def coef_x_of(m, par):
                n = 2 * m + par
                v.tensor_copy(coef_x[:, par], s["coef_x"][:, :, bass.ds(TPB * n, TPB)]).then_inc(coefx_ready, 1)

            def stats_tri(m, par, g):
                n = 2 * m + par
                dve.wait_ge(added, T0_SLOTS * n + g + 1)
                for t in range(4 * g, 4 * g + 4):
                    ins = v.bn_stats(stats_t[:, t, :], s["tri"][:, bass.ds(TPB * n + t, 1), :].rearrange("p o c -> p (o c)"))
                if g == T0_SLOTS - 1:
                    ins.then_inc(statted_t, 1)

            def coef_step_t(m, par, step):
                n = 2 * m + par
                before = (LN_STEPS + 1) * n
                now = coef_t[:, par]
                if step < LN_STEPS:
                    if step == 0:
                        dve.wait_ge(statted_t, n + 1)
                    ln_step(nc, dve, step, stepped_t, before, stats_t, work, HID, 1.0, EPS5, now[:, 0, :], now[:, 1, :])
                elif step == LN_STEPS:
                    dve.wait_ge(stepped_t, before + LN_STEPS)
                    v.tensor_scalar(now[:, 1, :], now[:, 1, :], 1.0, None, ALU.add).then_inc(stepped_t, 1)
                else:
                    dve.wait_ge(stepped_t, before + LN_STEPS + 1)
                    zm = s["mask"][:, bass.ds(TPB * n, TPB)].unsqueeze(1).broadcast_to([P, 2, TPB])
                    v.tensor_tensor(now, now, zm, ALU.mult).then_inc(coefst_ready, 1)

            def norm_tri(m, par, j):
                n = 2 * m + par
                if j == 0:
                    dve.wait_ge(coefst_ready, n + 1)
                need(dve, turned, PAIRS * n + j - 2)
                for i in range(2):
                    t = 2 * j + i
                    ins = v.tensor_scalar(tri_n[:, j % 3, i, :], s["tri"][:, bass.ds(TPB * n + t, 1), :].rearrange("p o c -> p (o c)"),
                                          coef_t[:, par, 0, t:t + 1], coef_t[:, par, 1, t:t + 1], ALU.mult, ALU.add)
                ins.then_inc(tri_normed, 1)

            def stats_x2(m, par, j):
                n = 2 * m + par
                dve.wait_ge(x2_made, PAIRS * n + j + 1)
                for t in (2 * j, 2 * j + 1):
                    ins = v.bn_stats(stats_x[:, par, t, :], x2[:, par, t, :])
                if j == PAIRS - 1:
                    ins.then_inc(statted_x, 1)

            def coef_step_x2(m, par, step):
                n = 2 * m + par
                before = LN_STEPS * n
                if step == 0:
                    dve.wait_ge(statted_x, n + 1)
                    need(dve, routed, len(ROUTE_SLOTS) * n)
                if step < LN_STEPS:
                    ln_step(nc, dve, step, stepped_x, before, stats_x[:, par], work, CH, 1.0, EPS5, coef_2[:, 0, :], coef_2[:, 1, :])
                else:
                    dve.wait_ge(stepped_x, before + LN_STEPS)
                    v.tensor_copy(s["coef_2"][:, :, bass.ds(TPB * n, TPB)], coef_2[:]).then_inc(coefs2_ready, 1)

            def slot(m, par, j):
                n = 2 * m + par
                now, ahead, behind = there(m, par), there(*next_block(m, par)), there(*last_block(m, par))
                two = after(m, par, j, 2)
                per_x, per_t = 4, 5
                for part in range(per_t):
                    if behind and 1 <= j < 6 and part < per_x and per_x * (j - 1) + part < steps_x:
                        coef_step_x2(*last_block(m, par), per_x * (j - 1) + part)
                    if ahead and 6 <= j < PAIRS - 2 and per_t * (j - 6) + part < steps_t:
                        coef_step_t(*next_block(m, par), per_t * (j - 6) + part)
                    if part == 0 and two:
                        norm_tri(*two)
                    if part == 1 and now:
                        if j == 0 and ahead:
                            coef_x_of(*next_block(m, par))
                        c = PAIRS * n + j
                        dve.wait_ge(tri_projected, c + 1)
                        dve.wait_ge(gated, c + 1)
                        need(dve, x2_made, c - 1)
                        v.tensor_tensor(y[:, j % 2], psW[:, j % 2, 0:2 * CH].rearrange("p (t c) -> p t c", t=2),
                                        gate[:, j % 2], ALU.mult).then_inc(y_made, 1)
                    if part == 2:
                        if j > 0 and now:
                            stats_x2(m, par, j - 1)
                        if j == 0 and behind:
                            stats_x2(*last_block(m, par), PAIRS - 1)
                    if part == 3 and j < T0_SLOTS and ahead:
                        stats_tri(*next_block(m, par), j)

            coef_x_of(0, 0)
            for g in range(T0_SLOTS):
                stats_tri(0, 0, g)
            for step in range(steps_t):
                coef_step_t(0, 0, step)
            for j in range(2):
                norm_tri(0, 0, j)
            loops(dve, slot, True)


def route_phase(nc, d, s):
    with ExitStack() as ctx:
        sb = lambda name, shape, dt=F32: ctx.enter_context(nc.sbuf_tensor(name, shape, dt))
        sem = lambda name: ctx.enter_context(nc.semaphore(name))
        E = EXPERTS
        wr, br = sb("wr", [CH, E]), sb("br", [1, E])
        shift_sum = sb("shift_sum", [P, 1])
        mean, mean_col = sb("mean_row", [1, CH]), sb("mean_col", [CH, 1])
        vec = sb("router_rows", [1, 12, E])
        scal = sb("router_scalars", [1, 16])
        sq = sb("router_squares", [1, 3, E, E])
        pick = sb("router_picks", [1, 2, E])
        pick_v = sb("router_pick_v", [1, 2, E])
        chosen, w_pair = sb("chosen", [1, 2], I32), sb("w_pair", [1, 2])
        chosen_f, val = sb("chosen_f", [1, 2]), sb("chosen_val", [1, 2])
        w_col = sb("w_col", [P, 2])
        w2_raw, b2_raw = sb("w2_raw", [P, NCHUNK, CH]), sb("b2_raw", [1, 2, CH])
        b2_row, b1_rows = sb("b2_row", [1, CH]), sb("b1_rows", [NCHUNK, P])
        ps = ctx.enter_context(nc.psum_tensor("ps_route", [P, 4, 512], F32))
        loaded, below_made, own, own_a = sem("route_loaded"), sem("below_made"), sem("dve_own_r"), sem("act_exp")
        summed_shift, summed_all, mean_made, turned, mean_kept, logits = (
            sem(k) for k in ("summed_shift", "summed_all", "mean_made", "mean_turned", "mean_kept", "logits"))
        max_made, probs_ready, gap_made, chosen_made, experts_loaded = (
            sem(k) for k in ("max_made", "probs_ready", "gap_made", "chosen_made", "experts_loaded"))
        weights_made, weights_spread, b1_turned, b2_made, b2_spread = (
            sem(k) for k in ("weights_made", "weights_spread", "b1_turned", "b2_made", "b2_spread"))
        block = ctx.enter_context(nc.Block())
        below = sq[:, 2]

        @block.gpsimd
        def _(pool):
            nc.gpsimd.memset(below, 1.0).then_inc(below_made, 1)
            pool.wait_ge(below_made, 1)
            nc.gpsimd.affine_select(out=below, in_=below, compare_op=ALU.is_gt, fill=0.0, base=0,
                                    pattern=[[1, E], [-1, E]], channel_multiplier=0).then_inc(below_made, 1)

        @block.sync
        def _(sp):
            sp.dma_start(wr[:], d["Wr"]).then_inc(loaded, 16)
            sp.dma_start(br[:], d["br"].rearrange("(o e) -> o e", o=1)).then_inc(loaded, 16)
            sp.wait_ge(chosen_made, 1)
            for k in range(2):
                e = sp.value_load(chosen[0:1, k:k + 1], min_val=0, max_val=E - 1)
                at = bass.ds(e, 1)
                half = slice(k * FF // P, (k + 1) * FF // P)
                sp.dma_start(s["w1"][:, k * FF:(k + 1) * FF], d["W1e"][at].rearrange("o c f -> (o c) f")).then_inc(experts_loaded, 16)
                sp.dma_start(w2_raw[:, half, :], d["W2e"][at].rearrange("o (c p) d -> p (o c) d", p=P)).then_inc(experts_loaded, 16)
                sp.dma_start(b1_rows[half, :], d["b1e"][at].rearrange("o (c p) -> (o c) p", p=P)).then_inc(experts_loaded, 16)
                sp.dma_start(b2_raw[0:1, k, :], d["b2e"][at]).then_inc(experts_loaded, 16)
            sp.wait_ge(experts_loaded, 8 * 16)

        @block.tensor
        def _(pe):
            ones = s["ones"]
            psR = s["psR"][0:1, 0:CH]
            pe.wait_ge(summed_shift, 1)
            nc.tensor.matmul(psR, shift_sum[:], ones[:], start=False, stop=True).then_inc(summed_all, 1)
            pe.wait_ge(mean_made, 1)
            nc.tensor.matmul(ps[:, 0, 0:1], mean[:], ones[0:1, 0:1], start=True, stop=True).then_inc(turned, 1)
            pe.wait_ge(mean_kept, 1)
            pe.wait_ge(loaded, 32)
            nc.tensor.matmul(ps[0:1, 1, 0:E], mean_col[:], wr[:], start=True, stop=False)
            nc.tensor.matmul(ps[0:1, 1, 0:E], ones[0:1, 0:1], br[:], start=False, stop=True).then_inc(logits, 1)
            pe.wait_ge(weights_made, 1)
            nc.tensor.matmul(ps[:, 2, 0:2], ones[0:1, :], w_pair[:], start=True, stop=True).then_inc(weights_spread, 1)
            pe.wait_ge(experts_loaded, 8 * 16)
            nc.tensor.transpose(ps[:, 0, 0:NCHUNK], b1_rows[:], s["ident"][0:NCHUNK, 0:NCHUNK]).then_inc(b1_turned, 1)
            pe.wait_ge(b2_made, 1)
            nc.tensor.matmul(ps[:, 3, 0:CH], ones[0:1, :], b2_row[:], start=True, stop=True).then_inc(b2_spread, 1)

        @block.scalar
        def _(act):
            act.wait_ge(max_made, 1)
            nc.scalar.activation(vec[:, 0], ps[0:1, 1, 0:E], ACT.Exp, bias=scal[:, 0:1], accum_out=scal[:, 1:2]).then_inc(own_a, 1)
            act.wait_ge(probs_ready, 1)
            nc.scalar.activation(vec[:, 3], vec[:, 2], ACT.Exp, bias=scal[:, 3:4], accum_out=scal[:, 4:5]).then_inc(own_a, 1)
            act.wait_ge(gap_made, 1)
            nc.scalar.activation(scal[:, 6:7], scal[:, 5:6], ACT.Exp).then_inc(own_a, 1)

        @block.vector
        def _(dve):
            chain = Chain(dve, own)
            v = nc.vector
            L = chain.link
            v.reduce_sum(shift_sum[:], s["coef_2"][:, 1, :], AX.X).then_inc(summed_shift, 1)
            dve.wait_ge(summed_all, 1)
            v.tensor_scalar(mean[:], s["psR"][0:1, 0:CH], 1.0 / TOKENS, None, ALU.mult).then_inc(mean_made, 1)
            dve.wait_ge(turned, 1)
            v.tensor_copy(mean_col[:], ps[:, 0, 0:1]).then_inc(mean_kept, 1)
            dve.wait_ge(logits, 1)
            L(v.reduce_max(scal[:, 2:3], ps[0:1, 1, 0:E], AX.X))
            v.tensor_scalar(scal[:, 0:1], scal[:, 2:3], -1.0, None, ALU.mult).then_inc(max_made, 1)
            dve.wait_ge(own_a, 1)
            L(v.reciprocal(scal[:, 7:8], scal[:, 1:2]))
            L(v.tensor_scalar(vec[:, 1], vec[:, 0], scal[:, 7:8], None, ALU.mult))
            L(v.tensor_scalar(vec[:, 2], vec[:, 1], CAPACITY / TOKENS, None, ALU.min))
            L(v.reduce_max(scal[:, 2:3], vec[:, 2], AX.X))
            v.tensor_scalar(scal[:, 3:4], scal[:, 2:3], -1.0, None, ALU.mult).then_inc(probs_ready, 1)
            by_f = vec[:, 2].unsqueeze(1).broadcast_to([1, E, E])
            by_e = vec[:, 2].unsqueeze(2).broadcast_to([1, E, E])
            dve.wait_ge(below_made, 2)
            v.tensor_tensor(sq[:, 0], by_f, by_e, ALU.is_gt)
            L(v.tensor_tensor(sq[:, 1], by_f, by_e, ALU.is_equal))
            L(v.tensor_tensor(sq[:, 1], sq[:, 1], below, ALU.mult))
            L(v.tensor_tensor(sq[:, 0], sq[:, 0], sq[:, 1], ALU.add))
            v.reduce_sum(vec[:, 4], sq[:, 0], AX.X)
            L(v.reduce_sum(vec[:, 5], below, AX.X))
            for k in range(2):
                ins = v.tensor_scalar(pick[:, k], vec[:, 4], float(k), None, ALU.is_equal)
            L(ins)
            L(v.tensor_tensor(pick_v[:], pick[:], vec[:, 5].unsqueeze(1).broadcast_to([1, 2, E]), ALU.mult))
            L(v.reduce_sum(chosen_f[:], pick_v[:], AX.X))
            v.tensor_copy(chosen[:], chosen_f[:]).then_inc(chosen_made, 1)
            dve.wait_ge(own_a, 2)
            L(v.reciprocal(scal[:, 8:9], scal[:, 4:5]))
            L(v.tensor_scalar(vec[:, 6], vec[:, 3], scal[:, 8:9], None, ALU.mult))
            L(v.tensor_tensor(pick_v[:], pick[:], vec[:, 6].unsqueeze(1).broadcast_to([1, 2, E]), ALU.mult))
            L(v.reduce_sum(val[:], pick_v[:], AX.X))
            v.tensor_tensor(scal[:, 5:6], val[:, 1:2], val[:, 0:1], ALU.subtract).then_inc(gap_made, 1)
            dve.wait_ge(own_a, 3)
            L(v.tensor_scalar(scal[:, 9:10], scal[:, 6:7], 1.0, None, ALU.add))
            L(v.reciprocal(w_pair[:, 0:1], scal[:, 9:10]))
            v.tensor_tensor(w_pair[:, 1:2], scal[:, 6:7], w_pair[:, 0:1], ALU.mult).then_inc(weights_made, 1)
            dve.wait_ge(weights_spread, 1)
            L(v.tensor_copy(w_col[:], ps[:, 2, 0:2]))
            dve.wait_ge(experts_loaded, 8 * 16)
            L(v.tensor_scalar(b2_raw[:, 1, :], b2_raw[:, 1, :], w_col[0:1, 1:2], None, ALU.mult))
            v.scalar_tensor_tensor(b2_row[:], b2_raw[:, 0, :], w_col[0:1, 0:1], b2_raw[:, 1, :], ALU.mult, ALU.add).then_inc(b2_made, 1)
            for k in range(2):
                half = slice(k * FF // P, (k + 1) * FF // P)
                v.tensor_scalar(s["w2"][:, half, :], w2_raw[:, half, :], w_col[:, k:k + 1], None, ALU.mult)
            dve.wait_ge(b2_spread, 1)
            v.tensor_copy(s["b2"][:], ps[:, 3, 0:CH])
            dve.wait_ge(b1_turned, 1)
            v.tensor_copy(s["b1"][:], ps[:, 0, 0:NCHUNK])


GROUPS_D = TPB // 4


def ffn_phase(nc, d, s):
    with ExitStack() as ctx:
        sb = lambda name, shape, dt=F32: ctx.enter_context(nc.sbuf_tensor(name, shape, dt))
        sem = lambda name: ctx.enter_context(nc.semaphore(name))
        G4 = 4 * CH
        x2 = sb("x2_d", [P, TPB, CH])
        x2b, vv, o_buf = sb("x2_beta", [P, TPB, CH]), sb("ffn_sum", [P, TPB, CH]), sb("out_buf", [P, TPB, CH])
        xh, xb, u = sb("xh_d", [P, 2, 4, CH]), sb("xh_b2", [P, 2, 4, CH]), sb("u_d", [P, 2, 4, CH])
        xT, hT = sb("xT_d", [P, 2, G4]), sb("hT", [P, 2, NCHUNK, G4])
        stats, work, coef = sb("stats_d", [P, 4, 6]), sb("work_d", [P, 6, 4]), sb("coef_d", [P, 2, 2, 4])
        psT = ctx.enter_context(nc.psum_tensor("psT_d", [P, 2, 512], F32))
        psH = ctx.enter_context(nc.psum_tensor("psH_d", [P, NCHUNK, 512], F32))
        psY = ctx.enter_context(nc.psum_tensor("psY_d", [P, 2, 512], F32))
        loaded, stored = [[sem(f"{k}_{i}") for i in range(len(CHUNKS))] for k in ("loaded_d", "stored_out")]
        normed, turned, copied, raised, gelued, lowered = (sem(f"{k}_d") for k in ("normed", "turned", "copied", "raised", "gelued", "lowered"))
        xb_made, x2b_made, v_made, u_made, scaled, final = (
            sem(k) for k in ("xb_made", "x2b_made", "v_made", "u_made", "scaled", "final"))
        statted, stepped = sem("statted_d"), sem("coef_stepped_d")
        block = ctx.enter_context(nc.Block())
        NG = GROUPS_D

        def loops(eng, slot, tail=0):
            for n in range(2):
                for g in range(NG):
                    slot(n, g, False)
            with eng.Fori(2, NBLK - 1) as n:
                for g in range(NG):
                    slot(n, g, False)
            for g in range(NG):
                slot(NBLK - 1, g, True)
            for g in range(tail):
                slot(NBLK, g, True)

        def back(n, g, k):
            if g >= k:
                return (n, g - k) if not isinstance(n, int) or n < NBLK else None
            return None if isinstance(n, int) and n == 0 else (n - 1, g - k + NG)

        def following(n, g, last):
            if g + 1 < NG:
                return (n, g + 1) if not isinstance(n, int) or n < NBLK else None
            return None if last else (n + 1, 0)

        @block.sync
        def _(sp):
            def load(n, k):
                lo, hi = CHUNKS[k]
                sp.dma_start(x2[:, lo:hi, :].rearrange("p t c -> p (t c)"),
                             d["s_x2"][bass.ds(n, 1), :, lo * CH:hi * CH].rearrange("o p c -> (o p) c")).then_inc(loaded[k], 16)

            def store(m, k):
                lo, hi = CHUNKS[k]
                sp.wait_ge(final, NG * m + hi // 4)
                if hi <= LOW:
                    sp.dma_start(d["out"][bass.ds(BLOCK_A * m + lo, hi - lo), 0:P, :].rearrange("a b c -> b a c"),
                                 o_buf[:, lo:hi, :]).then_inc(stored[k], 16)
                else:
                    for h in range(2):
                        sp.dma_start(d["out"][bass.ds(BLOCK_A * m + HALF_A * h, HALF_A), P:N, :].rearrange("a b c -> b a c"),
                                     o_buf[64 * h:64 * h + 64, lo:hi, :]).then_inc(stored[k], 16)

            for k in range(len(CHUNKS)):
                load(0, k)

            def slot(n, g, last):
                if g % 2 == 0:
                    return
                if g > 1:
                    store(n, g // 2 - 1)
                elif not isinstance(n, int) or n > 0:
                    store(n - 1, len(CHUNKS) - 1)
                if not last:
                    sp.wait_ge(normed, NG * n + g + 1)
                    sp.wait_ge(x2b_made, NG * n + g + 1)
                    load(n + 1, g // 2)
            loops(sp, slot)
            store(NBLK - 1, len(CHUNKS) - 1)
            for k in range(len(CHUNKS)):
                sp.wait_ge(stored[k], 16 * CHUNK_DMAS[k] * NBLK)

        @block.scalar
        def _(act):
            def copy_turned(n, g):
                act.wait_ge(turned, NG * n + g + 1)
                need(act, raised, NCHUNK * (NG * n + g - 1))
                nc.scalar.copy(xT[:, g % 2, :], psT[:, g % 2, :]).then_inc(copied, 1)

            def slot(n, g, last):
                for f in range(NCHUNK):
                    act.wait_ge(raised, NCHUNK * (NG * n + g) + f + 1)
                    if f == 0:
                        need(act, lowered, NG * n + g - 1)
                    nc.scalar.activation(hT[:, g % 2, f, :], psH[:, f, :], ACT.Gelu, bias=s["b1"][:, f:f + 1]).then_inc(gelued, 1)
                nxt = following(n, g, last)
                if nxt:
                    copy_turned(*nxt)
            copy_turned(0, 0)
            loops(act, slot)

        @block.tensor
        def _(pe):
            def turn(n, g):
                pe.wait_ge(normed, NG * n + g + 1)
                need(pe, copied, NG * n + g - 1)
                for i in range(4):
                    ins = nc.tensor.transpose(psT[:, g % 2, i * P:i * P + P], xh[:, g % 2, i, :], s["ident"][:])
                ins.then_inc(turned, 1)

            def slot(n, g, last):
                pe.wait_ge(copied, NG * n + g + 1)
                for f in range(NCHUNK):
                    need(pe, gelued, NCHUNK * (NG * n + g - 1) + f + 1)
                    nc.tensor.matmul(psH[:, f, :], s["w1"][:, f * P:f * P + P], xT[:, g % 2, :], start=True, stop=True
                                     ).then_inc(raised, 1)
                nxt = following(n, g, last)
                if nxt:
                    turn(*nxt)
                pe.wait_ge(gelued, NCHUNK * (NG * n + g) + NCHUNK)
                need(pe, v_made, NG * n + g - 1)
                for i in range(4):
                    for f in range(NCHUNK):
                        ins = nc.tensor.matmul(psY[:, g % 2, i * CH:i * CH + CH], hT[:, g % 2, f, i * P:i * P + P],
                                               s["w2"][:, f, :], start=(f == 0), stop=(f == NCHUNK - 1))
                ins.then_inc(lowered, 1)
            turn(0, 0)
            loops(pe, slot)

        @block.gpsimd
        def _(pool):
            def spread(row):
                return row.unsqueeze(1).broadcast_to([P, 4, CH])

            def slot(n, g, last):
                if not (isinstance(n, int) and n == NBLK):
                    k = CHUNK_OF[4 * g]
                    pool.wait_ge(normed, NG * n + g + 1)
                    need(pool, v_made, NG * n + g - 1)
                    nc.gpsimd.tensor_tensor(xb[:, g % 2], xh[:, g % 2], spread(s["b2"][:]), ALU.add).then_inc(xb_made, 1)
                    if 4 * g == CHUNKS[k][0]:
                        pool.wait_ge(loaded[k], 16 * (n + 1))
                    need(pool, final, NG * (n - 1) + g + 1)
                    nc.gpsimd.tensor_tensor(x2b[:, 4 * g:4 * g + 4, :], x2[:, 4 * g:4 * g + 4, :], spread(s["beta"][:]),
                                            ALU.add).then_inc(x2b_made, 1)
                two = back(n, g, 2)
                if two:
                    m, h = two
                    pool.wait_ge(u_made, NG * m + h + 1)
                    nc.gpsimd.tensor_tensor(u[:, h % 2], u[:, h % 2], spread(s["gamma"][:]), ALU.mult).then_inc(scaled, 1)
            loops(pool, slot, 2)

        @block.vector
        def _(dve):
            v = nc.vector

            def norm(n, g, i):
                t = 4 * g + i
                if i == 0:
                    k = CHUNK_OF[t]
                    if t == CHUNKS[k][0]:
                        dve.wait_ge(loaded[k], 16 * (n + 1))
                    need(dve, turned, NG * n + g - 1)
                    need(dve, xb_made, NG * n + g - 1)
                r, b = (s["coef_2"][:, q, bass.ds(TPB * n + t, 1)] for q in range(2))
                ins = v.tensor_scalar(xh[:, g % 2, i, :], x2[:, t, :], r, b, ALU.mult, ALU.add)
                if i == 3:
                    ins.then_inc(normed, 1)

            def stats_of(n, g):
                dve.wait_ge(v_made, NG * n + g + 1)
                for i in range(4):
                    ins = v.bn_stats(stats[:, i, :], vv[:, 4 * g + i, :])
                ins.then_inc(statted, 1)

            def coef_step(n, g, step):
                before = LN_STEPS * (NG * n + g)
                if step == 0:
                    dve.wait_ge(statted, NG * n + g + 1)
                    need(dve, stepped, before)
                ln_step(nc, dve, step, stepped, before, stats, work, CH, 1.0, EPS5, coef[:, g % 2, 0, :], coef[:, g % 2, 1, :])

            def scale_v(n, g, i):
                if i == 0:
                    dve.wait_ge(stepped, LN_STEPS * (NG * n + g + 1))
                    need(dve, final, NG * n + g - 1)
                ins = v.tensor_scalar(u[:, g % 2, i, :], vv[:, 4 * g + i, :], coef[:, g % 2, 0, i:i + 1],
                                      coef[:, g % 2, 1, i:i + 1], ALU.mult, ALU.add)
                if i == 3:
                    ins.then_inc(u_made, 1)

            def finish(n, g):
                k = CHUNK_OF[4 * g]
                dve.wait_ge(scaled, NG * n + g + 1)
                if 4 * g == CHUNKS[k][0]:
                    need(dve, stored[k], 16 * CHUNK_DMAS[k] * n)
                tiles = slice(4 * g, 4 * g + 4)
                v.tensor_tensor(o_buf[:, tiles, :], u[:, g % 2], x2b[:, tiles, :], ALU.add).then_inc(final, 1)

            def slot(n, g, last):
                one, two, nxt = back(n, g, 1), back(n, g, 2), following(n, g, last)
                if one:
                    stats_of(*one)
                for step in range(LN_STEPS):
                    if one:
                        coef_step(*one, step)
                    if step < 4 and nxt:
                        norm(*nxt, step)
                    if 4 <= step < 8 and two:
                        scale_v(*two, step - 4)
                    if step == 14 and two:
                        finish(*two)
                if not (isinstance(n, int) and n == NBLK):
                    dve.wait_ge(lowered, NG * n + g + 1)
                    dve.wait_ge(xb_made, NG * n + g + 1)
                    v.tensor_tensor(vv[:, 4 * g:4 * g + 4, :], psY[:, g % 2, :].rearrange("p (t c) -> p t c", t=4), xb[:, g % 2],
                                    ALU.add).then_inc(v_made, 1)

            for i in range(4):
                norm(0, 0, i)
            loops(dve, slot, 2)


def metaformer_kernel(nc, x, l_pair, protein_pair, inter_pair, z_mask, ln_g, ln_b, lnc_g, lnc_b, Wg1, bg1, Wg2, bg2,
                      Wg3, bg3, W1, b1, W2, b2, W3, b3, Wend, bend, Wsum, bsum, Wr, br, W1e, b1e, W2e, b2e, gamma, beta, out):
    grid = lambda ap: ap.rearrange("o a b c -> (o a) b c")
    d = dict(x=grid(x), lp=grid(l_pair), pp=grid(protein_pair), ip=grid(inter_pair), zm=z_mask.rearrange("o a b -> (o a) b"),
             ln_g=ln_g, ln_b=ln_b, lnc_g=lnc_g, lnc_b=lnc_b, Wg1=Wg1, bg1=bg1, Wg2=Wg2, bg2=bg2, Wg3=Wg3, bg3=bg3,
             W1=W1, b1=b1, W2=W2, b2=b2, W3=W3, b3=b3, Wend=Wend, bend=bend, Wsum=Wsum, bsum=bsum,
             Wr=Wr, br=br, W1e=W1e, b1e=b1e, W2e=W2e, b2e=b2e, gamma=gamma, beta=beta, out=grid(out))
    scratch = lambda name, shape: nc.dram_tensor(name, shape, F32, kind="Internal").ap()
    d["s_ab"] = scratch("scratch_ab", (N, 2 * NCG, N * CC))
    d["s_pp"] = scratch("scratch_pp", (N, NCG, N * CC))
    d["s_lp"] = scratch("scratch_lp", (N, NCG, N * CC))
    d["s_q"] = scratch("scratch_q", (NBLK, P, TPB * HID))
    d["s_x2"] = scratch("scratch_x2", (NBLK, P, TPB * CH))
    with ExitStack() as ctx:
        s = {}
        for name, shape in (("ident", [P, P]), ("ones", [P, P]), ("w_all", [P, 6 * HID + CH]), ("ws2", [P, 2 * CH]),
                            ("mask", [P, NBLK * TPB]), ("coef_x", [P, 2, NBLK * TPB]), ("coef_2", [P, 2, NBLK * TPB]),
                            ("w1", [P, 2 * FF]), ("w2", [P, NCHUNK, CH]), ("b1", [P, NCHUNK]), ("b2", [P, CH]),
                            ("gamma", [P, CH]), ("beta", [P, CH])):
            s[name] = ctx.enter_context(nc.sbuf_tensor(name, shape, F32))
        setup_phase(nc, d, s)
        project_phase(nc, d, s)
        with nc.sbuf_tensor("tri", [P, NBLK * TPB, HID], F32) as tri:
            s["tri"] = tri
            triangle_phase(nc, d, s)
            with nc.psum_tensor("psR", [P, 512], F32) as psR:
                s["psR"] = psR
                mix_phase(nc, d, s)
                route_phase(nc, d, s)
        ffn_phase(nc, d, s)


_CONV = ['l_pair', 'protein_pair', 'inter_pair', 'z_mask', 'ln_g', 'ln_b', 'lnc_g', 'lnc_b', 'Wg1', 'bg1', 'Wg2', 'bg2',
         'Wg3', 'bg3', 'W1', 'b1', 'W2', 'b2', 'W3', 'b3', 'Wend', 'bend', 'Wsum', 'bsum']
_FFN = ['Wr', 'br', 'W1', 'b1', 'W2', 'b2', 'gamma', 'beta']
_INS = ['x'] + ['L0_conv_' + n for n in _CONV] + ['L0_ffn_' + n for n in _FFN]


def kernel(**inputs):
    import numpy as _np
    import concourse.bacc as _bacc
    from concourse import mybir as _mybir
    from concourse.bass_utils import run_bass_kernel_spmd as _run

    nc = _bacc.Bacc("TRN2", target_bir_lowering=False, num_devices=1)
    arrays, args = {}, []
    for name in _INS:
        a = _np.ascontiguousarray(inputs[name])
        arrays[f"in_{name}_dram"] = a
        args.append(nc.dram_tensor(f"in_{name}_dram", a.shape, _mybir.dt.from_np(a.dtype), kind="ExternalInput").ap())
    out = nc.dram_tensor("out_0_dram", (1, N, N, CH), F32, kind="ExternalOutput").ap()
    metaformer_kernel(nc, *args, out)
    r = _run(nc, [arrays], core_ids=[0])
    return r.results[0]["out_0_dram"]
```

```python
from contextlib import ExitStack

import concourse.bass as bass
from concourse import mybir

F32 = mybir.dt.float32
F32R = mybir.dt.float32r
I32 = mybir.dt.int32
ALU = mybir.AluOpType
ACT = mybir.ActivationFunctionType
AX = mybir.AxisListType

P = 128
N = 192
CH = 128
HID = 64
BLOCK_A = 16
HALF_A = BLOCK_A // 2
NBLK = N // BLOCK_A
LOW = BLOCK_A
HIGH = HALF_A
TPB = LOW + HIGH
NB_HIGH = N - P
CC = 8
NCG = HID // CC
TOKENS = N * N
EXPERTS = 8
FF = 256
NCHUNK = 2 * FF // P
CAPACITY = -(-TOKENS * 5 // (4 * EXPERTS))
EPS5 = 1e-5
EPS6 = 1e-6
RSQRT_MAGIC = 0x5F3759DF
CHUNKS = ((0, 8), (8, 16), (16, 24))


def need(eng, sem, value):
    if isinstance(value, int) and value <= 0:
        return
    eng.wait_ge(sem, value)


LOAD_COUNT = 16 * (2 + 2)


class Chain:

    def __init__(self, eng, sem):
        self.eng, self.sem, self.count = eng, sem, 0

    def link(self, ins):
        self.count += 1
        ins.then_inc(self.sem, 1)
        self.eng.wait_ge(self.sem, self.count)


def load_tiles(eng, dst, src, n, sem, tiles=(0, TPB)):
    lo, hi = tiles
    for t in range(lo, min(hi, LOW), HALF_A):
        eng.dma_start(dst[:, t:t + HALF_A, :],
                      src[bass.ds(BLOCK_A * n + t, HALF_A), 0:P, :].rearrange("a b c -> b a c")).then_inc(sem, 16)
    if hi > LOW:
        for h in range(2):
            eng.dma_start(dst[64 * h:64 * h + 64, LOW:TPB, :],
                          src[bass.ds(BLOCK_A * n + HALF_A * h, HALF_A), P:N, :].rearrange("a b c -> b a c")
                          ).then_inc(sem, 16)


def wait_by_event(pool, sem, value, passed):
    pool.wait_ge(sem, value)
    pool.sem_inc(passed, 1)


LN_STEPS = 17


def ln_step(nc, dve, step, stepped, before, stats, work, channels, mulv, addv, rstd, shift, plus=0.0):
    v = nc.vector
    mean2, m2, diff, sq, var, t = (work[:, k, :] for k in range(6))
    y = rstd
    if step > 0:
        dve.wait_ge(stepped, before + step)
    if step == 0:
        ins = v.tensor_tensor(work[:, 0:2, :].rearrange("p k w -> p w k"), stats[:, :, 1:3], stats[:, :, 4:6], ALU.add)
    elif step == 1:
        ins = v.tensor_tensor(diff, stats[:, :, 1], stats[:, :, 4], ALU.subtract)
    elif step == 2:
        ins = v.scalar_tensor_tensor(sq, diff, 0.25 * mulv, diff, ALU.mult, ALU.mult)
    elif step == 3:
        ins = v.scalar_tensor_tensor(var, m2, mulv / channels, sq, ALU.mult, ALU.add)
    elif step == 4:
        ins = v.tensor_scalar(var, var, addv, None, ALU.add)
    elif step == 5:
        ins = v.tensor_scalar(t.bitcast(I32), var.bitcast(I32), 1, None, ALU.arith_shift_right)
    elif step == 6:
        ins = v.tensor_scalar(y.bitcast(I32), t.bitcast(I32), -1.0, float(RSQRT_MAGIC), ALU.mult, ALU.add)
    elif step < 16:
        if step % 3 == 1:
            ins = v.tensor_tensor(t, y, y, ALU.mult)
        elif step % 3 == 2:
            ins = v.scalar_tensor_tensor(t, t, -0.5, var, ALU.mult, ALU.mult)
        else:
            ins = v.scalar_tensor_tensor(y, t, 1.5, y, ALU.add, ALU.mult)
    else:
        ins = v.scalar_tensor_tensor(shift, mean2, -0.5, y, ALU.mult, ALU.mult)
    ins.then_inc(stepped, 1)


def setup_parts(nc, d, s, ctx, ps):
    sb = lambda name, shape, dt=F32: ctx.enter_context(nc.sbuf_tensor(name, shape, dt))
    sem = lambda name: ctx.enter_context(nc.semaphore(name))
    zm_low = sb("zm_low", [P, N])
    zm_high = sb("zm_high", [64, N])
    ln_g, ln_b = sb("ln_g_col", [P, 1]), sb("ln_b_col", [P, 1])
    lnc_g, lnc_b = sb("lnc_g_col", [P, 1]), sb("lnc_b_col", [P, 1])
    fold = sb("fold", [P, P])
    foldc = sb("foldc", [HID, P])
    zeros = sb("zeros", [P, P])
    w_raw = sb("w_raw", [P, 512])
    ws_raw = sb("ws_raw", [P, CH])
    bias_row = sb("bias_row", [1, 640])
    loaded, ident_made, const_made = sem("setup_loaded"), sem("ident_made"), sem("const_made")
    folds_made, folded, zm_turned, own = sem("folds_made"), sem("folded"), sem("zm_turned"), sem("setup_own")
    more_loaded, mask_made = sem("setup_more_loaded"), sem("mask_made")
    gate_order = ((0, "W1", "b1"), (64, "W2", "b2"), (128, "W3", "b3"),
                  (192, "Wg1", "bg1"), (256, "Wg2", "bg2"), (320, "Wg3", "bg3"))

    row = lambda ap: ap.rearrange("(o c) -> o c", o=1)
    col = lambda ap: ap.rearrange("(c o) -> c o", o=1)
    loads = [(ln_g[:], col(d["ln_g"])), (ln_b[:], col(d["ln_b"])),
             (w_raw[:, 384:512], d["Wend"]), (bias_row[:, 384:512], row(d["bend"])),
             (bias_row[:, 512:640], row(d["bsum"]))]
    for off, w, b in gate_order:
        loads += [(w_raw[:, off:off + HID], d[w]), (bias_row[:, off:off + HID], row(d[b]))]
    more_loads = [(zm_low[:], d["zm"][0:P, :]), (zm_high[:], d["zm"][P:N, :])]
    for h in range(2):
        half = slice(HID * h, HID * h + HID)
        more_loads += [(lnc_g[half, :], col(d["lnc_g"])), (lnc_b[half, :], col(d["lnc_b"])), (ws_raw[half, :], d["Wsum"])]
    n_loads = len(loads)

    def sync(sp):
        for dst, src in loads[0::2]:
            sp.dma_start(dst, src).then_inc(loaded, 16)

    def scalar(act):
        for dst, src in loads[1::2]:
            act.dma_start(dst, src).then_inc(loaded, 16)

    def gpsimd(pool):
        for dst, src in more_loads:
            pool.dma_start(dst, src).then_inc(more_loaded, 16)
        nc.gpsimd.memset(s["ident"][:], 0.0).then_inc(ident_made, 1)
        pool.wait_ge(ident_made, 1)
        nc.gpsimd.affine_select(out=s["ident"][:], in_=s["ident"][:], compare_op=ALU.not_equal, fill=1.0,
                                base=0, pattern=[[-1, P]], channel_multiplier=1).then_inc(ident_made, 1)
        nc.gpsimd.memset(s["ones"][:], 1.0).then_inc(const_made, 1)
        nc.gpsimd.memset(zeros[:], 0.0).then_inc(const_made, 1)
        nc.gpsimd.memset(s["ws2"][:], 0.0).then_inc(const_made, 1)

    def vector_first(dve):
        dve.wait_ge(const_made, 3)
        dve.wait_ge(loaded, 16 * n_loads)
        dve.wait_ge(more_loaded, 16 * len(more_loads))
        chain = Chain(dve, own)
        v = nc.vector
        chain.link(v.tensor_tensor(ln_b[:], ln_b[:], ln_g[:], ALU.subtract))
        chain.link(v.tensor_tensor(lnc_b[:], lnc_b[:], lnc_g[:], ALU.subtract))
        v.tensor_scalar(fold[:], zeros[:], ln_b[:, 0:1], 1.0 / CH, ALU.add, ALU.mult).then_inc(folds_made, 1)
        v.tensor_scalar(foldc[:], zeros[0:HID, :], lnc_b[0:HID, 0:1], 1.0 / HID, ALU.add, ALU.mult).then_inc(folds_made, 1)
        chain.link(v.tensor_scalar(bias_row[:, 0:512], bias_row[:, 0:512], 1.0 / CH, None, ALU.mult))
        v.tensor_scalar(bias_row[:, 512:640], bias_row[:, 512:640], 1.0 / HID, None, ALU.mult).then_inc(folds_made, 1)

    def vector(dve):
        v = nc.vector
        dve.wait_ge(folded, 1)
        v.scalar_tensor_tensor(s["w_all"][:], w_raw[:], ln_g[:, 0:1], ps[:, 0, :], ALU.mult, ALU.add)
        dve.wait_ge(folded, 2)
        for h in range(2):
            half = slice(HID * h, HID * h + HID)
            v.scalar_tensor_tensor(s["ws2"][half, CH * h:CH * h + CH], ws_raw[half, :], lnc_g[half, 0:1],
                                   ps[half, 1, 0:CH], ALU.mult, ALU.add)
        dve.wait_ge(zm_turned, 3)
        zt = s["mask"][:].rearrange("p (n u) -> p n u", u=TPB)
        v.tensor_copy(zt[:, :, 0:LOW], ps[:, 2, 0:N].rearrange("p (n u) -> p n u", u=BLOCK_A))
        for h in range(2):
            src = ps[64 * h:64 * h + 64, 3 + h, 0:N].rearrange("p (n u) -> p n u", u=BLOCK_A)
            ins = v.tensor_copy(zt[64 * h:64 * h + 64, :, LOW:TPB], src[:, :, HALF_A * h:HALF_A * h + HALF_A])
        ins.then_inc(mask_made, 1)

    def tensor(pe):
        pe.wait_ge(ident_made, 2)
        pe.wait_ge(loaded, 16 * n_loads)
        pe.wait_ge(more_loaded, 16 * len(more_loads))
        ident = s["ident"]
        for bank, cols in ((2, slice(0, P)), (3, slice(P, N)), (4, slice(64, N))):
            m = cols.stop - cols.start
            nc.tensor.transpose(ps[0:m, bank, 0:P], zm_low[:, cols], ident[:])
            nc.tensor.transpose(ps[0:m, bank, P:N], zm_high[:, cols], ident[0:64, 0:64]).then_inc(zm_turned, 1)
        pe.wait_ge(folds_made, 3)
        nc.tensor.matmul(ps[:, 0, :], fold[:], w_raw[:], start=True, stop=False)
        nc.tensor.matmul(ps[:, 0, :], s["ones"][0:1, :], bias_row[:, 0:512], start=False, stop=True).then_inc(folded, 1)
        nc.tensor.matmul(ps[:, 1, 0:CH], foldc[:], ws_raw[0:HID, :], start=True, stop=False)
        nc.tensor.matmul(ps[:, 1, 0:CH], s["ones"][0:1, :], bias_row[:, 512:640], start=False, stop=True).then_inc(folded, 1)

    return sync, scalar, gpsimd, vector_first, vector, tensor, mask_made


PASSES = (("x", 3, 2), ("pp", 1, 4), ("lp", 1, 4), ("ip", 1, 4))
GROUPS_A = []
for _s, (_name, _k, _size) in enumerate(PASSES):
    for _g in range(TPB // _size):
        GROUPS_A.append((_s, _g, _g * _size, _size))
NG_A = len(GROUPS_A)
PASS_END = [max(i for i, g in enumerate(GROUPS_A) if g[0] == s_) + 1 for s_ in range(len(PASSES))]


STATS_A = [[] for _ in range(NG_A)]
COEFS_A = [[] for _ in range(NG_A)]


def share_out(table, first, per, i, ahead, items):
    for k, item in enumerate(items):
        table[first + k // per].append((i, ahead, item))


QG = TPB // 4
AT_X, AT_PP, AT_LP, AT_IP = 0, PASS_END[0], PASS_END[1], PASS_END[2]
share_out(STATS_A, AT_X, 3, 2, 0, range(TPB))
share_out(STATS_A, AT_X + 8, 3, 3, 0, range(12))
share_out(STATS_A, AT_PP, 4, 3, 0, range(12, TPB))
share_out(STATS_A, AT_PP + 3, 2, 0, 1, range(6))
share_out(STATS_A, AT_LP, 5, 0, 1, range(6, TPB))
share_out(STATS_A, AT_IP, 4, 1, 1, range(TPB))
share_out(COEFS_A, AT_X, 4, 1, 0, range(LN_STEPS + 2))
share_out(COEFS_A, AT_X + 8, 4, 2, 0, range(LN_STEPS + 2))
share_out(COEFS_A, AT_PP + 3, 7, 3, 0, range(LN_STEPS + 2))
share_out(COEFS_A, AT_LP + 4, 7, 0, 1, range(LN_STEPS + 2))


OPERANDS = ("pp_low", "ab1_low", "ab1_high", "ab2_low", "lp_low", "mov_high", "sta_high")


def group_loads(bufs, d, g, a_lo, a_hi):
    cols = slice(CC * a_lo, CC * a_hi)
    view = lambda name, lo, hi, g: d[name][lo:hi, bass.ds(g, 1), cols].rearrange("b o c -> b (o c)")
    to = lambda name, rows=slice(0, P): bufs[name][rows].rearrange("p a c -> p (a c)")[:, cols]
    return [(to("pp_low"), view("s_pp", 0, P, g)), (to("ab1_low"), view("s_ab", 0, P, g)),
            (to("ab1_high", slice(0, 64)), view("s_ab", P, N, g)), (to("ab2_low"), view("s_ab", 0, P, g + NCG)),
            (to("lp_low"), view("s_lp", 0, P, g)), (to("mov_high", slice(0, 64)), view("s_pp", P, N, g)),
            (to("mov_high", slice(64, P)), view("s_ab", P, N, g + NCG)), (to("sta_high", slice(64, P)), view("s_lp", P, N, g))]


N_LOADS = 8


def project_phase(nc, d, s):
    with ExitStack() as ctx:
        sb = lambda name, shape, dt=F32: ctx.enter_context(nc.sbuf_tensor(name, shape, dt))
        sem = lambda name: ctx.enter_context(nc.semaphore(name))
        tiles_in = [sb(f"in_{name}", [P, TPB, CH]) for name, _, _ in PASSES]
        stats = [sb(f"stats_a{i}", [P, TPB, 6]) for i in range(len(PASSES))]
        work = sb("work_a", [P, 6, TPB])
        coef = [sb(f"coef_a{i}", [P, 2, TPB]) for i in range(len(PASSES))]
        coef_spare = sb("coef_spare", [P, 2, TPB])
        xT = sb("xT_a", [P, 2, 4 * P])
        sig = sb("sig_a", [P, 2, 2 * 3 * HID])
        ab3 = sb("ab3_a", [P, TPB, HID])
        ip_prod = sb("ip_prod", [P, 4, 4 * HID])
        q_out = sb("q_out", [P, TPB, HID])
        low_out = [sb("low_ab", [P, 2 * NCG, LOW, CC]), sb("low_pp", [P, NCG, LOW, CC]), sb("low_lp", [P, NCG, LOW, CC])]
        high_out = [sb("high_ab", [P, 2 * NCG, HIGH, CC]), sb("high_pp", [P, NCG, HIGH, CC]), sb("high_lp", [P, NCG, HIGH, CC])]
        psT = ctx.enter_context(nc.psum_tensor("psT_a", [P, 2, 512], F32))
        psZ = ctx.enter_context(nc.psum_tensor("psZ_a", [P, 3, 2, 512], F32))
        loaded = [sem(f"loaded_{name}") for name, _, _ in PASSES]
        statted, coefs_ready, own, pool_passed = sem("statted"), sem("coefs_ready"), sem("coef_stepped_a"), sem("pool_passed_a")
        q_made = sem("q_made")
        normed_act, normed_pool = sem("normed_act"), sem("normed_pool")
        turned, copied, projected = sem("turned"), sem("copied"), sem("projected")
        gated, masked, multiplied = sem("gated"), sem("masked"), sem("multiplied")
        stored = [sem("stored_ab"), sem("stored_pp"), sem("stored_lp"), s["stored_q"]]
        setup = setup_parts(nc, d, s, ctx, psZ[:].rearrange("p a b c -> p (a b) c"))
        setup_sync, setup_scalar, setup_gpsimd, setup_vector_first, setup_vector, setup_tensor, mask_made = setup
        block = ctx.enter_context(nc.Block())
        srcs = [d[name] for name, _, _ in PASSES]

        def ahead(G, step, last):
            if G + step < NG_A:
                return G + step, GROUPS_A[G + step]
            return None if last else (G + step, GROUPS_A[G + step - NG_A])

        def act_share(i, t0):
            return 2 if (i == 1 and t0 < 12) or (i == 3 and t0 == TPB - 4) else 1

        def act_tiles(i, t0, size):
            return list(range(t0, t0 + act_share(i, t0)))

        def pool_tiles(i, t0, size):
            return list(range(t0 + act_share(i, t0), t0 + size))

        def loops(eng, body):
            body(0, False)
            with eng.Fori(1, NBLK - 1) as n:
                body(n, False)
            body(NBLK - 1, True)

        @block.sync
        def _(sp):
            def load_operands(a_lo, a_hi, blocks):
                for i in range(3):
                    sp.wait_ge(stored[i], 48 * blocks)
                for dst, src in group_loads(s["operands"], d, 0, a_lo, a_hi):
                    sp.dma_start(dst, src).then_inc(s["operands_loaded"][0], 16)

            load_tiles(sp, tiles_in[0], srcs[0], 0, loaded[0])
            setup_sync(sp)
            for i in range(1, len(PASSES)):
                load_tiles(sp, tiles_in[i], srcs[i], 0, loaded[i])

            def body(n, last):
                for i in range(len(PASSES)):
                    if not last:
                        sp.wait_ge(turned, NG_A * n + PASS_END[i])
                        load_tiles(sp, tiles_in[i], srcs[i], n + 1, loaded[i])
                    if i < 3:
                        sp.wait_ge(multiplied, NG_A * n + PASS_END[i])
                        dst = (d["s_ab"], d["s_pp"], d["s_lp"])[i]
                        sp.dma_start(dst[0:P, :, bass.ds(CC * BLOCK_A * n, CC * BLOCK_A)],
                                     low_out[i][:].rearrange("p g a c -> p g (a c)")).then_inc(stored[i], 16)
                        for h in range(2):
                            sp.dma_start(dst[P:N, :, bass.ds(CC * BLOCK_A * n + CC * HALF_A * h, CC * HALF_A)],
                                         high_out[i][64 * h:64 * h + 64].rearrange("p g a c -> p g (a c)")
                                         ).then_inc(stored[i], 16)
                    else:
                        if last:
                            load_operands(N - BLOCK_A, N, NBLK)
                        sp.wait_ge(q_made, QG * (n + 1))
                        sp.dma_start(d["s_q"][bass.ds(n, 1)].rearrange("o p c -> (o p) c"),
                                     q_out[:].rearrange("p t c -> p (t c)")).then_inc(stored[3], 16)
            body(0, False)
            with sp.Fori(1, NBLK - 1) as n:
                body(n, False)
            load_operands(0, N - BLOCK_A, NBLK - 1)
            body(NBLK - 1, True)

        def norm(wait, engine_op, sem_out, n, G, which, last):
            if ahead(G, 3, last) is None:
                return
            count, (i, g, t0, size) = ahead(G, 3, last)
            if g == 0:
                wait(coefs_ready, len(PASSES) * (n + count // NG_A) + i + 1)
            for t in which(i, t0, size):
                ins = engine_op(tiles_in[i][:, t, :], coef[i][:, 0, t:t + 1], coef[i][:, 1, t:t + 1])
            ins.then_inc(sem_out, 1)

        @block.scalar
        def _(act):
            def op(x, r, b):
                return nc.scalar.activation(x, x, ACT.Identity, bias=b, scale=r)

            def copy_turned(n, count, grp):
                i, g, t0, size = grp
                act.wait_ge(turned, NG_A * n + count + 1)
                need(act, projected, NG_A * n + count - 1)
                nc.scalar.copy(xT[:, count % 2, 0:size * P], psT[:, count % 2, 0:size * P]).then_inc(copied, 1)

            def body(n, last):
                for G, (i, g, t0, size) in enumerate(GROUPS_A):
                    norm(act.wait_ge, op, normed_act, n, G, act_tiles, last)
                    nxt = ahead(G, 1, last)
                    if nxt:
                        copy_turned(n, *nxt)
                    k = PASSES[i][1]
                    act.wait_ge(projected, NG_A * n + G + 1)
                    if i == 0:
                        z = psZ[:, G % 3, :, 3 * HID:6 * HID]
                    else:
                        z = psZ[:, G % 3, 0, :].rearrange("p (t c) -> p t c", t=size)[:, :, HID:2 * HID]
                    need(act, multiplied, NG_A * n + G - 1)
                    nc.scalar.activation(sig[:, G % 2, 0:size * k * HID].rearrange("p (t c) -> p t c", t=size),
                                         z, ACT.Sigmoid).then_inc(gated, 1)

            setup_scalar(act)
            for G in (-3, -2, -1):
                norm(act.wait_ge, op, normed_act, 0, G, act_tiles, False)
            copy_turned(0, 0, GROUPS_A[0])
            loops(act, body)

        @block.gpsimd
        def _(pool):
            def op(x, r, b):
                return nc.gpsimd.tensor_scalar(x, x, r, b, ALU.mult, ALU.add)

            def wait(sem, value):
                wait_by_event(pool, sem, value, pool_passed)

            def times_ab3(n, g):
                if g == 0:
                    need(pool, stored[3], 16 * n)
                pool.wait_ge(multiplied, NG_A * n + AT_IP + g + 1)
                tiles = slice(4 * g, 4 * g + 4)
                nc.gpsimd.tensor_tensor(q_out[:, tiles, :], ip_prod[:, g % 4, :].rearrange("p (t c) -> p t c", t=4),
                                        ab3[:, tiles, :], ALU.mult).then_inc(q_made, 1)

            def body(n, last):
                for G, (i, g, t0, size) in enumerate(GROUPS_A):
                    norm(wait, op, normed_pool, n, G, pool_tiles, last)
                    if i == 0:
                        pool.wait_ge(gated, NG_A * n + G + 1)
                        gates = sig[:, G % 2, 0:size * 3 * HID].rearrange("p (t c) -> p t c", t=size)
                        zm = s["mask"][:, bass.ds(TPB * n + t0, size)].unsqueeze(2).broadcast_to([P, size, 3 * HID])
                        nc.gpsimd.tensor_tensor(gates, gates, zm, ALU.mult).then_inc(masked, 1)
                    if i == 3 and g >= 2:
                        times_ab3(n, g - 2)
                    if i == 0 and g < 2 and not (isinstance(n, int) and n == 0):
                        times_ab3(n - 1, g + QG - 2)

            setup_gpsimd(pool)
            for G in (-3, -2, -1):
                norm(wait, op, normed_pool, 0, G, pool_tiles, False)
            pool.wait_ge(mask_made, 1)
            loops(pool, body)
            for g in (QG - 2, QG - 1):
                times_ab3(NBLK - 1, g)

        @block.tensor
        def _(pe):
            setup_tensor(pe)
            w = s["w_all"]
            pair1 = w[:, 0:6 * HID].rearrange("p (q k c) -> p q k c", q=2, k=3)
            rhs = [w[:, 0:6 * HID], pair1[:, :, 1, :], pair1[:, :, 0, :], pair1[:, :, 0, :]]

            def turn(n, count, grp):
                i, g, t0, size = grp
                pe.wait_ge(normed_act, NG_A * n + count + 1)
                pe.wait_ge(normed_pool, NG_A * n + count + 1)
                need(pe, copied, NG_A * n + count - 1)
                for j in range(size):
                    ins = nc.tensor.transpose(psT[:, count % 2, j * P:j * P + P], tiles_in[i][:, t0 + j, :], s["ident"][:])
                ins.then_inc(turned, 1)

            def body(n, last):
                for G, (i, g, t0, size) in enumerate(GROUPS_A):
                    nxt = ahead(G, 1, last)
                    if nxt:
                        turn(n, *nxt)
                    pe.wait_ge(copied, NG_A * n + G + 1)
                    need(pe, multiplied, NG_A * n + G - 2)
                    for j in range(size):
                        out = psZ[:, G % 3, j, 0:6 * HID] if i == 0 else psZ[:, G % 3, 0, j * P:j * P + P]
                        ins = nc.tensor.matmul(out, xT[:, G % 2, j * P:j * P + P], rhs[i], start=True, stop=True)
                    ins.then_inc(projected, 1)

            turn(0, 0, GROUPS_A[0])
            pe.wait_ge(mask_made, 1)
            loops(pe, body)

        @block.vector
        def _(dve):
            v = nc.vector
            NP = len(PASSES)
            steps = LN_STEPS + 1

            def stats_of(n, i, tiles):
                if tiles[0] == 0:
                    dve.wait_ge(loaded[i], LOAD_COUNT * (n + 1))
                for t in tiles:
                    ins = v.bn_stats(stats[i][:, t, :], tiles_in[i][:, t, :])
                if tiles[-1] == TPB - 1:
                    ins.then_inc(statted, 1)

            def coef_step(n, i, step):
                before = steps * (NP * n + i)
                mulv, addv = (1.0 + EPS5, EPS5 * EPS6) if i == 0 else (1.0, EPS5)
                if step == 0:
                    dve.wait_ge(statted, NP * n + i + 1)
                    if i == 0:
                        need(dve, turned, NG_A * (n - 1) + PASS_END[0])
                if step < LN_STEPS:
                    ln_step(nc, dve, step, own, before, stats[i], work, CH, mulv, addv, coef[i][:, 0, :], coef[i][:, 1, :])
                elif step == LN_STEPS:
                    dve.wait_ge(own, before + LN_STEPS)
                    v.tensor_scalar(coef[i][:, 1, :], coef[i][:, 1, :], 1.0, None, ALU.add).then_inc(own, 1)
                else:
                    dve.wait_ge(own, before + steps)
                    v.tensor_copy(s["coef_x"][:, :, bass.ds(TPB * n, TPB)] if i == 0 else coef_spare[:],
                                  coef[i][:]).then_inc(coefs_ready, 1)

            def body(n, last):
                for G, (i, g, t0, size) in enumerate(GROUPS_A):
                    coefs, tiles = COEFS_A[G], STATS_A[G]
                    for k in range(max(len(coefs), len(tiles))):
                        if k < len(coefs) and not (last and coefs[k][1]):
                            coef_step(n + coefs[k][1], coefs[k][0], coefs[k][2])
                        if k < len(tiles) and not (last and tiles[k][1]):
                            stats_of(n + tiles[k][1], tiles[k][0], [tiles[k][2]])
                    if i == 0:
                        dve.wait_ge(masked, (TPB // 2) * n + g + 1)
                    else:
                        dve.wait_ge(gated, NG_A * n + G + 1)
                    if g == 0 and i < 3:
                        need(dve, stored[i], 48 * n)
                    if i == 0 and g % 2 == 0:
                        need(dve, q_made, QG * (n - 1) + g // 2 + 1)
                    if i == 3:
                        need(dve, q_made, QG * n + g - 3)
                    if i < 3:
                        out = low_out[i][:, :, t0:t0 + size, :] if t0 < LOW else high_out[i][:, :, t0 - LOW:t0 - LOW + size, :]
                        out = out.rearrange("p g a c -> p a g c")
                    gate = sig[:, G % 2, :]
                    if i == 0:
                        z = psZ[:, G % 3, :, :]
                        gate = gate.rearrange("p (t c) -> p t c", t=size)
                        v.tensor_tensor(out, z[:, :, 0:2 * HID].rearrange("p t (g c) -> p t g c", c=CC),
                                        gate[:, :, 0:2 * HID].rearrange("p t (g c) -> p t g c", c=CC), ALU.mult)
                        v.tensor_tensor(ab3[:, t0:t0 + size, :], z[:, :, 2 * HID:3 * HID], gate[:, :, 2 * HID:3 * HID],
                                        ALU.mult).then_inc(multiplied, 1)
                    else:
                        z = psZ[:, G % 3, 0, :].rearrange("p (t c) -> p t c", t=size)[:, :, 0:HID]
                        gate = gate[:, 0:size * HID].rearrange("p (t c) -> p t c", t=size)
                        if i < 3:
                            v.tensor_tensor(out, z.rearrange("p t (g c) -> p t g c", c=CC),
                                            gate.rearrange("p t (g c) -> p t g c", c=CC), ALU.mult).then_inc(multiplied, 1)
                        else:
                            prod = ip_prod[:, g % 4, :].rearrange("p (t c) -> p t c", t=size)
                            v.tensor_tensor(prod, z, gate, ALU.mult).then_inc(multiplied, 1)

            stats_of(0, 0, list(range(TPB)))
            setup_vector_first(dve)
            for k in range(steps + 1):
                coef_step(0, 0, k)
            setup_vector(dve)
            stats_of(0, 1, list(range(TPB)))
            loops(dve, body)


def mix_buffers(s):
    shared = s["shared"][:].rearrange("p k a c -> p (k a c)")
    X, Q = 2 * TPB * CH, TPB * HID
    return (shared[:, 0:X].rearrange("p (r t c) -> p r t c", r=2, t=TPB),
            shared[:, X:X + Q].rearrange("p (t c) -> p t c", t=TPB),
            shared[:, X + Q:X + Q + 8 * CH].rearrange("p (r t c) -> p r t c", r=4, t=2))


def load_q(eng, d, s, n, k):
    lo, hi = CHUNKS[k]
    eng.dma_start(mix_buffers(s)[1][:, lo:hi, :].rearrange("p t c -> p (t c)"),
                  d["s_q"][bass.ds(n, 1), :, lo * HID:hi * HID].rearrange("o p c -> (o p) c")).then_inc(s["loaded_q"][k], 16)


def triangle_phase(nc, d, s):
    with ExitStack() as ctx:
        sb = lambda name, shape, dt=F32: ctx.enter_context(nc.sbuf_tensor(name, shape, dt))
        sem = lambda name: ctx.enter_context(nc.semaphore(name))
        sets = [s["operands"], {name: sb(name + "1", [P, N, CC]) for name in OPERANDS}]
        pp_low, ab1_low, ab1_high, ab2_low, lp_low, mov_high, sta_high = ([b[name] for b in sets] for name in OPERANDS)
        ab1T = sb("ab1T", [P, 2, N])
        psT = ctx.enter_context(nc.psum_tensor("psT_b", [P, 2, 512], F32))
        psO = ctx.enter_context(nc.psum_tensor("psO_b", [P, 4, 512], F32))
        loaded = s["operands_loaded"]
        turned, copied, summed, taken = sem("turned_b"), sem("copied_b"), sem("summed_b"), sem("taken_b")
        block = ctx.enter_context(nc.Block())
        def loops(eng, body):
            body(0, False)
            with eng.Fori(1, NCG // 2 - 1) as m:
                body(m, False)
            body(NCG // 2 - 1, True)

        @block.sync
        def _(sp):
            sp.wait_ge(s["stored_q"], 16 * NBLK)
            def body(m, last):
                for par in range(2):
                    g = 2 * m + par
                    need(sp, summed, CC * (g - 2) + CC if not isinstance(m, int) or m > 0 else 0)
                    if isinstance(m, int) and g == 0:
                        continue
                    for dst, src in group_loads(sets[par], d, g, 0, N):
                        sp.dma_start(dst, src).then_inc(loaded[par], 16)
            loops(sp, body)
            sp.wait_ge(summed, CC * (NCG - 1))
            for k in range(len(CHUNKS)):
                load_q(sp, d, s, 0, k)
            for p in range(2):
                for k, ch in enumerate(CHUNKS):
                    load_tiles(sp, mix_buffers(s)[0][:, p], d["x"], p, s["loaded_x"][p][k], ch)

        @block.tensor
        def _(pe):
            ident = s["ident"]

            def turn(m, par, c):
                C = CC * par + c
                if c == 0:
                    pe.wait_ge(loaded[par], 16 * N_LOADS * (m + 2 - par))
                need(pe, copied, 2 * CC * m + C - 1)
                lo, hi, t = ab1_low[par], ab1_high[par], psT[:, C % 2, :]
                nc.tensor.transpose(t[:, 0:P], lo[:, 0:P, c], ident[:])
                nc.tensor.transpose(t[:, P:N], hi[0:64, 0:P, c], ident[0:64, 0:64])
                nc.tensor.transpose(t[0:64, N:N + P], lo[:, P:N, c], ident[:])
                nc.tensor.transpose(t[0:64, N + P:2 * N], hi[0:64, P:N, c], ident[0:64, 0:64]).then_inc(turned, 1)

            def body(m, last):
                for C in range(2 * CC):
                    par, c = divmod(C, CC)
                    if c + 1 < CC:
                        turn(m, par, c + 1)
                    pe.wait_ge(copied, 2 * CC * m + C + 1)
                    need(pe, taken, 2 * CC * m + C - 3)
                    out = psO[:, C % 4, :]
                    steps = ((ab1T[:, C % 2, :], pp_low[par][:, :, c]), (lp_low[par][:, :, c], ab2_low[par][:, :, c]),
                             (sta_high[par][:, :, c], mov_high[par][:, :, c]))
                    for k, (sta, mov) in enumerate(steps):
                        nc.tensor.matmul(out[:, 0:N], sta[:, 0:P], mov, start=(k == 0), stop=(k == 2))
                    for h in range(2):
                        for k, (sta, mov) in enumerate(steps):
                            part = mov.rearrange("p (n u) -> p n u", u=BLOCK_A)[:, :, HALF_A * h:HALF_A * h + HALF_A]
                            ins = nc.tensor.matmul(out[64 * h:64 * h + 64, N:N + N // 2], sta[:, P:N], part,
                                                   start=(k == 0), stop=(k == 2))
                    ins.then_inc(summed, 1)
                    if C + 1 == CC:
                        turn(m, 1, 0)
                    elif C + 1 == 2 * CC and not last:
                        turn(m + 1, 0, 0)

            turn(0, 0, 0)
            loops(pe, body)

        @block.scalar
        def _(act):
            def body(m, last):
                for C in range(2 * CC):
                    par, c = divmod(C, CC)
                    act.wait_ge(turned, 2 * CC * m + C + 1)
                    need(act, summed, 2 * CC * m + C - 1)
                    nc.scalar.copy(ab1T[:, C % 2, :], psT[:, C % 2, 0:N])
                    nc.scalar.copy(sta_high[par][0:64, :, c], psT[0:64, C % 2, N:2 * N]).then_inc(copied, 1)
            loops(act, body)

        @block.vector
        def _(dve):
            tri = s["tri"][:].rearrange("p (n u) c -> p n u c", u=TPB)
            dve.wait_ge(s["stored_q"], 16 * NBLK)

            def body(m, last):
                for C in range(2 * CC):
                    dve.wait_ge(summed, 2 * CC * m + C + 1)
                    src = psO[:, C % 4, :]
                    at = bass.ds(2 * CC * m + C, 1)
                    nc.vector.tensor_copy(tri[:, :, 0:LOW, at].rearrange("p n u o -> p n (u o)"),
                                          src[:, 0:N].rearrange("p (n u) -> p n u", u=LOW))
                    nc.vector.tensor_copy(tri[:, :, LOW:TPB, at].rearrange("p n u o -> p n (u o)"),
                                          src[:, N:N + N // 2].rearrange("p (n u) -> p n u", u=HIGH)).then_inc(taken, 1)
            loops(dve, body)


PAIRS = TPB // 2
CHUNK_OF = [k for k, (lo, hi) in enumerate(CHUNKS) for _ in range(lo, hi)]
CHUNK_DMAS = (1, 1, 2)


def mix_phase(nc, d, s):
    with ExitStack() as ctx:
        sb = lambda name, shape, dt=F32: ctx.enter_context(nc.sbuf_tensor(name, shape, dt))
        sem = lambda name: ctx.enter_context(nc.semaphore(name))
        x_in, q_in, xh = mix_buffers(s)
        x2 = sb("x2_c", [P, 2, TPB, CH])
        coef_x, coef_t = sb("coef_x_now", [P, 2, 2, TPB]), sb("coef_t", [P, 2, 2, TPB])
        coef_2 = sb("coef_2_now", [P, 2, 2, TPB])
        tri_n = sb("tri_n", [P, 4, 2, HID])
        xT, gate, y = sb("xT_c", [P, 2, 3 * P]), sb("end_gate", [P, 2, 2, CH]), sb("y_c", [P, 2, 2, CH])
        stats_t, stats_x = sb("stats_t", [P, 2, TPB, 6]), sb("stats_x2", [P, 2, TPB, 6])
        work = sb("work_c", [P, 6, TPB])
        psT = ctx.enter_context(nc.psum_tensor("psT_c", [P, 2, 512], F32))
        psZ = ctx.enter_context(nc.psum_tensor("psZ_c", [P, 2, 512], F32))
        psW = ctx.enter_context(nc.psum_tensor("psW_c", [P, 2, 512], F32))
        chunk_sems = lambda name: [sem(f"{name}_{k}") for k in range(len(CHUNKS))]
        loaded_q, loaded_x = s["loaded_q"], s["loaded_x"]
        stored = [chunk_sems(f"stored_x2{par}") for par in range(2)]
        coefx_ready, normed_act, normed_pool = sem("coefx_ready"), sem("normed_act_c"), sem("normed_pool_c")
        tri_normed, turned, copied, projected, gated, tri_projected = (
            sem(k) for k in ("tri_normed_dve", "turned_c", "copied_c", "projected_c", "gated_c", "tri_projected"))
        tri_normed_act = sem("tri_normed_act")
        added, statted_t, statted_x, pool_passed = sem("added"), sem("statted_t"), sem("statted_x"), sem("pool_passed_c")
        stepped_t, stepped_x, coefst_ready, coefs2_ready = (
            sem(k) for k in ("stepped_t", "stepped_x2", "coefst_ready", "coefs2_ready"))
        y_made, x2_made, routed = sem("y_made"), sem("x2_made"), sem("routed")
        block = ctx.enter_context(nc.Block())
        ROUTE_FROM = 10
        PEELED = 2

        def loops(eng, slot, tail=0):
            for par in range(2):
                for j in range(PAIRS):
                    slot(0, par, j)
            with eng.Fori(1, NBLK // 2 - PEELED) as m:
                for par in range(2):
                    for j in range(PAIRS):
                        slot(m, par, j)
            for m in range(NBLK // 2 - PEELED, NBLK // 2):
                for par in range(2):
                    for j in range(PAIRS):
                        slot(m, par, j)
            for j in range(tail):
                slot(NBLK // 2, j // PAIRS, j % PAIRS)

        def there(m, par):
            return not isinstance(m, int) or 0 <= 2 * m + par < NBLK

        def after(m, par, j, k):
            if j + k >= PAIRS:
                m, par, j = (m, 1, j - PAIRS) if par == 0 else (m + 1, 0, j - PAIRS)
            return (m, par, j + k) if there(m, par) else None

        def next_block(m, par):
            return (m, 1) if par == 0 else (m + 1, 0)

        def last_block(m, par):
            return (m, 0) if par == 1 else (m - 1, 1)

        def to_add(m, par, j):
            if isinstance(m, int) and (m, par) == (0, 0):
                block = (0, 1) if j < PAIRS // 2 else (1, 0)
                return [block + (2 * j % PAIRS + i,) for i in range(2)]
            return [(m + 1, par, j)] if there(m + 1, par) else []

        @block.sync
        def _(sp):
            for k, (lo, hi) in enumerate(CHUNKS):
                sp.wait_ge(added, hi // 2)
                load_q(sp, d, s, 1, k)

            def slot(m, par, j):
                n = 2 * m + par
                for am, apar, pair in to_add(m, par, j):
                    k = CHUNK_OF[2 * pair]
                    if 2 * pair + 2 == CHUNKS[k][1] and there(*next_block(am, apar)):
                        sp.wait_ge(added, PAIRS * (2 * am + apar) + pair + 1)
                        load_q(sp, d, s, 2 * am + apar + 1, k)
                for k, (lo, hi) in enumerate(CHUNKS):
                    if j == hi // 2 - 1:
                        sp.wait_ge(x2_made, PAIRS * n + hi // 2)
                        sp.dma_start(d["s_x2"][bass.ds(n, 1), :, lo * CH:hi * CH].rearrange("o p c -> (o p) c"),
                                     x2[:, par, lo:hi, :].rearrange("p t c -> p (t c)")).then_inc(stored[par][k], 16)
                        if there(m + 1, par):
                            load_tiles(sp, x_in[:, par], d["x"], n + 2, loaded_x[par][k], (lo, hi))
            loops(sp, slot)
            for par in range(2):
                for k in range(len(CHUNKS)):
                    sp.wait_ge(stored[par][k], 16 * NBLK // 2)

        def norm_x(wait, op, sem_out, m, par, j, which):
            n, t = 2 * m + par, 2 * j + which
            k = CHUNK_OF[t]
            if j == 0:
                wait(coefx_ready, n + 1)
            if 2 * j == CHUNKS[k][0]:
                wait(loaded_x[par][k], 16 * CHUNK_DMAS[k] * (m + 1))
            if not isinstance(m, int) or PAIRS * n + j > 3:
                wait(turned, PAIRS * n + j - 3)
            op(xh[:, j % 4, which, :], x_in[:, par, t, :], coef_x[:, par, 0, t:t + 1], coef_x[:, par, 1, t:t + 1]
               ).then_inc(sem_out, 1)

        def norm_tri(eng, op, sem_out, m, par, j, which):
            n, t = 2 * m + par, 2 * j + which
            if j == 0:
                eng.wait_ge(coefst_ready, n + 1)
            need(eng, turned, PAIRS * n + j - 3)
            op(tri_n[:, j % 4, which, :], s["tri"][:, bass.ds(TPB * n + t, 1), :].rearrange("p o c -> p (o c)"),
               coef_t[:, par, 0, t:t + 1], coef_t[:, par, 1, t:t + 1]).then_inc(sem_out, 1)

        @block.scalar
        def _(act):
            def op(out, x, r, b):
                return nc.scalar.activation(out, x, ACT.Identity, bias=b, scale=r)

            def copy_turned(m, par, j):
                c = PAIRS * (2 * m + par) + j
                act.wait_ge(turned, c + 1)
                need(act, tri_projected, c - 1)
                nc.scalar.copy(xT[:, j % 2, :], psT[:, j % 2, 0:3 * P]).then_inc(copied, 1)

            def slot(m, par, j):
                c = PAIRS * (2 * m + par) + j
                three, one = after(m, par, j, 3), after(m, par, j, 1)
                if three:
                    norm_x(act.wait_ge, op, normed_act, *three, 0)
                    norm_tri(act, op, tri_normed_act, *three, 0)
                if one:
                    copy_turned(*one)
                act.wait_ge(projected, c + 1)
                need(act, y_made, c - 1)
                nc.scalar.activation(gate[:, j % 2], psZ[:, j % 2, 0:2 * CH].rearrange("p (t c) -> p t c", t=2),
                                     ACT.Sigmoid).then_inc(gated, 1)

            for j in range(3):
                norm_x(act.wait_ge, op, normed_act, 0, 0, j, 0)
                norm_tri(act, op, tri_normed_act, 0, 0, j, 0)
            copy_turned(0, 0, 0)
            loops(act, slot)

        @block.gpsimd
        def _(pool):
            def op(out, x, r, b):
                return nc.gpsimd.tensor_scalar(out, x, r, b, ALU.mult, ALU.add)

            def wait(sem, value):
                wait_by_event(pool, sem, value, pool_passed)

            def add_q(m, par, j):
                n, k = 2 * m + par, CHUNK_OF[2 * j]
                if 2 * j == CHUNKS[k][0]:
                    pool.wait_ge(loaded_q[k], 16 * (n + 1))
                pair = s["tri"][:, bass.ds(TPB * n + 2 * j, 2), :]
                nc.gpsimd.tensor_tensor(pair, pair, q_in[:, 2 * j:2 * j + 2, :], ALU.add).then_inc(added, 1)

            def slot(m, par, j):
                n = 2 * m + par
                three = after(m, par, j, 3)
                if three:
                    norm_x(wait, op, normed_pool, *three, 1)
                for pair in to_add(m, par, j):
                    add_q(*pair)
                k = CHUNK_OF[2 * j]
                pool.wait_ge(y_made, PAIRS * n + j + 1)
                if 2 * j == CHUNKS[k][0]:
                    need(pool, stored[par][k], 16 * m)
                if not isinstance(m, int) or m > 0:
                    pool.wait_ge(routed, PAIRS * (n - 2) + j + 1)
                nc.gpsimd.tensor_tensor(x2[:, par, 2 * j:2 * j + 2, :], y[:, j % 2], x_in[:, par, 2 * j:2 * j + 2, :],
                                        ALU.add).then_inc(x2_made, 1)

            for j in range(PAIRS):
                add_q(0, 0, j)
            for j in range(3):
                norm_x(wait, op, normed_pool, 0, 0, j, 1)
            loops(pool, slot)

        @block.tensor
        def _(pe):
            w_end = s["w_all"][:, 6 * HID:6 * HID + CH]

            def turn(m, par, j):
                c = PAIRS * (2 * m + par) + j
                pe.wait_ge(normed_act, c + 1)
                pe.wait_ge(normed_pool, c + 1)
                need(pe, copied, c - 1)
                for i in range(2):
                    nc.tensor.transpose(psT[:, j % 2, i * P:i * P + P], xh[:, j % 4, i, :], s["ident"][:])
                pe.wait_ge(tri_normed_act, c + 1)
                pe.wait_ge(tri_normed, c + 1)
                nc.tensor.transpose(psT[:, j % 2, 2 * P:3 * P], tri_n[:, j % 4].rearrange("p t c -> p (t c)"), s["ident"][:]
                                    ).then_inc(turned, 1)

            def slot(m, par, j):
                n = 2 * m + par
                c = PAIRS * n + j
                if there(m, par):
                    one = after(m, par, j, 1)
                    if one:
                        turn(*one)
                    pe.wait_ge(copied, c + 1)
                    need(pe, gated, c - 1)
                    for i in range(2):
                        ins = nc.tensor.matmul(psZ[:, j % 2, CH * i:CH * i + CH], xT[:, j % 2, i * P:i * P + P], w_end,
                                               start=True, stop=True)
                    ins.then_inc(projected, 1)
                    need(pe, y_made, c - 1)
                    nc.tensor.matmul(psW[:, j % 2, 0:2 * CH], xT[:, j % 2, 2 * P:3 * P], s["ws2"][:], start=True, stop=True
                                     ).then_inc(tri_projected, 1)
                if j >= ROUTE_FROM:
                    (rm, rpar), pair = last_block(m, par), j - ROUTE_FROM
                else:
                    (rm, rpar), pair = (m - 1, par), j + PAIRS - ROUTE_FROM
                if there(rm, rpar):
                    if pair == 0:
                        pe.wait_ge(coefs2_ready, 2 * rm + rpar + 1)
                    for t in (2 * pair, 2 * pair + 1):
                        ins = nc.tensor.matmul(s["psR"][0:1, 0:CH], coef_2[:, rpar, 0, t:t + 1], x2[:, rpar, t, :],
                                               start=False, stop=False)
                    ins.then_inc(routed, 1)

            nc.tensor.matmul(s["psR"][0:1, 0:CH], s["ones"][0:HID, 0:1], s["ws2"][0:HID, CH:2 * CH], start=True, stop=False)
            turn(0, 0, 0)
            loops(pe, slot, PAIRS + ROUTE_FROM)

        @block.vector
        def _(dve):
            v = nc.vector
            steps_t, steps_x = LN_STEPS + 2, LN_STEPS + 1

            def coef_x_of(m, par):
                n = 2 * m + par
                v.tensor_copy(coef_x[:, par], s["coef_x"][:, :, bass.ds(TPB * n, TPB)]).then_inc(coefx_ready, 1)

            def op(out, x, r, b):
                return v.tensor_scalar(out, x, r, b, ALU.mult, ALU.add)

            def stats_tri(m, par, j):
                n = 2 * m + par
                dve.wait_ge(added, PAIRS * n + j + 1)
                for t in (2 * j, 2 * j + 1):
                    ins = v.bn_stats(stats_t[:, par, t, :], s["tri"][:, bass.ds(TPB * n + t, 1), :].rearrange("p o c -> p (o c)"))
                if j == PAIRS - 1:
                    ins.then_inc(statted_t, 1)

            def coef_step_t(m, par, step):
                n = 2 * m + par
                before = (LN_STEPS + 1) * n
                now = coef_t[:, par]
                if step < LN_STEPS:
                    if step == 0:
                        dve.wait_ge(statted_t, n + 1)
                    ln_step(nc, dve, step, stepped_t, before, stats_t[:, par], work, HID, 1.0, EPS5, now[:, 0, :], now[:, 1, :])
                elif step == LN_STEPS:
                    dve.wait_ge(stepped_t, before + LN_STEPS)
                    v.tensor_scalar(now[:, 1, :], now[:, 1, :], 1.0, None, ALU.add).then_inc(stepped_t, 1)
                else:
                    dve.wait_ge(stepped_t, before + LN_STEPS + 1)
                    zm = s["mask"][:, bass.ds(TPB * n, TPB)].unsqueeze(1).broadcast_to([P, 2, TPB])
                    v.tensor_tensor(now, now, zm, ALU.mult).then_inc(coefst_ready, 1)

            def stats_x2(m, par, j):
                n = 2 * m + par
                dve.wait_ge(x2_made, PAIRS * n + j + 1)
                for t in (2 * j, 2 * j + 1):
                    ins = v.bn_stats(stats_x[:, par, t, :], x2[:, par, t, :])
                if j == PAIRS - 1:
                    ins.then_inc(statted_x, 1)

            def coef_step_x2(m, par, step):
                n = 2 * m + par
                before = LN_STEPS * n
                if step == 0:
                    dve.wait_ge(statted_x, n + 1)
                    need(dve, routed, PAIRS * (n - 1) + 1)
                if step < LN_STEPS:
                    ln_step(nc, dve, step, stepped_x, before, stats_x[:, par], work, CH, 1.0, EPS5, coef_2[:, par, 0, :], coef_2[:, par, 1, :])
                else:
                    dve.wait_ge(stepped_x, before + LN_STEPS)
                    v.tensor_copy(s["coef_2"][:, :, bass.ds(TPB * n, TPB)], coef_2[:, par]).then_inc(coefs2_ready, 1)

            def slot(m, par, j):
                n = 2 * m + par
                now, ahead, behind = there(m, par), there(*next_block(m, par)), there(*last_block(m, par))
                three = after(m, par, j, 3)
                first_t, per_t = (6, 7) if isinstance(m, int) and (m, par) == (0, 0) else (0, 4)
                first_x, per_x = 5, 4
                for part in range(max(per_t, per_x)):
                    if behind and j >= first_x and part < per_x and per_x * (j - first_x) + part < steps_x:
                        coef_step_x2(*last_block(m, par), per_x * (j - first_x) + part)
                    if ahead and j >= first_t and part < per_t and per_t * (j - first_t) + part < steps_t:
                        coef_step_t(*next_block(m, par), per_t * (j - first_t) + part)
                    if part == 0 and three:
                        norm_tri(dve, op, tri_normed, *three, 1)
                    if part == 1 and now:
                        if j == 0 and ahead:
                            coef_x_of(*next_block(m, par))
                        c = PAIRS * n + j
                        dve.wait_ge(tri_projected, c + 1)
                        dve.wait_ge(gated, c + 1)
                        need(dve, x2_made, c - 1)
                        v.tensor_tensor(y[:, j % 2], psW[:, j % 2, 0:2 * CH].rearrange("p (t c) -> p t c", t=2),
                                        gate[:, j % 2], ALU.mult).then_inc(y_made, 1)
                    if part == 2:
                        if j > 0 and now:
                            stats_x2(m, par, j - 1)
                        if j == 0 and behind:
                            stats_x2(*last_block(m, par), PAIRS - 1)
                    if part == 3:
                        for pair in to_add(m, par, j):
                            stats_tri(*pair)

            coef_x_of(0, 0)
            for j in range(PAIRS):
                stats_tri(0, 0, j)
            for step in range(steps_t):
                coef_step_t(0, 0, step)
            for j in range(3):
                norm_tri(dve, op, tri_normed, 0, 0, j, 1)
            loops(dve, slot, ROUTE_FROM)


def load_x2(eng, d, s, n, k):
    lo, hi = CHUNKS[k]
    eng.dma_start(s["x2"][:, lo:hi, :].rearrange("p t c -> p (t c)"),
                  d["s_x2"][bass.ds(n, 1), :, lo * CH:hi * CH].rearrange("o p c -> (o p) c")).then_inc(s["x2_loaded"][k], 16)


def norm_x2(nc, s, n, g, i):
    t = 4 * g + i
    r, b = (s["coef_2"][:, q, bass.ds(TPB * n + t, 1)] for q in range(2))
    ins = nc.vector.tensor_scalar(s["xh_d"][:, g % 2, i, :], s["x2"][:, t, :], r, b, ALU.mult, ALU.add)
    if i == 3:
        ins.then_inc(s["normed_d"], 1)


def route_phase(nc, d, s):
    with ExitStack() as ctx:
        sb = lambda name, shape, dt=F32: ctx.enter_context(nc.sbuf_tensor(name, shape, dt))
        sem = lambda name: ctx.enter_context(nc.semaphore(name))
        E = EXPERTS
        wr, br = sb("wr", [CH, E]), sb("br", [1, E])
        shift_sum = sb("shift_sum", [P, 1])
        mean, mean_col = sb("mean_row", [1, CH]), sb("mean_col", [CH, 1])
        vec = sb("router_rows", [1, 12, E])
        scal = sb("router_scalars", [1, 16])
        sq = sb("router_squares", [1, 3, E, E])
        pick = sb("router_picks", [1, 2, E])
        pick_v = sb("router_pick_v", [1, 2, E])
        chosen, w_pair = sb("chosen", [1, 2], I32), sb("w_pair", [1, 2])
        chosen_f, val = sb("chosen_f", [1, 2]), sb("chosen_val", [1, 2])
        w_col = sb("w_col", [P, 2])
        w2_raw, b2_raw = sb("w2_raw", [P, NCHUNK, CH]), sb("b2_raw", [1, 2, CH])
        b2_row, b1_rows = sb("b2_row", [1, CH]), sb("b1_rows", [NCHUNK, P])
        ps = ctx.enter_context(nc.psum_tensor("ps_route", [P, 4, 512], F32))
        loaded, below_made, own, own_a = sem("route_loaded"), sem("below_made"), sem("dve_own_r"), sem("act_exp")
        summed_shift, summed_all, mean_made, turned, mean_kept, logits = (
            sem(k) for k in ("summed_shift", "summed_all", "mean_made", "mean_turned", "mean_kept", "logits"))
        max_made, probs_ready, gap_made, chosen_made, experts_loaded = (
            sem(k) for k in ("max_made", "probs_ready", "gap_made", "chosen_made", "experts_loaded"))
        weights_made, weights_spread, b1_turned, b2_made, b2_spread = (
            sem(k) for k in ("weights_made", "weights_spread", "b1_turned", "b2_made", "b2_spread"))
        block = ctx.enter_context(nc.Block())
        affine_loaded = sem("affine_loaded")
        below = sq[:, 2]

        @block.gpsimd
        def _(pool):
            nc.gpsimd.memset(below, 1.0).then_inc(below_made, 1)
            pool.wait_ge(below_made, 1)
            nc.gpsimd.affine_select(out=below, in_=below, compare_op=ALU.is_gt, fill=0.0, base=0,
                                    pattern=[[1, E], [-1, E]], channel_multiplier=0).then_inc(below_made, 1)

        @block.sync
        def _(sp):
            sp.dma_start(wr[:], d["Wr"]).then_inc(loaded, 16)
            sp.dma_start(br[:], d["br"].rearrange("(o e) -> o e", o=1)).then_inc(loaded, 16)
            for k in range(len(CHUNKS)):
                load_x2(sp, d, s, 0, k)
            for k in ("gamma", "beta"):
                sp.dma_start(s[k][:], d[k].rearrange("(o c) -> o c", o=1).broadcast_to([P, CH])).then_inc(affine_loaded, 16)
            sp.wait_ge(chosen_made, 1)
            for k in range(2):
                e = sp.value_load(chosen[0:1, k:k + 1], min_val=0, max_val=E - 1)
                at = bass.ds(e, 1)
                half = slice(k * FF // P, (k + 1) * FF // P)
                sp.dma_start(s["w1"][:, k * FF:(k + 1) * FF], d["W1e"][at].rearrange("o c f -> (o c) f")).then_inc(experts_loaded, 16)
                sp.dma_start(w2_raw[:, half, :], d["W2e"][at].rearrange("o (c p) d -> p (o c) d", p=P)).then_inc(experts_loaded, 16)
                sp.dma_start(b1_rows[half, :], d["b1e"][at].rearrange("o (c p) -> (o c) p", p=P)).then_inc(experts_loaded, 16)
                sp.dma_start(b2_raw[0:1, k, :], d["b2e"][at]).then_inc(experts_loaded, 16)
            sp.wait_ge(experts_loaded, 8 * 16)
            sp.wait_ge(affine_loaded, 2 * 16)

        @block.tensor
        def _(pe):
            ones = s["ones"]
            psR = s["psR"][0:1, 0:CH]
            pe.wait_ge(summed_shift, 1)
            nc.tensor.matmul(psR, shift_sum[:], ones[:], start=False, stop=True).then_inc(summed_all, 1)
            pe.wait_ge(mean_made, 1)
            nc.tensor.matmul(ps[:, 0, 0:1], mean[:], ones[0:1, 0:1], start=True, stop=True).then_inc(turned, 1)
            pe.wait_ge(mean_kept, 1)
            pe.wait_ge(loaded, 32)
            nc.tensor.matmul(ps[0:1, 1, 0:E], mean_col[:], wr[:], start=True, stop=False)
            nc.tensor.matmul(ps[0:1, 1, 0:E], ones[0:1, 0:1], br[:], start=False, stop=True).then_inc(logits, 1)
            pe.wait_ge(weights_made, 1)
            nc.tensor.matmul(ps[:, 2, 0:2], ones[0:1, :], w_pair[:], start=True, stop=True).then_inc(weights_spread, 1)
            pe.wait_ge(experts_loaded, 8 * 16)
            nc.tensor.transpose(ps[:, 0, 0:NCHUNK], b1_rows[:], s["ident"][0:NCHUNK, 0:NCHUNK]).then_inc(b1_turned, 1)
            pe.wait_ge(b2_made, 1)
            nc.tensor.matmul(ps[:, 3, 0:CH], ones[0:1, :], b2_row[:], start=True, stop=True).then_inc(b2_spread, 1)

        @block.scalar
        def _(act):
            act.wait_ge(max_made, 1)
            nc.scalar.activation(vec[:, 0], ps[0:1, 1, 0:E], ACT.Exp, bias=scal[:, 0:1], accum_out=scal[:, 1:2]).then_inc(own_a, 1)
            act.wait_ge(probs_ready, 1)
            nc.scalar.activation(vec[:, 3], vec[:, 2], ACT.Exp, bias=scal[:, 3:4], accum_out=scal[:, 4:5]).then_inc(own_a, 1)
            act.wait_ge(gap_made, 1)
            nc.scalar.activation(scal[:, 6:7], scal[:, 5:6], ACT.Exp).then_inc(own_a, 1)

        @block.vector
        def _(dve):
            chain = Chain(dve, own)
            v = nc.vector
            L = chain.link
            v.reduce_sum(shift_sum[:], s["coef_2"][:, 1, :], AX.X).then_inc(summed_shift, 1)
            dve.wait_ge(summed_all, 1)
            v.tensor_scalar(mean[:], s["psR"][0:1, 0:CH], 1.0 / TOKENS, None, ALU.mult).then_inc(mean_made, 1)
            dve.wait_ge(turned, 1)
            v.tensor_copy(mean_col[:], ps[:, 0, 0:1]).then_inc(mean_kept, 1)
            dve.wait_ge(logits, 1)
            L(v.reduce_max(scal[:, 2:3], ps[0:1, 1, 0:E], AX.X))
            v.tensor_scalar(scal[:, 0:1], scal[:, 2:3], -1.0, None, ALU.mult).then_inc(max_made, 1)
            dve.wait_ge(own_a, 1)
            L(v.reciprocal(scal[:, 7:8], scal[:, 1:2]))
            L(v.tensor_scalar(vec[:, 1], vec[:, 0], scal[:, 7:8], None, ALU.mult))
            L(v.tensor_scalar(vec[:, 2], vec[:, 1], CAPACITY / TOKENS, None, ALU.min))
            L(v.reduce_max(scal[:, 2:3], vec[:, 2], AX.X))
            v.tensor_scalar(scal[:, 3:4], scal[:, 2:3], -1.0, None, ALU.mult).then_inc(probs_ready, 1)
            by_f = vec[:, 2].unsqueeze(1).broadcast_to([1, E, E])
            by_e = vec[:, 2].unsqueeze(2).broadcast_to([1, E, E])
            dve.wait_ge(below_made, 2)
            v.tensor_tensor(sq[:, 0], by_f, by_e, ALU.is_gt)
            L(v.tensor_tensor(sq[:, 1], by_f, by_e, ALU.is_equal))
            L(v.tensor_tensor(sq[:, 1], sq[:, 1], below, ALU.mult))
            L(v.tensor_tensor(sq[:, 0], sq[:, 0], sq[:, 1], ALU.add))
            v.reduce_sum(vec[:, 4], sq[:, 0], AX.X)
            L(v.reduce_sum(vec[:, 5], below, AX.X))
            for k in range(2):
                ins = v.tensor_scalar(pick[:, k], vec[:, 4], float(k), None, ALU.is_equal)
            L(ins)
            L(v.tensor_tensor(pick_v[:], pick[:], vec[:, 5].unsqueeze(1).broadcast_to([1, 2, E]), ALU.mult))
            L(v.reduce_sum(chosen_f[:], pick_v[:], AX.X))
            v.tensor_copy(chosen[:], chosen_f[:]).then_inc(chosen_made, 1)
            dve.wait_ge(own_a, 2)
            L(v.reciprocal(scal[:, 8:9], scal[:, 4:5]))
            L(v.tensor_scalar(vec[:, 6], vec[:, 3], scal[:, 8:9], None, ALU.mult))
            L(v.tensor_tensor(pick_v[:], pick[:], vec[:, 6].unsqueeze(1).broadcast_to([1, 2, E]), ALU.mult))
            L(v.reduce_sum(val[:], pick_v[:], AX.X))
            v.tensor_tensor(scal[:, 5:6], val[:, 1:2], val[:, 0:1], ALU.subtract).then_inc(gap_made, 1)
            dve.wait_ge(own_a, 3)
            L(v.tensor_scalar(scal[:, 9:10], scal[:, 6:7], 1.0, None, ALU.add))
            L(v.reciprocal(w_pair[:, 0:1], scal[:, 9:10]))
            v.tensor_tensor(w_pair[:, 1:2], scal[:, 6:7], w_pair[:, 0:1], ALU.mult).then_inc(weights_made, 1)
            dve.wait_ge(s["x2_loaded"][0], 16)
            for g in range(2):
                for k in range(4):
                    norm_x2(nc, s, 0, g, k)
            dve.wait_ge(weights_spread, 1)
            L(v.tensor_copy(w_col[:], ps[:, 2, 0:2]))
            dve.wait_ge(experts_loaded, 8 * 16)
            L(v.tensor_scalar(b2_raw[:, 1, :], b2_raw[:, 1, :], w_col[0:1, 1:2], None, ALU.mult))
            v.scalar_tensor_tensor(b2_row[:], b2_raw[:, 0, :], w_col[0:1, 0:1], b2_raw[:, 1, :], ALU.mult, ALU.add).then_inc(b2_made, 1)
            for k in range(2):
                half = slice(k * FF // P, (k + 1) * FF // P)
                v.tensor_scalar(s["w2"][:, half, :], w2_raw[:, half, :], w_col[:, k:k + 1], None, ALU.mult)
            L(v.tensor_copy(s["w1_high"][:], s["w1"][:]))
            v.tensor_tensor(s["w1_low"][:], s["w1"][:], s["w1_high"][:].bitcast(F32), ALU.subtract)
            dve.wait_ge(b2_spread, 1)
            v.tensor_copy(s["b2"][:], ps[:, 3, 0:CH])
            dve.wait_ge(b1_turned, 1)
            v.tensor_copy(s["b1"][:], ps[:, 0, 0:NCHUNK])


GROUPS_D = TPB // 4


def ffn_phase(nc, d, s):
    with ExitStack() as ctx:
        sb = lambda name, shape, dt=F32: ctx.enter_context(nc.sbuf_tensor(name, shape, dt))
        sem = lambda name: ctx.enter_context(nc.semaphore(name))
        G4 = 4 * CH
        x2 = s["x2"]
        x2b, vv, o_buf = sb("x2_beta", [P, TPB, CH]), sb("ffn_sum", [P, TPB, CH]), sb("out_buf", [P, TPB, CH])
        xh, xb, u = s["xh_d"], sb("xh_b2", [P, 2, 4, CH]), sb("u_d", [P, 2, 4, CH])
        xT_high, xT_low = sb("xT_high", [P, 2, G4], F32R), sb("xT_low", [P, 2, G4], F32R)
        hT = sb("hT", [P, 2, NCHUNK, G4])
        stats, work, coef = sb("stats_d", [P, 2, 4, 6]), sb("work_d", [P, 6, 4]), sb("coef_d", [P, 2, 2, 4])
        psT = ctx.enter_context(nc.psum_tensor("psT_d", [P, 2, 512], F32))
        psH = ctx.enter_context(nc.psum_tensor("psH_d", [P, NCHUNK, 512], F32))
        psY = ctx.enter_context(nc.psum_tensor("psY_d", [P, 2, 512], F32))
        loaded, stored = s["x2_loaded"], [sem(f"stored_out_{i}") for i in range(len(CHUNKS))]
        normed = s["normed_d"]
        turned, copied, raised, gelued, lowered = (sem(f"{k}_d") for k in ("turned", "copied", "raised", "gelued", "lowered"))
        xb_made, x2b_made, v_made, u_made, scaled, final = (
            sem(k) for k in ("xb_made", "x2b_made", "v_made", "u_made", "scaled", "final"))
        split = sem("split_d")
        statted, stepped = sem("statted_d"), sem("coef_stepped_d")
        block = ctx.enter_context(nc.Block())
        NG = GROUPS_D

        def loops(eng, slot, tail=0):
            for n in range(2):
                for g in range(NG):
                    slot(n, g, False)
            with eng.Fori(2, NBLK - 1) as n:
                for g in range(NG):
                    slot(n, g, False)
            for g in range(NG):
                slot(NBLK - 1, g, True)
            for g in range(tail):
                slot(NBLK, g, True)

        def back(n, g, k):
            if g >= k:
                return (n, g - k) if not isinstance(n, int) or n < NBLK else None
            return None if isinstance(n, int) and n == 0 else (n - 1, g - k + NG)

        def following(n, g, last, k=1):
            if g + k < NG:
                return (n, g + k) if not isinstance(n, int) or n < NBLK else None
            return None if last else (n + 1, g + k - NG)

        @block.sync
        def _(sp):
            def store(m, k):
                lo, hi = CHUNKS[k]
                sp.wait_ge(final, NG * m + hi // 4)
                if hi <= LOW:
                    sp.dma_start(d["out"][bass.ds(BLOCK_A * m + lo, hi - lo), 0:P, :].rearrange("a b c -> b a c"),
                                 o_buf[:, lo:hi, :]).then_inc(stored[k], 16)
                else:
                    for h in range(2):
                        sp.dma_start(d["out"][bass.ds(BLOCK_A * m + HALF_A * h, HALF_A), P:N, :].rearrange("a b c -> b a c"),
                                     o_buf[64 * h:64 * h + 64, lo:hi, :]).then_inc(stored[k], 16)

            def slot(n, g, last):
                if g % 2 == 0:
                    return
                if g == NG - 1:
                    store(n, 0)
                elif not isinstance(n, int) or n > 0:
                    store(n - 1, g // 2 + 1)
                if not last:
                    sp.wait_ge(normed, NG * n + g + 1)
                    sp.wait_ge(x2b_made, NG * n + g + 1)
                    load_x2(sp, d, s, n + 1, g // 2)
            loops(sp, slot)
            store(NBLK - 1, 1)
            store(NBLK - 1, 2)
            for k in range(len(CHUNKS)):
                sp.wait_ge(stored[k], 16 * CHUNK_DMAS[k] * NBLK)

        @block.scalar
        def _(act):
            def copy_turned(n, g):
                act.wait_ge(turned, NG * n + g + 1)
                need(act, raised, NCHUNK * (NG * n + g - 1))
                nc.scalar.copy(xT_high[:, g % 2, :], psT[:, g % 2, :]).then_inc(copied, 1)

            def scale_v(n, g):
                act.wait_ge(stepped, LN_STEPS * (NG * n + g + 1))
                need(act, final, NG * n + g - 1)
                for i in range(4):
                    ins = nc.scalar.activation(u[:, g % 2, i, :], vv[:, 4 * g + i, :], ACT.Identity,
                                               bias=coef[:, g % 2, 1, i:i + 1], scale=coef[:, g % 2, 0, i:i + 1])
                ins.then_inc(u_made, 1)

            def slot(n, g, last):
                if not (isinstance(n, int) and n == NBLK):
                    for f in range(NCHUNK):
                        act.wait_ge(raised, NCHUNK * (NG * n + g) + f + 1)
                        if f == 0:
                            need(act, lowered, NG * n + g - 1)
                        nc.scalar.activation(hT[:, g % 2, f, :], psH[:, f, :], ACT.Gelu, bias=s["b1"][:, f:f + 1]).then_inc(gelued, 1)
                nxt, three = following(n, g, last), back(n, g, 3)
                if nxt:
                    copy_turned(*nxt)
                if three:
                    scale_v(*three)
            copy_turned(0, 0)
            loops(act, slot, 3)

        @block.tensor
        def _(pe):
            def turn(n, g):
                pe.wait_ge(normed, NG * n + g + 1)
                need(pe, split, NG * n + g - 1)
                for i in range(4):
                    ins = nc.tensor.transpose(psT[:, g % 2, i * P:i * P + P], xh[:, g % 2, i, :], s["ident"][:])
                ins.then_inc(turned, 1)

            def slot(n, g, last):
                pe.wait_ge(copied, NG * n + g + 1)
                pe.wait_ge(split, NG * n + g + 1)
                for f in range(NCHUNK):
                    need(pe, gelued, NCHUNK * (NG * n + g - 1) + f + 1)
                    high, low = (s[w][:, f * P:f * P + P] for w in ("w1_high", "w1_low"))
                    nc.tensor.matmul(psH[:, f, :], high, xT_high[:, g % 2, :], start=True, stop=False)
                    nc.tensor.matmul(psH[:, f, :], high, xT_low[:, g % 2, :], start=False, stop=False)
                    nc.tensor.matmul(psH[:, f, :], low, xT_high[:, g % 2, :], start=False, stop=True).then_inc(raised, 1)
                nxt = following(n, g, last)
                if nxt:
                    turn(*nxt)
                need(pe, v_made, NG * n + g - 1)
                for i in range(4):
                    for f in range(NCHUNK):
                        if i == 0:
                            pe.wait_ge(gelued, NCHUNK * (NG * n + g) + f + 1)
                        ins = nc.tensor.matmul(psY[:, g % 2, i * CH:i * CH + CH], hT[:, g % 2, f, i * P:i * P + P],
                                               s["w2"][:, f, :], start=(f == 0), stop=(f == NCHUNK - 1))
                ins.then_inc(lowered, 1)
            turn(0, 0)
            loops(pe, slot)

        @block.gpsimd
        def _(pool):
            def spread(row):
                return row.unsqueeze(1).broadcast_to([P, 4, CH])

            def slot(n, g, last):
                four = back(n, g, 4)
                if four:
                    m, h = four
                    pool.wait_ge(u_made, NG * m + h + 1)
                    nc.gpsimd.tensor_tensor(u[:, h % 2], u[:, h % 2], spread(s["gamma"][:]), ALU.mult).then_inc(scaled, 1)
                if not (isinstance(n, int) and n == NBLK):
                    k = CHUNK_OF[4 * g]
                    pool.wait_ge(normed, NG * n + g + 1)
                    need(pool, v_made, NG * n + g - 1)
                    nc.gpsimd.tensor_tensor(xb[:, g % 2], xh[:, g % 2], spread(s["b2"][:]), ALU.add).then_inc(xb_made, 1)
                    if 4 * g == CHUNKS[k][0]:
                        pool.wait_ge(loaded[k], 16 * (n + 1))
                    need(pool, final, NG * (n - 1) + g + 1)
                    nc.gpsimd.tensor_tensor(x2b[:, 4 * g:4 * g + 4, :], x2[:, 4 * g:4 * g + 4, :], spread(s["beta"][:]),
                                            ALU.add).then_inc(x2b_made, 1)
            loops(pool, slot, 4)

        @block.vector
        def _(dve):
            v = nc.vector

            def norm(n, g, i):
                t = 4 * g + i
                if i == 0:
                    k = CHUNK_OF[t]
                    if t == CHUNKS[k][0]:
                        dve.wait_ge(loaded[k], 16 * (n + 1))
                    need(dve, turned, NG * n + g - 1)
                    need(dve, xb_made, NG * n + g - 1)
                norm_x2(nc, s, n, g, i)

            def split_low(n, g):
                dve.wait_ge(copied, NG * n + g + 1)
                need(dve, raised, NCHUNK * (NG * n + g - 1))
                v.tensor_tensor(xT_low[:, g % 2, :], psT[:, g % 2, :], xT_high[:, g % 2, :].bitcast(F32), ALU.subtract
                                ).then_inc(split, 1)

            def stats_of(n, g, i):
                if i == 0:
                    dve.wait_ge(v_made, NG * n + g + 1)
                ins = v.bn_stats(stats[:, g % 2, i, :], vv[:, 4 * g + i, :])
                if i == 3:
                    ins.then_inc(statted, 1)

            def coef_step(n, g, step):
                before = LN_STEPS * (NG * n + g)
                if step == 0:
                    dve.wait_ge(statted, NG * n + g + 1)
                    need(dve, stepped, before)
                    need(dve, u_made, NG * n + g - 1)
                ln_step(nc, dve, step, stepped, before, stats[:, g % 2], work, CH, 1.0, EPS5, coef[:, g % 2, 0, :], coef[:, g % 2, 1, :])

            def finish(n, g):
                k = CHUNK_OF[4 * g]
                dve.wait_ge(scaled, NG * n + g + 1)
                if 4 * g == CHUNKS[k][0]:
                    need(dve, stored[k], 16 * CHUNK_DMAS[k] * n)
                tiles = slice(4 * g, 4 * g + 4)
                v.tensor_tensor(o_buf[:, tiles, :], u[:, g % 2], x2b[:, tiles, :], ALU.add).then_inc(final, 1)

            def slot(n, g, last):
                one, two, four = (back(n, g, k) for k in (1, 2, 4))
                nxt, nxt2 = following(n, g, last), following(n, g, last, 2)
                for step in range(LN_STEPS):
                    if two:
                        coef_step(*two, step)
                    if step < 4 and nxt2:
                        norm(*nxt2, step)
                    if 4 <= step < 8 and one:
                        stats_of(*one, step - 4)
                    if step == 8 and four:
                        finish(*four)
                    if step == 11 and nxt:
                        split_low(*nxt)
                if not (isinstance(n, int) and n == NBLK):
                    dve.wait_ge(lowered, NG * n + g + 1)
                    dve.wait_ge(xb_made, NG * n + g + 1)
                    v.tensor_tensor(vv[:, 4 * g:4 * g + 4, :], psY[:, g % 2, :].rearrange("p (t c) -> p t c", t=4), xb[:, g % 2],
                                    ALU.add).then_inc(v_made, 1)

            split_low(0, 0)
            loops(dve, slot, 4)


def metaformer_kernel(nc, x, l_pair, protein_pair, inter_pair, z_mask, ln_g, ln_b, lnc_g, lnc_b, Wg1, bg1, Wg2, bg2,
                      Wg3, bg3, W1, b1, W2, b2, W3, b3, Wend, bend, Wsum, bsum, Wr, br, W1e, b1e, W2e, b2e, gamma, beta, out):
    grid = lambda ap: ap.rearrange("o a b c -> (o a) b c")
    d = dict(x=grid(x), lp=grid(l_pair), pp=grid(protein_pair), ip=grid(inter_pair), zm=z_mask.rearrange("o a b -> (o a) b"),
             ln_g=ln_g, ln_b=ln_b, lnc_g=lnc_g, lnc_b=lnc_b, Wg1=Wg1, bg1=bg1, Wg2=Wg2, bg2=bg2, Wg3=Wg3, bg3=bg3,
             W1=W1, b1=b1, W2=W2, b2=b2, W3=W3, b3=b3, Wend=Wend, bend=bend, Wsum=Wsum, bsum=bsum,
             Wr=Wr, br=br, W1e=W1e, b1e=b1e, W2e=W2e, b2e=b2e, gamma=gamma, beta=beta, out=grid(out))
    scratch = lambda name, shape: nc.dram_tensor(name, shape, F32, kind="Internal").ap()
    d["s_ab"] = scratch("scratch_ab", (N, 2 * NCG, N * CC))
    d["s_pp"] = scratch("scratch_pp", (N, NCG, N * CC))
    d["s_lp"] = scratch("scratch_lp", (N, NCG, N * CC))
    d["s_q"] = scratch("scratch_q", (NBLK, P, TPB * HID))
    d["s_x2"] = scratch("scratch_x2", (NBLK, P, TPB * CH))
    with ExitStack() as ctx:
        s = {}
        for name, shape in (("ident", [P, P]), ("ones", [P, P]), ("w_all", [P, 6 * HID + CH]), ("ws2", [P, 2 * CH]),
                            ("mask", [P, NBLK * TPB]), ("coef_x", [P, 2, NBLK * TPB]), ("coef_2", [P, 2, NBLK * TPB]),
                            ("w1", [P, 2 * FF]), ("w2", [P, NCHUNK, CH]), ("b1", [P, NCHUNK]), ("b2", [P, CH]),
                            ("gamma", [P, CH]), ("beta", [P, CH])):
            s[name] = ctx.enter_context(nc.sbuf_tensor(name, shape, F32))
        for name in ("w1_high", "w1_low"):
            s[name] = ctx.enter_context(nc.sbuf_tensor(name, [P, 2 * FF], F32R))
        s["x2"] = ctx.enter_context(nc.sbuf_tensor("x2_d", [P, TPB, CH], F32))
        s["x2_loaded"] = [ctx.enter_context(nc.semaphore(f"loaded_d_{k}")) for k in range(len(CHUNKS))]
        s["stored_q"], s["normed_d"] = (ctx.enter_context(nc.semaphore(k)) for k in ("stored_q", "normed_d"))
        s["xh_d"] = ctx.enter_context(nc.sbuf_tensor("xh_d", [P, 2, 4, CH], F32))
        chunk_sems = lambda name: [ctx.enter_context(nc.semaphore(f"{name}_{k}")) for k in range(len(CHUNKS))]
        s["loaded_q"], s["loaded_x"] = chunk_sems("loaded_qc"), [chunk_sems(f"loaded_xc{par}") for par in range(2)]
        s["operands_loaded"] = [ctx.enter_context(nc.semaphore(f"loaded_{k}")) for k in ("even", "odd")]
        s["shared"] = ctx.enter_context(nc.sbuf_tensor("shared", [P, len(OPERANDS), N, CC], F32))
        s["operands"] = {name: s["shared"][:, k] for k, name in enumerate(OPERANDS)}
        project_phase(nc, d, s)
        with nc.sbuf_tensor("tri", [P, NBLK * TPB, HID], F32) as tri:
            s["tri"] = tri
            triangle_phase(nc, d, s)
            with nc.psum_tensor("psR", [P, 512], F32) as psR:
                s["psR"] = psR
                mix_phase(nc, d, s)
                route_phase(nc, d, s)
        ffn_phase(nc, d, s)


_CONV = ['l_pair', 'protein_pair', 'inter_pair', 'z_mask', 'ln_g', 'ln_b', 'lnc_g', 'lnc_b', 'Wg1', 'bg1', 'Wg2', 'bg2',
         'Wg3', 'bg3', 'W1', 'b1', 'W2', 'b2', 'W3', 'b3', 'Wend', 'bend', 'Wsum', 'bsum']
_FFN = ['Wr', 'br', 'W1', 'b1', 'W2', 'b2', 'gamma', 'beta']
_INS = ['x'] + ['L0_conv_' + n for n in _CONV] + ['L0_ffn_' + n for n in _FFN]


def kernel(**inputs):
    import numpy as _np
    import concourse.bacc as _bacc
    from concourse import mybir as _mybir
    from concourse.bass_utils import run_bass_kernel_spmd as _run

    nc = _bacc.Bacc("TRN2", target_bir_lowering=False, num_devices=1)
    arrays, args = {}, []
    for name in _INS:
        a = _np.ascontiguousarray(inputs[name])
        arrays[f"in_{name}_dram"] = a
        args.append(nc.dram_tensor(f"in_{name}_dram", a.shape, _mybir.dt.from_np(a.dtype), kind="ExternalInput").ap())
    out = nc.dram_tensor("out_0_dram", (1, N, N, CH), F32, kind="ExternalOutput").ap()
    metaformer_kernel(nc, *args, out)
    r = _run(nc, [arrays], core_ids=[0])
    return r.results[0]["out_0_dram"]
```
